# Optimizing a Trainium2 kernel written in Bass

```python
import numpy as np
import jax
import jax.numpy as jnp

def _softmax(x, axis=-1):
    return jax.nn.softmax(x, axis=axis)

def _gelu(x):
    return jax.nn.gelu(x, approximate=True)

def _silu(x):
    return jax.nn.silu(x)

def _sigmoid(x):
    return jax.nn.sigmoid(x)

def _layernorm(x, axis=-1, eps=1e-05):
    m = jnp.mean(x, axis=axis, keepdims=True)
    v = jnp.var(x, axis=axis, keepdims=True)
    return (x - m) / jnp.sqrt(v + eps)

def _scatter_add(tgt, idx, src, axis=0):
    return tgt.at[idx].add(src)

def _segment_sum(src, seg, n):
    return jax.ops.segment_sum(src, seg, n)
kernel_name = 'mk_decoder_preln_d1_seqx_r4_18d151'

def setup_inputs(seed: int=0):
    np.random.seed(seed)
    _w = jnp.asarray

    def _rec_inputs():
        import jax
        import jax.numpy as jnp
        _rk = jax.random.key(seed)
        x = -0.0002928 + 1 * jax.random.normal(jax.random.fold_in(_rk, 1), (2, 512, 256), jnp.float32)
        _lenS = 512 - jax.random.randint(jax.random.fold_in(_rk, 7), (2,), 0, max(1, 512 // 4) + 1, jnp.int32)
        _lenS2 = 1024 - jax.random.randint(jax.random.fold_in(_rk, 8), (2,), 0, max(1, 1024 // 4) + 1, jnp.int32)
        _ctx_512P = jax.random.normal(jax.random.fold_in(_rk, 11), (2, 16, 128), jnp.float32)
        _ctx_512c = jax.random.dirichlet(jax.random.fold_in(_rk, 511), 0.3 * jnp.ones((16,), jnp.float32), (2, 1024))
        _ctx_512t = jnp.einsum('bsk,bkd->bsd', _ctx_512c, _ctx_512P)
        _ctx_512t = _ctx_512t * jax.lax.rsqrt(jnp.mean(jnp.square(_ctx_512t)) + 1e-12) * 0.953939
        ctx_512 = -1.52775e-05 + 0.999936 * (_ctx_512t + 0.3 * jax.random.normal(jax.random.fold_in(_rk, 611), (2, 1024, 128), jnp.float32))
        return (x, ctx_512)
    x, ctx_512 = _rec_inputs()

    def _L0_attn_setup():
        import jax, jax.numpy as jnp
        import numpy as np
        import math
        N_HEAD = 16
        N_KV_HEAD = 4
        WINDOW = 128
        EPS = 1e-06

        def _rotate_half(t):
            t1, t2 = jnp.split(t, 2, axis=-1)
            return jnp.concatenate([-t2, t1], axis=-1)

        def _rope_tables(T, head_dim):
            theta = 1.0 / 10000.0 ** (jnp.arange(0, head_dim, 2, dtype=jnp.float32) / head_dim)
            pos = jnp.arange(T, dtype=jnp.float32)
            freqs = jnp.outer(pos, theta)
            cos = jnp.concatenate([jnp.cos(freqs), jnp.cos(freqs)], axis=-1)
            sin = jnp.concatenate([jnp.sin(freqs), jnp.sin(freqs)], axis=-1)
            return (cos, sin)
        key = jax.random.key(seed)
        k1, k2, k3, k4 = jax.random.split(key, 4)
        B, T, C = (1, 512, 256)
        kv_out = 2 * N_KV_HEAD * (C // N_HEAD)
        x = jax.random.normal(k1, (B, T, C), dtype=jnp.float32)
        Wq = jax.random.normal(k2, (C, C), dtype=jnp.float32) * 0.02
        Wkv = jax.random.normal(k3, (kv_out, C), dtype=jnp.float32) * 0.02
        Wproj = jax.random.normal(k4, (C, C), dtype=jnp.float32) * 0.02
        return {'x': x, 'Wq': Wq, 'Wkv': Wkv, 'Wproj': Wproj}
    _L0_attn_all = _L0_attn_setup()
    _L0_attn_in = {k: v for k, v in _L0_attn_all.items() if k in ('Wq', 'Wkv', 'Wproj')}
    del _L0_attn_all

    def _L0_xattn_setup():
        import jax, jax.numpy as jnp
        import numpy as np
        NUM_HEADS = 16
        HEAD_DIM = 64
        Q_DIM = 256
        KV_DIM = 128
        INNER = NUM_HEADS * HEAD_DIM
        key = jax.random.key(seed)
        ks = jax.random.split(key, 7)
        B, N, M = (32, 128, 512)
        q = jax.random.normal(ks[0], (B, N, Q_DIM), dtype=jnp.float32)
        kv = jax.random.normal(ks[1], (B, M, KV_DIM), dtype=jnp.float32)
        Wq = jax.random.normal(ks[2], (Q_DIM, INNER), dtype=jnp.float32) / np.sqrt(Q_DIM)
        Wk = jax.random.normal(ks[3], (KV_DIM, INNER), dtype=jnp.float32) / np.sqrt(KV_DIM)
        Wv = jax.random.normal(ks[4], (KV_DIM, INNER), dtype=jnp.float32) / np.sqrt(KV_DIM)
        Wo = jax.random.normal(ks[5], (INNER, Q_DIM), dtype=jnp.float32) / np.sqrt(INNER)
        bo = jax.random.normal(ks[6], (Q_DIM,), dtype=jnp.float32) * 0.01
        return {'q': q, 'kv': kv, 'Wq': Wq, 'Wk': Wk, 'Wv': Wv, 'Wo': Wo, 'bo': bo}
    _L0_xattn_all = _L0_xattn_setup()
    _L0_xattn_in = {k: v for k, v in _L0_xattn_all.items() if k in ('Wq', 'Wk', 'Wv', 'Wo', 'bo')}
    del _L0_xattn_all

    def _L0_ffn_setup():
        import jax, jax.numpy as jnp
        import numpy as np
        H = 256
        I = 128
        E = 32
        TOP_K = 6
        N_GROUP = 8
        TOPK_GROUP = 4
        SCALE = 2.5
        N_SHARED = 2
        SI = I * N_SHARED
        B, S = (2, 256)
        key = jax.random.key(seed)
        ks = jax.random.split(key, 8)
        x = jax.random.normal(ks[0], (B, S, H), jnp.float32)
        gate_weight = jax.random.normal(ks[1], (E, H), jnp.float32) * 0.02
        e_score_correction_bias = jax.random.normal(ks[2], (E,), jnp.float32) * 0.01
        experts_gate_up = jax.random.normal(ks[3], (E, 2 * I, H), jnp.float32) * 0.02
        experts_down = jax.random.normal(ks[4], (E, H, I), jnp.float32) * 0.02
        shared_gate_w = jax.random.normal(ks[5], (SI, H), jnp.float32) * 0.02
        shared_up_w = jax.random.normal(ks[6], (SI, H), jnp.float32) * 0.02
        shared_down_w = jax.random.normal(ks[7], (H, SI), jnp.float32) * 0.02
        return {'x': x, 'gate_weight': gate_weight, 'e_score_correction_bias': e_score_correction_bias, 'experts_gate_up': experts_gate_up, 'experts_down': experts_down, 'shared_gate_w': shared_gate_w, 'shared_up_w': shared_up_w, 'shared_down_w': shared_down_w}
    _L0_ffn_all = _L0_ffn_setup()
    _L0_ffn_in = {k: v for k, v in _L0_ffn_all.items() if k in ('gate_weight', 'e_score_correction_bias', 'experts_gate_up', 'experts_down', 'shared_gate_w', 'shared_up_w', 'shared_down_w')}
    del _L0_ffn_all
    return {'x': x, 'ctx_512': ctx_512, 'L0_attn_Wq': _L0_attn_in['Wq'], 'L0_attn_Wkv': _L0_attn_in['Wkv'], 'L0_attn_Wproj': _L0_attn_in['Wproj'], 'L0_xattn_Wq': _L0_xattn_in['Wq'], 'L0_xattn_Wk': _L0_xattn_in['Wk'], 'L0_xattn_Wv': _L0_xattn_in['Wv'], 'L0_xattn_Wo': _L0_xattn_in['Wo'], 'L0_xattn_bo': _L0_xattn_in['bo'], 'L0_ffn_gate_weight': _L0_ffn_in['gate_weight'], 'L0_ffn_e_score_correction_bias': _L0_ffn_in['e_score_correction_bias'], 'L0_ffn_experts_gate_up': _L0_ffn_in['experts_gate_up'], 'L0_ffn_experts_down': _L0_ffn_in['experts_down'], 'L0_ffn_shared_gate_w': _L0_ffn_in['shared_gate_w'], 'L0_ffn_shared_up_w': _L0_ffn_in['shared_up_w'], 'L0_ffn_shared_down_w': _L0_ffn_in['shared_down_w']}

def reference(x, ctx_512, L0_attn_Wq, L0_attn_Wkv, L0_attn_Wproj, L0_xattn_Wq, L0_xattn_Wk, L0_xattn_Wv, L0_xattn_Wo, L0_xattn_bo, L0_ffn_gate_weight, L0_ffn_e_score_correction_bias, L0_ffn_experts_gate_up, L0_ffn_experts_down, L0_ffn_shared_gate_w, L0_ffn_shared_up_w, L0_ffn_shared_down_w):
    import jax
    import jax.numpy as jnp

    def _L0_attn_ref(x, Wq, Wkv, Wproj):
        import jax, jax.numpy as jnp
        import numpy as np
        import math
        N_HEAD = 16
        N_KV_HEAD = 4
        WINDOW = 128
        EPS = 1e-06

        def _rotate_half(t):
            t1, t2 = jnp.split(t, 2, axis=-1)
            return jnp.concatenate([-t2, t1], axis=-1)

        def _rope_tables(T, head_dim):
            theta = 1.0 / 10000.0 ** (jnp.arange(0, head_dim, 2, dtype=jnp.float32) / head_dim)
            pos = jnp.arange(T, dtype=jnp.float32)
            freqs = jnp.outer(pos, theta)
            cos = jnp.concatenate([jnp.cos(freqs), jnp.cos(freqs)], axis=-1)
            sin = jnp.concatenate([jnp.sin(freqs), jnp.sin(freqs)], axis=-1)
            return (cos, sin)
        B, T, C = x.shape
        H, KV = (N_HEAD, N_KV_HEAD)
        d = C // H
        n_rep = H // KV
        q = (x @ Wq.T).reshape(B, T, H, d).transpose(0, 2, 1, 3)
        kv = x @ Wkv.T
        k, v = jnp.split(kv, 2, axis=2)
        k = k.reshape(B, T, KV, d).transpose(0, 2, 1, 3)
        v = v.reshape(B, T, KV, d).transpose(0, 2, 1, 3)
        q = q / (jnp.linalg.norm(q, axis=-1, keepdims=True) + EPS)
        k = k / (jnp.linalg.norm(k, axis=-1, keepdims=True) + EPS)
        cos, sin = _rope_tables(T, d)
        cos = cos[None, None]
        sin = sin[None, None]
        q = q * cos + _rotate_half(q) * sin
        k = k * cos + _rotate_half(k) * sin
        k = jnp.repeat(k, n_rep, axis=1)
        v = jnp.repeat(v, n_rep, axis=1)
        rows = jnp.arange(T)[:, None]
        cols = jnp.arange(T)[None, :]
        mask = (cols <= rows) & (cols > rows - WINDOW)
        scale = 1.0 / math.sqrt(d)
        scores = jnp.einsum('bhqd,bhkd->bhqk', q, k) * scale
        scores = jnp.where(mask[None, None], scores, -jnp.inf)
        attn = jax.nn.softmax(scores, axis=-1)
        y = jnp.einsum('bhqk,bhkd->bhqd', attn, v)
        y = y.transpose(0, 2, 1, 3).reshape(B, T, C)
        return y @ Wproj.T

    def _L0_xattn_ref(q, kv, Wq, Wk, Wv, Wo, bo):
        import jax, jax.numpy as jnp
        import numpy as np
        NUM_HEADS = 16
        HEAD_DIM = 64
        Q_DIM = 256
        KV_DIM = 128
        INNER = NUM_HEADS * HEAD_DIM
        B, N, _ = q.shape
        M = kv.shape[1]
        scale = HEAD_DIM ** (-0.5)
        qh = (q @ Wq).reshape(B, N, NUM_HEADS, HEAD_DIM).transpose(0, 2, 1, 3)
        kh = (kv @ Wk).reshape(B, M, NUM_HEADS, HEAD_DIM).transpose(0, 2, 1, 3)
        vh = (kv @ Wv).reshape(B, M, NUM_HEADS, HEAD_DIM).transpose(0, 2, 1, 3)
        scores = jnp.einsum('bhnd,bhmd->bhnm', qh, kh) * scale
        attn = jax.nn.softmax(scores, axis=-1)
        out = jnp.einsum('bhnm,bhmd->bhnd', attn, vh)
        out = out.transpose(0, 2, 1, 3).reshape(B, N, INNER)
        return out @ Wo + bo

    def _L0_ffn_ref(x, gate_weight, e_score_correction_bias, experts_gate_up, experts_down, shared_gate_w, shared_up_w, shared_down_w):
        import jax, jax.numpy as jnp
        import numpy as np
        H = 256
        I = 128
        E = 32
        TOP_K = 6
        N_GROUP = 8
        TOPK_GROUP = 4
        SCALE = 2.5
        N_SHARED = 2
        SI = I * N_SHARED
        B, S = (2, 256)
        b, s, h = x.shape
        xf = x.reshape(-1, h)
        T = xf.shape[0]
        logits = xf.astype(jnp.float32) @ gate_weight.astype(jnp.float32).T
        scores = jax.nn.sigmoid(logits)
        sfc = scores + e_score_correction_bias[None, :]
        gs = E // N_GROUP
        group_scores = sfc.reshape(T, N_GROUP, gs).max(axis=-1)
        _, gidx = jax.lax.top_k(group_scores, TOPK_GROUP)
        gmask = jnp.zeros((T, N_GROUP), bool).at[jnp.arange(T)[:, None], gidx].set(True)
        smask = jnp.repeat(gmask, gs, axis=1)
        masked = jnp.where(smask, sfc, 0.0)
        _, topk_idx = jax.lax.top_k(masked, TOP_K)
        tw = jnp.take_along_axis(scores, topk_idx, axis=1)
        tw = tw / (tw.sum(-1, keepdims=True) + 1e-20)
        tw = (tw * SCALE).astype(xf.dtype)
        combine = jnp.zeros((T, E), xf.dtype).at[jnp.arange(T)[:, None], topk_idx].add(tw)

        def expert_step(acc, inp):
            gu, dn, c = inp
            g = xf @ gu[:I].T
            u = xf @ gu[I:].T
            o = jax.nn.silu(g) * u @ dn.T
            return (acc + c[:, None] * o, None)
        routed, _ = jax.lax.scan(expert_step, jnp.zeros_like(xf), (experts_gate_up, experts_down, combine.T))
        sh = jax.nn.silu(xf @ shared_gate_w.T) * (xf @ shared_up_w.T)
        shared_out = sh @ shared_down_w.T
        return (routed + shared_out).reshape(b, s, h)
    x = x + _L0_attn_ref(_layernorm(x, axis=-1), L0_attn_Wq, L0_attn_Wkv, L0_attn_Wproj)
    x = x + _L0_xattn_ref(_layernorm(x, axis=-1), ctx_512, L0_xattn_Wq, L0_xattn_Wk, L0_xattn_Wv, L0_xattn_Wo, L0_xattn_bo)
    x = x + _L0_ffn_ref(_layernorm(x, axis=-1), L0_ffn_gate_weight, L0_ffn_e_score_correction_bias, L0_ffn_experts_gate_up, L0_ffn_experts_down, L0_ffn_shared_gate_w, L0_ffn_shared_up_w, L0_ffn_shared_down_w)
    return x

_drawn_inputs = setup_inputs


def setup_inputs(seed=0):
    import zlib

    import numpy as np

    out = dict(_drawn_inputs(seed))
    spreads = {}
    factors = {'L0_attn_Wq': 8.0,
     'L0_attn_Wkv': 4.94,
     'L0_attn_Wproj': 4.874,
     'L0_xattn_bo': 6.187,
     'L0_ffn_gate_weight': 5.929,
     'L0_ffn_e_score_correction_bias': 8.0,
     'L0_ffn_experts_gate_up': 5.279,
     'L0_ffn_experts_down': 5.291,
     'L0_ffn_shared_gate_w': 3.788,
     'L0_ffn_shared_up_w': 3.744,
     'L0_ffn_shared_down_w': 3.731}
    for name, (base, spread) in spreads.items():
        noise = np.random.default_rng([zlib.crc32(name.encode()), seed]).standard_normal(out[name].shape)
        drawn = base * np.exp(spread * noise) if base else spread * noise
        out[name] = jnp.asarray(drawn.astype(out[name].dtype))
    for name, factor in factors.items():
        out[name] = (out[name] * factor).astype(out[name].dtype)
    return out
```

```python
from contextlib import ExitStack

import numpy as np

import concourse.bass as bass
from concourse import mybir

ACT = mybir.ActivationFunctionType
ALU = mybir.AluOpType
AX = mybir.AxisListType
F32 = mybir.dt.float32
F32R = mybir.dt.float32r
BF16 = mybir.dt.bfloat16

P = 128
B, T, C = 2, 512, 256
TILES = T // P
NT = B * TILES
KC = C // P
EPS_LN = 1e-5
EPS_NORM = 1e-6

NH, NKV, HD = 16, 4, 16
REP = NH // NKV
QKH = NH + NKV
QKC = QKH * HD
QKV = QKC + NKV * HD
SCALE_A = HD ** -0.5
VW = HD + 1
OSTEP = 32

XH, XD, M, CD = 16, 64, 1024, 128
SCALE_X = XD ** -0.5
PAIRS = XH // 2
UNITS_X = B * PAIRS
QB = T // P
KB = M // P
WPAIR = (KC + 2) * P
JOBS = 10

NE, NI, GROUPS, TOP_GROUPS, TOP_K, ROUTE_SCALE, SHARED = 32, 128, 8, 4, 6, 2.5, 2
GS = NE // GROUPS
EXPERTS = NE + SHARED
WEXP = KC * 2 * NI + C
PARTS = 3
NONE, TAKEN = -1e30, 1e30


def mk_decoder(nc, ins, out):
    ctx = ExitStack()
    stage_a = ExitStack()
    with ctx:
        def sb(name, shape, dt, stack=ctx):
            return stack.enter_context(nc.sbuf_tensor(name, shape, dt))

        def sem(name):
            return ctx.enter_context(nc.semaphore(name))

        banks = ctx.enter_context(nc.psum_tensor("banks", [P, 8, 512], F32))

        ident = sb("ident", [P, P], F32)
        x_sb = sb("x_sb", [P, NT, C], F32)
        stats = sb("stats", [P, NT, 6], F32)
        mv = sb("mv", [P, NT, 2], F32)
        ve = sb("ve", [P, NT], F32)
        sd = sb("sd", [P, NT], F32)
        sr = sb("sr", [P, NT], F32)
        rstd = sb("rstd", [P, NT], F32)
        xn = sb("xn", [P, 2, C], F32)
        nT_h = sb("nT_h", [P, KC, B * T], F32R)
        nT_l = sb("nT_l", [P, KC, B * T], F32R)
        wraw = sb("wraw", [P, 2, WPAIR], F32)
        ctx_h = sb("ctx_h", [P, B * M], F32R)
        ctx_l = sb("ctx_l", [P, B * M], F32R)

        def sa(name, shape, dt):
            return sb(name, shape, dt, stage_a)

        wqkv = sa("wqkv", [P, KC, QKV], F32)
        wqkv_h = sa("wqkv_h", [P, KC, QKV], F32R)
        wqkv_l = sa("wqkv_l", [P, KC, QKV], F32R)
        wp = sa("wp", [P, KC, C], F32)
        wp_h = sa("wp_h", [P, KC, C], F32R)
        wp_l = sa("wp_l", [P, KC, C], F32R)
        cosv = sa("cosv", [P, TILES, HD], F32)
        sinv = sa("sinv", [P, TILES, HD], F32)
        mask = sa("mask", [P, 2, P], F32)
        xh = sa("xh", [P, KC, T], F32R)
        xl = sa("xl", [P, KC, T], F32R)
        qkv = sa("qkv", [P, TILES, QKV], F32)
        sq = sa("sq", [P, TILES, QKC], F32)
        ss = sa("ss", [P, TILES * QKH], F32)
        s0 = sa("s0", [P, TILES * QKH], F32)
        s1 = sa("s1", [P, TILES * QKH], F32)
        rn = sa("rn", [P, TILES * QKH], F32)
        qn = sa("qn", [P, TILES, QKH, HD], F32)
        ra = sa("ra", [P, TILES, QKH, HD], F32)
        rb = sa("rb", [P, TILES, QKH, HD], F32)
        hl = sa("hl", [P, TILES * QKH, 4, HD], F32R)
        qT = sa("qT", [64, NH, T], F32R)
        kT = sa("kT", [64, NKV, T], F32R)
        va = sa("va", [P, TILES, NKV, VW], F32)
        E = sa("E", [P, 2, 2, REP, P], F32)
        y = sa("y", [P, 2, C], F32)
        ri = sa("ri", [P, NH], F32)
        yh = sa("yh", [P, KC, P], F32R)
        yl = sa("yl", [P, KC, P], F32R)

        ctxT = sa("ctxT", [P, B * M], F32)
        stage_a.close()

        stage_b = ExitStack()

        def sx(name, shape, dt):
            return sb(name, shape, dt, stage_b)

        wq_h = sx("wq_h", [P, 2, KC, P], F32R)
        wq_l = sx("wq_l", [P, 2, KC, P], F32R)
        wk_h = sx("wk_h", [P, 2, P], F32R)
        wk_l = sx("wk_l", [P, 2, P], F32R)
        wv_h = sx("wv_h", [P, P], F32R)
        wv_l = sx("wv_l", [P, P], F32R)
        k_raw = sx("k_raw", [P, M], F32)
        q_raw = sx("q_raw", [P, T], F32)
        v_raw = sx("v_raw", [P, KB, XD], F32)
        vT = sx("vT", [P, M], F32)
        k_st = sx("k_st", [P, 2, M], F32R)
        q_hh = sx("q_hh", [P, 2, T], F32R)
        q_ll = sx("q_ll", [P, 2, T], F32R)
        v_hl = sx("v_hl", [P, 2, KB, 2, XD], F32R)
        nmax = sx("nmax", [P, 2 * QB], F32)
        pT_h = sx("pT_h", [P, 4, T], F32R)
        pT_l = sx("pT_l", [P, 4, T], F32R)
        o_low = sx("o_low", [64, T], F32)
        o_all = sx("o_all", [P, UNITS_X, T], F32)
        sums = sx("sums", [P, 2 * UNITS_X * QB], F32)
        rsum = sx("rsum", [P, UNITS_X, 2, QB], F32)
        wo = sx("wo", [P, PAIRS, C], F32)
        wo_h = sx("wo_h", [P, PAIRS, C], F32R)
        wo_l = sx("wo_l", [P, PAIRS, C], F32R)
        bo2 = sx("bo2", [1, 2 * C], F32)
        ones1 = sx("ones1", [1, P], F32)
        heads = ExitStack()
        probs = sb("probs", [P, 2, QB, M], F32, heads)
        heads.close()
        rexp = sx("rexp", [P, 2, QB, P], F32)
        on = sx("on", [P, 2, T], F32)
        on_h = sx("on_h", [P, 2, T], F32R)
        on_l = sx("on_l", [P, 2, T], F32R)
        stage_b.close()

        stage_f = ExitStack()

        def sf(name, shape, dt):
            return sb(name, shape, dt, stage_f)

        wf_raw = sf("wf_raw", [P, 2, WEXP], F32)
        wf_h = sf("wf_h", [P, 2, WEXP], F32R)
        wf_l = sf("wf_l", [P, 2, WEXP], F32R)
        sel = sf("sel", [PARTS * EXPERTS, EXPERTS * P], BF16)
        wg = sf("wg", [P, KC, NE], F32)
        wg_h = sf("wg_h", [P, KC, NE], F32R)
        wg_l = sf("wg_l", [P, KC, NE], F32R)
        ebias = sf("ebias", [P, NE], F32)
        identb = sf("identb", [P, P], BF16)
        zrow = sf("zrow", [1, 512], F32)
        lgT = sf("lgT", [NE, B * T], F32)
        sc = sf("sc", [P, NT, NE], F32)
        sfc = sf("sfc", [P, NT, NE], F32)
        gval = sf("gval", [P, NT, GROUPS + 8], F32)
        gtop = sf("gtop", [P, NT, 8], F32)
        gout = sf("gout", [P, NT, GROUPS + 8], F32)
        gmask = sf("gmask", [P, NT, GROUPS], F32)
        evalue = sf("evalue", [P, NT, NE + 8], F32)
        etop = sf("etop", [P, NT, 8], F32)
        eout = sf("eout", [P, NT, NE + 8], F32)
        tw = sf("tw", [P, NT, NE], F32)
        tsum = sf("tsum", [P, NT], F32)
        comb = sf("comb", [P, NT, EXPERTS], F32)
        cres = sf("cres", [P, NT, EXPERTS], F32)
        parts = sf("parts", [P, NT, PARTS, EXPERTS], BF16)
        combT = sf("combT", [PARTS * EXPERTS, B * T], BF16)
        sg = sf("sg", [P, 2, 512], F32)
        gc = sf("gc", [P, 2, 512], F32)
        hid = sf("hid", [P, 2, 512], F32)
        hid_h = sf("hid_h", [P, 2, 512], F32R)
        hid_l = sf("hid_l", [P, 2, 512], F32R)
        yT = sf("yT", [P, 4, 512], F32)
        y_out = sf("y_out", [P, NT, C], F32)
        stage_f.close()

        YF_BANK, G_BANK, C_BANK, U_BANK = 0, 4, 6, 7

        S_BANK, PT_BANK, O_BANK, MISC = 0, 4, 6, 7
        Y_BANK, R_BANK = 0, 2

        ctx_in = sem("ctx_in")
        ctx_hi = sem("ctx_hi")
        ctx_ok = sem("ctx_ok")
        wx_in = sem("wx_in")
        wo_in = sem("wo_in")
        wo_hi = sem("wo_hi")
        wo_ok = sem("wo_ok")
        wx_used = sem("wx_used")
        wq_ok = sem("wq_ok")
        wk_ok = sem("wk_ok")
        wv_ok = sem("wv_ok")
        pool_step = sem("pool_step")
        pool_go = sem("pool_go")
        pe_go = sem("pe_go")
        misc_ps = sem("misc_ps")
        misc_out = sem("misc_out")
        k_ok = sem("k_ok")
        q_ok = sem("q_ok")
        v_ok = sem("v_ok")
        sx_ps = sem("sx_ps")
        max_ok = sem("max_ok")
        ex_ok = sem("ex_ok")
        pT_ps = sem("pT_ps")
        pTh_ok = sem("pTh_ok")
        pTl_ok = sem("pTl_ok")
        o_ps = sem("o_ps")
        olow_ok = sem("olow_ok")
        o_free = sem("o_free")
        rs_ok = sem("rs_ok")
        rexp_ok = sem("rexp_ok")
        rT_ps = sem("rT_ps")
        on_ok = sem("on_ok")
        onh_ok = sem("onh_ok")
        onl_ok = sem("onl_ok")
        y_used = sem("y_used")
        bias_ok = sem("bias_ok")
        var2_ok = sem("var2_ok")
        sqrt2_ok = sem("sqrt2_ok")
        xn2_ok = sem("xn2_ok")
        nT2_ps = sem("nT2_ps")
        nTh2_ok = sem("nTh2_ok")
        nTl2_ok = sem("nTl2_ok")
        x2_ok = sem("x2_ok")

        var3_ok = sem("var3_ok")
        sqrt3_ok = sem("sqrt3_ok")
        xn3_ok = sem("xn3_ok")
        nT3_ps = sem("nT3_ps")
        nTh3_ok = sem("nTh3_ok")
        nTl3_ok = sem("nTl3_ok")
        gate_in = sem("gate_in")
        f_const = sem("f_const")
        wg_hi = sem("wg_hi")
        wg_ok = sem("wg_ok")
        lg_ps = sem("lg_ps")
        lgT_ok = sem("lgT_ok")
        lgN_ps = sem("lgN_ps")
        sc_ok = sem("sc_ok")
        parts_ok = sem("parts_ok")
        combT_ps = sem("combT_ps")
        combT_ok = sem("combT_ok")
        wf_in = [sem("wf_in0"), sem("wf_in1")]
        wf_step = sem("wf_step")
        wf_ok = sem("wf_ok")
        g_ps = sem("g_ps")
        c_ps = sem("c_ps")
        u_ps = sem("u_ps")
        d_ps = sem("d_ps")
        sg_ok = sem("sg_ok")
        gc_ok = sem("gc_ok")
        hid_ok = sem("hid_ok")
        hh_ok = sem("hh_ok")
        hlo_ok = sem("hlo_ok")
        yT_a = sem("yT_a")
        yT_d = sem("yT_d")
        yN_ps = sem("yN_ps")
        y_fin = sem("y_fin")

        x_in = sem("x_in")
        wa_in = sem("wa_in")
        const_in = sem("const_in")
        ident_ok = sem("ident_ok")
        ones_ok = sem("ones_ok")
        wa_hi = sem("wa_hi")
        wa_ok = sem("wa_ok")
        var_ok = sem("var_ok")
        sqrt_ok = sem("sqrt_ok")
        rope_b = sem("rope_b")
        dve_step = sem("dve_step")
        xn_ok = sem("xn_ok")
        xT_ps = sem("xT_ps")
        xh_ok = sem("xh_ok")
        xl_ok = sem("xl_ok")
        qkv_ps = sem("qkv_ps")
        qkv_ok = sem("qkv_ok")
        sq_ok = sem("sq_ok")
        ss_ok = sem("ss_ok")
        s0_ok = sem("s0_ok")
        qn_ok = sem("qn_ok")
        r_ok = sem("r_ok")
        hi_ok = sem("hi_ok")
        hl_ok = sem("hl_ok")
        kswap_ok = sem("kswap_ok")
        qkT_ps = sem("qkT_ps")
        even_ok = sem("even_ok")
        odd_ok = sem("odd_ok")
        s_ps = sem("s_ps")
        exp_ok = sem("exp_ok")
        mcur_ok = sem("mcur_ok")
        mprev_ok = sem("mprev_ok")
        pv_done = sem("pv_done")
        y_ok = sem("y_ok")
        yT_ps = sem("yT_ps")
        yh_ok = sem("yh_ok")
        yl_ok = sem("yl_ok")
        proj_ps = sem("proj_ps")
        x1_ok = sem("x1_ok")
        out_done = sem("out_done")

        UNITS = TILES * NKV
        def prev_masks(n):
            return max(0, n - NKV)

        block = ctx.enter_context(nc.Block())

        @block.sync
        def _(sp):
            sp.dma_start(x_sb[:], ins["x"].rearrange("b (t p) c -> p (b t) c", p=P)).then_inc(x_in, 16)
            sp.dma_start(wqkv[:], ins["wqkv"].rearrange("(k p) n -> p k n", p=P)).then_inc(wa_in, 16)
            sp.dma_start(wp[:], ins["wp"].rearrange("(k p) n -> p k n", p=P)).then_inc(wa_in, 16)
            sp.dma_start(cosv[:], ins["cosv"].rearrange("(t p) d -> p t d", p=P)).then_inc(const_in, 16)
            sp.dma_start(sinv[:], ins["sinv"].rearrange("(t p) d -> p t d", p=P)).then_inc(const_in, 16)
            sp.dma_start(mask[:], ins["mask"]).then_inc(const_in, 16)
            sp.sem_inc(o_free, 1)
            sp.sem_inc(y_used, 2)
            sp.sem_inc(nTl2_ok, 2)
            sp.sem_inc(nTl3_ok, 2)
            sp.dma_start(ctxT[:], ins["ctxT"]).then_inc(ctx_in, 16)

            def load_pair(unit):
                sp.dma_start(wraw[:, bass.ds(unit % 2, 1), :].rearrange("p o n -> p (o n)"),
                             ins["wx"][bass.ds(unit % PAIRS, 1)].rearrange("o p n -> p (o n)")).then_inc(wx_in, 16)

            sp.dma_start(wraw[:, 0], ins["wx"][0]).then_inc(wx_in, 16)
            sp.wait_ge(wx_in, 16)
            sp.dma_start(wraw[:, 1], ins["wx"][1]).then_inc(wx_in, 16)
            sp.wait_ge(x1_ok, NT)
            sp.dma_start(wo[:], ins["wo"].rearrange("(u p) n -> p u n", p=P)).then_inc(wo_in, 16)
            sp.dma_start(bo2[:], ins["bo2"]).then_inc(wo_in, 16)
            with sp.Fori(0, UNITS_X - 1) as u:
                sp.wait_ge(wx_used, u + 1)
                sp.wait_ge(wx_in, u * 16 + 32)
                load_pair(u + 2)
            sp.wait_ge(x2_ok, B)
            sp.dma_start(wg[:], ins["wg"].rearrange("(k p) e -> p k e", p=P)).then_inc(gate_in, 16)
            sp.dma_start(ebias[:], ins["ebias"].partition_broadcast(P)).then_inc(gate_in, 16)
            sp.dma_start(sel[:], ins["sel"]).then_inc(gate_in, 16)
            for j in range(2):
                sp.dma_start(wf_raw[:, j], ins["wf"][j]).then_inc(wf_in[j], 16)
            with sp.Fori(1, EXPERTS // 2) as i:
                for j in range(2):
                    sp.wait_ge(wf_ok, i * 2 + j - 1)
                    sp.dma_start(wf_raw[:, j], ins["wf"][bass.ds(i * 2 + j, 1)].rearrange("o p n -> p (o n)"))\
                        .then_inc(wf_in[j], 16)
            o_v = out.rearrange("b (t p) c -> p (b t) c", p=P)
            for r in range(NT // 2):
                sp.wait_ge(y_fin, r + 1)
                sp.dma_start(o_v[:, 2 * r:2 * r + 2], y_out[:, 2 * r:2 * r + 2]).then_inc(out_done, 16)
            sp.wait_ge(out_done, 16 * (NT // 2))

        @block.gpsimd
        def _(pool):
            pool.memset(ident[:], 0.0).then_inc(ident_ok, 1)
            pool.wait_ge(ident_ok, 1)
            pool.affine_select(out=ident[:], in_=ident[:], compare_op=ALU.not_equal, fill=1.0, base=0,
                               pattern=[[-1, P]], channel_multiplier=1).then_inc(ident_ok, 1)
            pool.memset(va[:, :, :, HD:VW], 1.0).then_inc(ones_ok, 1)
            pool.wait_ge(wa_in, 32)
            pool.tensor_copy(wqkv_h[:], wqkv[:]).then_inc(wa_hi, 1)
            pool.tensor_copy(wp_h[:], wp[:]).then_inc(wa_hi, 1)
            pool.wait_ge(wa_hi, 2)
            pool.tensor_tensor(wqkv_l[:], wqkv[:], wqkv_h[:].bitcast(F32), ALU.subtract).then_inc(wa_ok, 1)
            pool.tensor_tensor(wp_l[:], wp[:], wp_h[:].bitcast(F32), ALU.subtract).then_inc(wa_ok, 1)
            pool.wait_ge(ctx_in, 16)
            pool.tensor_copy(ctx_h[:], ctxT[:]).then_inc(ctx_hi, 1)
            pool.wait_ge(ctx_hi, 1)
            pool.tensor_tensor(ctx_l[:], ctxT[:], ctx_h[:].bitcast(F32), ALU.subtract).then_inc(ctx_ok, 1)
            pool.wait_ge(const_in, 48)
            with pool.Fori(0, B) as b:
                pool.wait_ge(qn_ok, b + 1)
                for half in range(2):
                    lo, hi = (0, HD // 2) if half == 0 else (HD // 2, HD)
                    src = slice(HD // 2, HD) if half == 0 else slice(0, HD // 2)
                    pool.tensor_tensor(
                        rb[:, :, :, lo:hi], qn[:, :, :, src],
                        sinv[:, :, lo:hi].unsqueeze(2).broadcast_to([P, TILES, QKH, HD // 2]),
                        ALU.mult).then_inc(rope_b, 1)
                for n in range(UNITS):
                    pool.wait_ge(exp_ok, b * UNITS + n + 1)
                    pool.tensor_tensor(E[:, n % 2, 1], E[:, n % 2, 1],
                                       mask[:, 1, :].unsqueeze(1).broadcast_to([P, REP, P]),
                                       ALU.mult).then_inc(mcur_ok, 1)

            pool.wait_ge(x1_ok, NT)
            pool.memset(ones1[:], 1.0).then_inc(ones_ok, 1)

            psteps = [0]

            def split(h_out, l_out, raw_h, raw_l, h_in, base, ready, waits):
                for s_, v_ in waits:
                    pool.wait_ge(s_, v_)
                pool.sem_inc(pool_go, 1)
                psteps[0] += 1
                pool.tensor_copy(h_out, raw_h).then_inc(pool_step, 1)
                pool.wait_ge(pool_step, base + psteps[0])
                pool.sem_inc(pool_go, 1)
                pool.tensor_tensor(l_out, raw_l, h_in.bitcast(F32), ALU.subtract).then_inc(*ready)

            def raw_w(unit):
                slot = bass.ds(unit % 2, 1) if not isinstance(unit, int) else slice(unit % 2, unit % 2 + 1)
                return wraw[:, slot, :].rearrange("p o n -> p (o n)")

            def split_wq(unit, s_, base, waits):
                raw = raw_w(unit)[:, 0:KC * P].rearrange("p (k h d) -> p k h d", k=KC, h=2)[:, :, s_, :]\
                    .unsqueeze(2).broadcast_to([P, KC, 2, XD])
                split(wq_h[:, s_].rearrange("p k (r d) -> p k r d", r=2), wq_l[:, s_].rearrange("p k (r d) -> p k r d", r=2),
                      raw, raw, wq_h[:, s_].rearrange("p k (r d) -> p k r d", r=2), base, (wq_ok, 1), waits)

            def split_wk(unit, base, waits):
                raw = raw_w(unit)[:, KC * P:(KC + 1) * P].rearrange("p (h d) -> p h d", h=2)\
                    .unsqueeze(2).broadcast_to([P, 2, 2, XD])
                split(wk_h[:].rearrange("p h (r d) -> p h r d", r=2), wk_l[:].rearrange("p h (r d) -> p h r d", r=2),
                      raw, raw, wk_h[:].rearrange("p h (r d) -> p h r d", r=2), base, (wk_ok, 1), waits)

            def split_wv(unit, base, waits):
                raw = raw_w(unit)[:, (KC + 1) * P:WPAIR]
                split(wv_h[:], wv_l[:], raw, raw, wv_h[:], base, (wv_ok, 1), waits)

            def split_k(s_, head, base, waits):
                split(k_st[:, s_], k_st[64:P, s_], k_raw[:], k_raw[64:P], k_st[64:P, s_], base, (k_ok, 1), waits)
                pool.wait_ge(k_ok, head + 1)

            def split_q(s_, base, waits):
                split(q_hh[:, s_], q_ll[:, s_], q_raw[:], q_raw[:], q_hh[:, s_], base, (q_ok, 1), waits)

            def split_v(s_, base, waits):
                split(v_hl[:, s_, :, 0], v_hl[:, s_, :, 1], v_raw[:], v_raw[:], v_hl[:, s_, :, 0], base, (v_ok, 1), waits)

            split_wk(0, 0, [(wx_in, 16)])
            split_wq(0, 0, 0, [])
            split_wq(0, 1, 0, [])
            split_wv(0, 0, [])
            pool.wait_ge(wv_ok, 1)
            pool.sem_inc(wx_used, 1)
            split_k(0, 0, 0, [(misc_out, 2)])
            split_wq(1, 0, 0, [(wx_in, 32), (misc_ps, 3)])
            split_q(0, 0, [(misc_out, 3)])
            split_wk(1, 0, [(misc_ps, 5)])
            split_k(1, 1, 0, [(misc_out, 5)])
            split_wv(1, 0, [(misc_ps, 7)])
            split_q(1, 0, [(misc_out, 8)])
            split_wq(1, 1, 0, [(misc_ps, 8)])
            pool.wait_ge(wq_ok, 4)
            pool.sem_inc(wx_used, 1)
            split_v(0, 0, [(misc_out, 9)])
            first_split = psteps[0]
            PER_UNIT = 10
            with pool.Fori(0, UNITS_X - 1) as u:
                psteps[0] = 0
                base = u * PER_UNIT + first_split
                job = u * JOBS + JOBS - 1
                split_k(0, u * 2 + 2, base, [(misc_out, job + 2)])
                split_wq(u + 2, 0, base, [(wx_in, u * 16 + 48), (misc_ps, job + 3)])
                split_q(0, base, [(misc_out, job + 3)])
                split_v(1, base, [(misc_out, job + 4)])
                split_wk(u + 2, base, [(misc_ps, job + 6)])
                split_k(1, u * 2 + 3, base, [(misc_out, job + 6)])
                split_wv(u + 2, base, [(misc_ps, job + 8)])
                split_q(1, base, [(misc_out, job + 9)])
                split_wq(u + 2, 1, base, [(misc_ps, job + 9)])
                pool.wait_ge(wq_ok, u * 2 + 6)
                pool.sem_inc(wx_used, 1)
                split_v(0, base, [(misc_out, job + 10)])
                assert psteps[0] == PER_UNIT
            psteps[0] = 0
            end_base = first_split + (UNITS_X - 1) * PER_UNIT
            split_v(1, end_base, [(misc_out, JOBS * UNITS_X)])

            pool.wait_ge(wo_in, 32)
            pool.tensor_copy(wo_h[:], wo[:]).then_inc(wo_hi, 1)
            pool.wait_ge(wo_hi, 1)
            pool.tensor_tensor(wo_l[:], wo[:], wo_h[:].bitcast(F32), ALU.subtract).then_inc(wo_ok, 1)
            pool.wait_ge(rs_ok, 1)
            pool.wait_ge(o_free, 2 * UNITS_X + 1)
            with pool.Fori(0, UNITS_X // 2) as i:
                for j in range(2):
                    pool.wait_ge(y_used, i * 2 + j + 1)
                    pool.sem_inc(pool_go, 1)
                    pool.tensor_copy(rexp[:, j].rearrange("p q (h d) -> p q h d", h=2),
                                     rsum[:, bass.ds(i * 2 + j, 1)].rearrange("p o h q -> p q (o h)").unsqueeze(3)
                                     .broadcast_to([P, QB, 2, XD])).then_inc(rexp_ok, 1)
                for j in range(2):
                    pool.wait_ge(onh_ok, i * 2 + j + 1)
                    pool.tensor_tensor(on_l[:, j], on[:, j], on_h[:, j].bitcast(F32), ALU.subtract).then_inc(onl_ok, 1)

            pool.wait_ge(x2_ok, B)
            pool.memset(identb[:], 0.0).then_inc(f_const, 1)
            pool.wait_ge(f_const, 1)
            pool.affine_select(out=identb[:], in_=identb[:], compare_op=ALU.not_equal, fill=1.0, base=0,
                               pattern=[[-1, P]], channel_multiplier=1).then_inc(f_const, 1)
            pool.memset(zrow[:], 0.0).then_inc(f_const, 1)
            pool.wait_ge(gate_in, 48)
            pool.tensor_copy(wg_h[:], wg[:]).then_inc(wg_hi, 1)
            pool.wait_ge(wg_hi, 1)
            pool.tensor_tensor(wg_l[:], wg[:], wg_h[:].bitcast(F32), ALU.subtract).then_inc(wg_ok, 1)

            def split_expert(j, e):
                pool.tensor_copy(wf_h[:, j], wf_raw[:, j]).then_inc(wf_step, 1)
                pool.wait_ge(wf_step, e + 1)
                pool.tensor_tensor(wf_l[:, j], wf_raw[:, j], wf_h[:, j].bitcast(F32), ALU.subtract).then_inc(wf_ok, 1)

            for e in range(2):
                pool.wait_ge(wf_in[e], 16)
                split_expert(e, e)
            with pool.Fori(1, EXPERTS // 2) as i:
                for j in range(2):
                    e = i * 2 + j
                    pool.wait_ge(wf_in[j], i * 16 + 16)
                    pool.wait_ge(d_ps, i * 4 + 2 * j - 2)
                    pool.sem_inc(pool_go, 1)
                    split_expert(j, e)

        @block.scalar
        def _(act):
            def copy_yh(act, b, t):
                act.wait_ge(yT_ps, b * TILES + t + 1)
                act.activation(yh[:], banks[:, 2, 0:C].rearrange("p (k n) -> p k n", k=KC), ACT.Copy).then_inc(yh_ok, 1)

            act.wait_ge(var_ok, 1)
            act.activation(sd[:], ve[:], ACT.Sqrt).then_inc(sqrt_ok, 1)
            with act.Fori(0, B) as b:
                def copy_xh(t):
                    act.wait_ge(xT_ps, b * TILES + t + 1)
                    act.activation(xh[:, :, t * P:(t + 1) * P],
                                   banks[:, t % 2, 0:C].rearrange("p (k n) -> p k n", k=KC),
                                   ACT.Copy).then_inc(xh_ok, 1)

                def copy_qkv(t):
                    act.wait_ge(qkv_ps, b * TILES + t + 1)
                    act.activation(qkv[:, t, :], banks[:, 2 + t % 2, 0:QKV], ACT.Copy).then_inc(qkv_ok, 1)

                copy_xh(0)
                copy_xh(1)
                copy_qkv(0)
                copy_xh(2)
                copy_qkv(1)
                copy_xh(3)
                copy_qkv(2)
                copy_qkv(3)
                act.wait_ge(qkv_ok, (b + 1) * TILES)
                act.activation(sq[:], qkv[:, :, 0:QKC], ACT.Square).then_inc(sq_ok, 1)
                act.wait_ge(ones_ok, 1)
                act.activation(va[:, :, :, 0:HD], qkv[:, :, QKC:QKV].rearrange("p t (g d) -> p t g d", g=NKV),
                               ACT.Copy).then_inc(sq_ok, 1)
                act.wait_ge(ss_ok, b + 1)
                act.activation(s0[:], ss[:], ACT.Sqrt).then_inc(s0_ok, 1)
                act.wait_ge(r_ok, b + 1)
                act.activation(hl[:, :, 0:2, :], ra[:].rearrange("p t h d -> p (t h) d").unsqueeze(2)
                               .broadcast_to([P, TILES * QKH, 2, HD]), ACT.Copy).then_inc(hi_ok, 1)
                act.wait_ge(hl_ok, b + 1)
                kr = hl[:].rearrange("p (t h) c d -> p t h c d", t=TILES)[:, :, NH:QKH]
                act.activation(kr[:, :, :, 1, :], kr[:, :, :, 3, :].bitcast(F32), ACT.Copy).then_inc(kswap_ok, 1)
                act.activation(kr[:, :, :, 2, :], kr[:, :, :, 0, :].bitcast(F32), ACT.Copy).then_inc(kswap_ok, 1)
                for t in range(TILES):
                    act.wait_ge(qkT_ps, b * TILES + t + 1)
                    act.activation(qT[:, 0:NH:2, t * P:(t + 1) * P],
                                   banks[0:64, 4 + 2 * (t % 2):6 + 2 * (t % 2), :].rearrange("p a (h n) -> p (a h) n", n=P),
                                   ACT.Copy)
                    act.activation(kT[:, 0:NKV:2, t * P:(t + 1) * P],
                                   banks[0:64, t % 2, 0:C].rearrange("p (h n) -> p h n", n=P),
                                   ACT.Copy).then_inc(even_ok, 1)
                for n in range(UNITS):
                    t, g = n // NKV, n % NKV
                    act.wait_ge(s_ps, b * UNITS + n + 1)
                    if n >= 2:
                        act.wait_ge(pv_done, b * UNITS + n - 1)
                    k0 = 0 if t else 1
                    r = 4 + 2 * (n % 2)
                    act.activation(E[:, n % 2, k0:2], banks[:, r + k0:r + 2, :].rearrange("p a (h n) -> p a h n", n=P),
                                   ACT.Exp, scale=SCALE_A).then_inc(exp_ok, 1)
                    if g == 1 and t >= 1:
                        copy_yh(act, b, t - 1)
                copy_yh(act, b, TILES - 1)

            act.wait_ge(var2_ok, 1)
            act.activation(sd[:], ve[:], ACT.Sqrt).then_inc(sqrt2_ok, 1)

            def turn_out(i, ps, ok):
                for j in range(2):
                    act.wait_ge(ps, i * 2 + j + 1)
                    act.activation(nT_h[:, :, bass.ds((i * 2 + j) * P, P)],
                                   banks[:, j, 0:C].rearrange("p (k n) -> p k n", k=KC), ACT.Copy).then_inc(ok, 1)

            with act.Fori(0, NT // 2) as i:
                turn_out(i, nT2_ps, nTh2_ok)

            def misc(job, dst, scale=1.0):
                act.wait_ge(misc_ps, job + 1)
                act.activation(dst, banks[:, MISC], ACT.Copy, scale=scale).then_inc(misc_out, 1)

            def exp_x(head, s_, q):
                act.wait_ge(max_ok, head * QB + q + 1)
                act.activation(probs[:, s_, q], banks[:, S_BANK + 2 * (q % 2):S_BANK + 2 * (q % 2) + 2]
                               .rearrange("p a n -> p (a n)"), ACT.Exp, bias=nmax[:, s_ * QB + q:s_ * QB + q + 1],
                               accum_out=sums[:, bass.ds(head * QB + q, 1)]).then_inc(ex_ok, 1)

            def high_p(head, kb):
                act.wait_ge(pT_ps, head * KB + kb + 1)
                act.activation(pT_h[:, kb % 4], banks[:, PT_BANK + kb % 2], ACT.Copy).then_inc(pTh_ok, 1)

            def low_o(head):
                act.wait_ge(o_ps, head + 1)
                act.activation(o_low[:], banks[64:P, O_BANK], ACT.Copy).then_inc(olow_ok, 1)

            misc(0, k_raw[:, 0:512])
            misc(2, q_raw[:], SCALE_X)
            act.wait_ge(k_ok, 1)
            misc(3, k_raw[:, 0:512])
            misc(5, vT[:, 0:512])
            act.wait_ge(q_ok, 1)
            misc(7, q_raw[:], SCALE_X)
            for q in range(QB):
                exp_x(0, 0, q)
            with act.Fori(0, UNITS_X - 1) as u:
                job = u * JOBS + JOBS - 1
                for s_ in range(2):
                    h, H, sH = u * 2 + s_, u * 2 + s_ + 1, 1 - s_
                    high_p(h, 0)
                    high_p(h, 1)
                    exp_x(H, sH, 0)
                    misc(job + (0 if s_ == 0 else 4), k_raw[:, 0:512])
                    high_p(h, 2)
                    exp_x(H, sH, 1)
                    high_p(h, 3)
                    if s_ == 1:
                        misc(job + 6, vT[:, 0:512])
                    high_p(h, 4)
                    exp_x(H, sH, 2)
                    high_p(h, 5)
                    misc(job + (2 if s_ == 0 else 8), q_raw[:], SCALE_X)
                    high_p(h, 6)
                    exp_x(H, sH, 3)
                    high_p(h, 7)
                    low_o(h)
            for s_ in range(2):
                h = 2 * UNITS_X - 2 + s_
                for kb in range(KB):
                    high_p(h, kb)
                    if s_ == 0 and kb % 2 == 1:
                        exp_x(h + 1, 1, kb // 2)
                low_o(h)
            with act.Fori(0, UNITS_X // 2) as i:
                for j in range(2):
                    act.wait_ge(on_ok, i * 2 + j + 1)
                    act.activation(on_h[:, j], on[:, j], ACT.Copy).then_inc(onh_ok, 1)

            act.wait_ge(var3_ok, 1)
            act.activation(sd[:], ve[:], ACT.Sqrt).then_inc(sqrt3_ok, 1)
            with act.Fori(0, NT // 2) as i:
                turn_out(i, nT3_ps, nTh3_ok)
            act.wait_ge(lg_ps, 2)
            act.activation(lgT[:], banks[0:NE, 2:4].rearrange("p a n -> p (a n)"), ACT.Copy).then_inc(lgT_ok, 1)
            act.wait_ge(lgN_ps, 1)
            act.activation(sc[:], banks[:, 4, 0:NT * NE].rearrange("p (t e) -> p t e", e=NE), ACT.Sigmoid)\
                .then_inc(sc_ok, 1)
            act.wait_ge(combT_ps, 1)
            act.activation(combT[:], banks[0:PARTS * EXPERTS, 5].bitcast(BF16), ACT.Copy).then_inc(combT_ok, 1)

            def silu(n, c):
                act.wait_ge(g_ps, n + 1)
                act.activation(sg[:, c], banks[:, G_BANK + c], ACT.Silu).then_inc(sg_ok, 1)

            def high_h(n, c):
                act.wait_ge(hid_ok, n + 1)
                act.activation(hid_h[:, c], hid[:, c], ACT.Copy).then_inc(hh_ok, 1)

            silu(0, 0)
            with act.Fori(0, EXPERTS // 2 - 1) as i:
                for m in range(4):
                    silu(i * 4 + m + 1, (m + 1) % 2)
                    high_h(i * 4 + m, m % 2)
            last_n = 2 * EXPERTS - 4
            for m in range(4):
                if m < 3:
                    silu(last_n + m + 1, (m + 1) % 2)
                high_h(last_n + m, m % 2)
            act.wait_ge(d_ps, 2 * EXPERTS)
            for r in range(2):
                act.activation(yT[:, r], banks[:, YF_BANK + r], ACT.Copy).then_inc(yT_a, 1)

        @block.vector
        def _(dve):
            def add_x1(dve, b, t):
                dve.wait_ge(proj_ps, b * TILES + t + 1)
                xt = x_sb[:, bass.ds(b * TILES + t, 1), :].rearrange("p o c -> p (o c)")
                dve.tensor_tensor(xt, banks[:, 3, 0:C], xt, ALU.add).then_inc(x1_ok, 1)

            steps = [0]

            def step(ins_, base=0):
                steps[0] += 1
                ins_.then_inc(dve_step, 1)
                dve.wait_ge(dve_step, base + steps[0])

            dve.wait_ge(x_in, 16)
            for t in range(NT):
                last = dve.bn_stats(stats[:, t, :], x_sb[:, t, :])
            step(last)
            for t in range(NT):
                last = dve.bn_aggr(mv[:, t, :], stats[:, t, :])
            step(last)
            dve.tensor_scalar(ve[:], mv[:, :, 1], EPS_LN, None, ALU.add).then_inc(var_ok, 1)
            dve.wait_ge(sqrt_ok, 1)
            step(dve.reciprocal(sr[:], sd[:]))
            step(dve.tensor_tensor(sr[:], sr[:], ve[:], ALU.mult))
            step(dve.tensor_tensor(sd[:], sd[:], sr[:], ALU.add))
            step(dve.tensor_scalar(sd[:], sd[:], 0.5, None, ALU.mult))
            step(dve.reciprocal(rstd[:], sd[:]))
            first = steps[0]
            PER_BATCH = 13
            with dve.Fori(0, B) as b:
                steps[0] = 0
                base = b * PER_BATCH + first

                def norm_x(t):
                    dve.tensor_scalar(xn[:, t % 2], x_sb[:, bass.ds(b * TILES + t, 1), :].rearrange("p o c -> p (o c)"),
                                      mv[:, bass.ds(b * TILES + t, 1), 0], rstd[:, bass.ds(b * TILES + t, 1)],
                                      ALU.subtract, ALU.mult).then_inc(xn_ok, 1)

                def low_x(t):
                    dve.wait_ge(xh_ok, b * TILES + t + 1)
                    dve.tensor_tensor(xl[:, :, t * P:(t + 1) * P],
                                      banks[:, t % 2, 0:C].rearrange("p (k n) -> p k n", k=KC),
                                      xh[:, :, t * P:(t + 1) * P].bitcast(F32), ALU.subtract).then_inc(xl_ok, 1)

                norm_x(0)
                norm_x(1)
                low_x(0)
                norm_x(2)
                low_x(1)
                norm_x(3)
                low_x(2)
                low_x(3)
                dve.wait_ge(sq_ok, 2 * b + 1)
                dve.tensor_reduce(ss[:], sq[:].rearrange("p t (h d) -> p (t h) d", d=HD), AX.X, ALU.add)\
                    .then_inc(ss_ok, 1)
                dve.wait_ge(s0_ok, b + 1)
                step(dve.tensor_scalar(s1[:], s0[:], 1e-30, None, ALU.max), base)
                step(dve.reciprocal(s1[:], s1[:]), base)
                step(dve.tensor_tensor(s1[:], s1[:], ss[:], ALU.mult), base)
                step(dve.tensor_tensor(s1[:], s1[:], s0[:], ALU.add), base)
                step(dve.tensor_scalar(s1[:], s1[:], 0.5, EPS_NORM, ALU.mult, ALU.add), base)
                step(dve.reciprocal(rn[:], s1[:]), base)
                dve.tensor_tensor(qn[:], qkv[:, :, 0:QKC].rearrange("p t (h d) -> p t h d", d=HD),
                                  rn[:].rearrange("p (t h) -> p t h", t=TILES).unsqueeze(3)
                                  .broadcast_to([P, TILES, QKH, HD]), ALU.mult).then_inc(qn_ok, 1)
                dve.wait_ge(qn_ok, b + 1)
                dve.wait_ge(const_in, 48)
                step(dve.tensor_tensor(ra[:], qn[:], cosv[:].unsqueeze(2).broadcast_to([P, TILES, QKH, HD]),
                                       ALU.mult), base)
                dve.wait_ge(rope_b, 2 * b + 2)
                dve.tensor_tensor(ra[:], ra[:], rb[:], ALU.add).then_inc(r_ok, 1)
                dve.wait_ge(hi_ok, b + 1)
                dve.wait_ge(r_ok, b + 1)
                dve.tensor_tensor(hl[:, :, 2:4, :], ra[:].rearrange("p t h d -> p (t h) d").unsqueeze(2)
                                  .broadcast_to([P, TILES * QKH, 2, HD]),
                                  hl[:, :, 0:2, :].bitcast(F32), ALU.subtract).then_inc(hl_ok, 1)
                for t in range(TILES):
                    dve.wait_ge(qkT_ps, b * TILES + t + 1)
                    dve.tensor_copy(qT[:, 1:NH:2, t * P:(t + 1) * P],
                                    banks[64:128, 4 + 2 * (t % 2):6 + 2 * (t % 2), :]
                                    .rearrange("p a (h n) -> p (a h) n", n=P))
                    dve.tensor_copy(kT[:, 1:NKV:2, t * P:(t + 1) * P],
                                    banks[64:128, t % 2, 0:C].rearrange("p (h n) -> p h n", n=P)).then_inc(odd_ok, 1)
                for n in range(UNITS):
                    t, g = n // NKV, n % NKV
                    if t:
                        dve.wait_ge(exp_ok, b * UNITS + n + 1)
                        dve.tensor_tensor(E[:, n % 2, 0], E[:, n % 2, 0],
                                          mask[:, 0, :].unsqueeze(1).broadcast_to([P, REP, P]),
                                          ALU.mult).then_inc(mprev_ok, 1)
                    if g == 1 and t >= 1:
                        dve.wait_ge(yh_ok, b * TILES + t)
                        dve.tensor_tensor(yl[:], banks[:, 2, 0:C].rearrange("p (k n) -> p k n", k=KC),
                                          yh[:].bitcast(F32), ALU.subtract).then_inc(yl_ok, 1)
                    if g == 2 and t >= 1:
                        add_x1(dve, b, t - 1)
                    if g == NKV - 1:
                        dve.wait_ge(pv_done, b * UNITS + n + 1)
                        o = banks[:, t % 2, :].rearrange("p (h w) -> p h w", w=OSTEP)
                        step(dve.reciprocal(ri[:], o[:, :, HD]), base)
                        dve.tensor_tensor(y[:, t % 2].rearrange("p (h d) -> p h d", d=HD), o[:, :, 0:HD],
                                          ri[:].unsqueeze(2).broadcast_to([P, NH, HD]), ALU.mult).then_inc(y_ok, 1)
                dve.wait_ge(yh_ok, (b + 1) * TILES)
                dve.tensor_tensor(yl[:], banks[:, 2, 0:C].rearrange("p (k n) -> p k n", k=KC),
                                  yh[:].bitcast(F32), ALU.subtract).then_inc(yl_ok, 1)
                add_x1(dve, b, TILES - 1)
                step(dve.memset(ri[:], 0.0), base)
                step(dve.memset(ri[:], 0.0), base)
                assert steps[0] == PER_BATCH, steps

            def spread(done, var_sem, sqrt_sem, base):
                for s_, v_ in done:
                    dve.wait_ge(s_, v_)
                for t in range(NT):
                    last = dve.bn_stats(stats[:, t, :], x_sb[:, t, :])
                step(last, base)
                for t in range(NT):
                    last = dve.bn_aggr(mv[:, t, :], stats[:, t, :])
                step(last, base)
                dve.tensor_scalar(ve[:], mv[:, :, 1], EPS_LN, None, ALU.add).then_inc(var_sem, 1)
                dve.wait_ge(sqrt_sem, 1)
                step(dve.reciprocal(sr[:], sd[:]), base)
                step(dve.tensor_tensor(sr[:], sr[:], ve[:], ALU.mult), base)
                step(dve.tensor_tensor(sd[:], sd[:], sr[:], ALU.add), base)
                step(dve.tensor_scalar(sd[:], sd[:], 0.5, None, ALU.mult), base)
                step(dve.reciprocal(rstd[:], sd[:]), base)

            def norm_turn(i, ok, hi, lo):
                for j in range(2):
                    tt = i * 2 + j
                    dve.tensor_scalar(xn[:, j], x_sb[:, bass.ds(tt, 1), :].rearrange("p o c -> p (o c)"),
                                      mv[:, bass.ds(tt, 1), 0], rstd[:, bass.ds(tt, 1)],
                                      ALU.subtract, ALU.mult).then_inc(ok, 1)
                for j in range(2):
                    tt = i * 2 + j
                    dve.wait_ge(hi, tt + 1)
                    dve.tensor_tensor(nT_l[:, :, bass.ds(tt * P, P)],
                                      banks[:, j, 0:C].rearrange("p (k n) -> p k n", k=KC),
                                      nT_h[:, :, bass.ds(tt * P, P)].bitcast(F32), ALU.subtract).then_inc(lo, 1)

            end_a = first + B * PER_BATCH
            steps[0] = 0
            spread([(x1_ok, NT)], var2_ok, sqrt2_ok, end_a)
            with dve.Fori(0, NT // 2) as i:
                norm_turn(i, xn2_ok, nTh2_ok, nTl2_ok)

            def misc(job, dst):
                dve.wait_ge(misc_ps, job + 1)
                dve.tensor_copy(dst, banks[:, MISC]).then_inc(misc_out, 1)

            def max_x(head, s_, q):
                dve.wait_ge(sx_ps, head * QB + q + 1)
                dve.tensor_reduce(nmax[:, s_ * QB + q:s_ * QB + q + 1],
                                  banks[:, S_BANK + 2 * (q % 2):S_BANK + 2 * (q % 2) + 2]
                                  .rearrange("p a n -> p (a n)"), AX.X, ALU.max, negate=True).then_inc(max_ok, 1)

            def low_p(head, kb):
                dve.wait_ge(pTh_ok, head * KB + kb + 1)
                dve.tensor_tensor(pT_l[:, kb % 4], banks[:, PT_BANK + kb % 2], pT_h[:, kb % 4].bitcast(F32),
                                  ALU.subtract).then_inc(pTl_ok, 1)

            def add_o(head, s_, unit):
                dve.wait_ge(olow_ok, head + 1)
                dve.tensor_tensor(o_all[64 * s_:64 * s_ + 64, bass.ds(unit, 1), :].rearrange("p o n -> p (o n)"),
                                  banks[0:64, O_BANK], o_low[:], ALU.add).then_inc(o_free, 1)

            vr = v_raw[:].rearrange("p k d -> p (k d)")
            misc(1, k_raw[:, 512:M])
            dve.wait_ge(k_ok, 1)
            misc(4, k_raw[:, 512:M])
            misc(6, vT[:, 512:M])
            misc(8, vr)
            for q in range(QB):
                max_x(0, 0, q)
            with dve.Fori(0, UNITS_X - 1) as u:
                job = u * JOBS + JOBS - 1
                for s_ in range(2):
                    h, H, sH = u * 2 + s_, u * 2 + s_ + 1, 1 - s_
                    max_x(H, sH, 0)
                    low_p(h, 0)
                    low_p(h, 1)
                    max_x(H, sH, 1)
                    if s_ == 1:
                        misc(job + 5, k_raw[:, 512:M])
                    low_p(h, 2)
                    low_p(h, 3)
                    if s_ == 0:
                        misc(job + 1, k_raw[:, 512:M])
                    max_x(H, sH, 2)
                    if s_ == 1:
                        misc(job + 7, vT[:, 512:M])
                    low_p(h, 4)
                    low_p(h, 5)
                    max_x(H, sH, 3)
                    low_p(h, 6)
                    low_p(h, 7)
                    misc(job + (3 if s_ == 0 else 9), vr)
                    add_o(h, s_, u)
            for s_ in range(2):
                h = 2 * UNITS_X - 2 + s_
                for kb in range(KB):
                    if s_ == 0 and kb % 2 == 0:
                        max_x(h + 1, 1, kb // 2)
                    low_p(h, kb)
                if s_ == 0:
                    misc(JOBS * UNITS_X - 1, vr)
                add_o(h, s_, UNITS_X - 1)
            dve.wait_ge(ex_ok, 2 * UNITS_X * QB)
            dve.reciprocal(rsum[:].rearrange("p u h q -> p (u h q)"), sums[:]).then_inc(rs_ok, 1)
            with dve.Fori(0, B) as b:
                with dve.Fori(0, PAIRS // 2) as i:
                    for j in range(2):
                        unit = b * PAIRS + i * 2 + j
                        dve.wait_ge(rT_ps, unit + 1)
                        dve.tensor_tensor(on[:, j], banks[:, R_BANK + j],
                                          o_all[:, bass.ds(unit, 1), :].rearrange("p o n -> p (o n)"),
                                          ALU.mult).then_inc(on_ok, 1)
                dve.wait_ge(y_used, b * PAIRS + PAIRS + 2)
                xt = x_sb[:, bass.ds(b * TILES, TILES), :].rearrange("p t c -> p (t c)")
                dve.tensor_tensor(xt, banks[:, Y_BANK:Y_BANK + 2].rearrange("p a n -> p (a n)"), xt, ALU.add)\
                    .then_inc(x2_ok, 1)

            spread([(x2_ok, B)], var3_ok, sqrt3_ok, end_a)
            with dve.Fori(0, NT // 2) as i:
                norm_turn(i, xn3_ok, nTh3_ok, nTl3_ok)
            base_f = end_a
            dve.memset(gval[:], NONE)
            step(dve.memset(evalue[:], NONE), base_f)
            dve.wait_ge(sc_ok, 1)
            dve.wait_ge(gate_in, 48)
            step(dve.tensor_tensor(sfc[:], sc[:], ebias[:].unsqueeze(1).broadcast_to([P, NT, NE]), ALU.add), base_f)
            step(dve.tensor_reduce(gval[:, :, 0:GROUPS], sfc[:].rearrange("p t (g s) -> p t g s", s=GS),
                                   AX.X, ALU.max), base_f)
            for t in range(NT):
                last = dve.max(gtop[:, t], gval[:, t, 0:GROUPS])
            step(last, base_f)
            step(dve.memset(gtop[:, :, TOP_GROUPS:8], NONE), base_f)
            for t in range(NT):
                last = dve.match_replace(gout[:, t], gtop[:, t], gval[:, t], TAKEN)
            step(last, base_f)
            step(dve.tensor_scalar(gmask[:], gout[:, :, 0:GROUPS], TAKEN, None, ALU.is_ge), base_f)
            step(dve.tensor_tensor(evalue[:, :, 0:NE].rearrange("p t (g s) -> p t g s", s=GS),
                                   sfc[:].rearrange("p t (g s) -> p t g s", s=GS),
                                   gmask[:].unsqueeze(3).broadcast_to([P, NT, GROUPS, GS]), ALU.mult), base_f)
            for t in range(NT):
                last = dve.max(etop[:, t], evalue[:, t, 0:NE])
            step(last, base_f)
            step(dve.memset(etop[:, :, TOP_K:8], NONE), base_f)
            for t in range(NT):
                last = dve.match_replace(eout[:, t], etop[:, t], evalue[:, t], TAKEN)
            step(last, base_f)
            step(dve.tensor_scalar(tw[:], eout[:, :, 0:NE], TAKEN, None, ALU.is_ge), base_f)
            step(dve.tensor_tensor(tw[:], tw[:], sc[:], ALU.mult), base_f)
            step(dve.tensor_reduce(tsum[:], tw[:], AX.X, ALU.add), base_f)
            step(dve.tensor_scalar(tsum[:], tsum[:], 1e-20, None, ALU.add), base_f)
            step(dve.reciprocal(tsum[:], tsum[:]), base_f)
            step(dve.memset(comb[:], 1.0), base_f)
            step(dve.tensor_tensor(comb[:, :, 0:NE], tw[:], tsum[:].unsqueeze(2).broadcast_to([P, NT, NE]),
                                   ALU.mult), base_f)
            step(dve.tensor_scalar(comb[:, :, 0:NE], comb[:, :, 0:NE], ROUTE_SCALE, None, ALU.mult), base_f)
            step(dve.tensor_copy(parts[:, :, 0], comb[:]), base_f)
            step(dve.tensor_tensor(cres[:], comb[:], parts[:, :, 0], ALU.subtract), base_f)
            step(dve.tensor_copy(parts[:, :, 1], cres[:]), base_f)
            step(dve.tensor_tensor(comb[:], cres[:], parts[:, :, 1], ALU.subtract), base_f)
            dve.tensor_copy(parts[:, :, 2], comb[:]).then_inc(parts_ok, 1)

            def weigh_gate(n, c):
                dve.wait_ge(sg_ok, n + 1)
                dve.wait_ge(c_ps, n + 1)
                dve.tensor_tensor(gc[:, c], banks[:, C_BANK], sg[:, c], ALU.mult).then_inc(gc_ok, 1)

            def hidden(n, c):
                dve.wait_ge(u_ps, n + 1)
                dve.wait_ge(gc_ok, n + 1)
                dve.tensor_tensor(hid[:, c], banks[:, U_BANK], gc[:, c], ALU.mult).then_inc(hid_ok, 1)
                dve.wait_ge(hh_ok, n + 1)
                dve.tensor_tensor(hid_l[:, c], hid[:, c], hid_h[:, c].bitcast(F32), ALU.subtract).then_inc(hlo_ok, 1)

            with dve.Fori(0, EXPERTS // 2) as i:
                for m in range(4):
                    weigh_gate(i * 4 + m, m % 2)
                    hidden(i * 4 + m, m % 2)
            dve.wait_ge(d_ps, 2 * EXPERTS)
            for r in range(2, 4):
                dve.tensor_copy(yT[:, r], banks[:, YF_BANK + r]).then_inc(yT_d, 1)
            for r in range(NT // 2):
                dve.wait_ge(yN_ps, r + 1)
                dve.tensor_tensor(y_out[:, 2 * r:2 * r + 2].rearrange("p t c -> p (t c)"), banks[:, 4 + r],
                                  x_sb[:, 2 * r:2 * r + 2].rearrange("p t c -> p (t c)"), ALU.add).then_inc(y_fin, 1)

        @block.tensor
        def _(pe):
            pe.wait_ge(ident_ok, 2)
            with pe.Fori(0, B) as b:
                def turn_x(t):
                    pe.wait_ge(xn_ok, b * TILES + t + 1)
                    for k in range(KC):
                        mm = pe.transpose(banks[:, t % 2, k * P:(k + 1) * P], xn[:, t % 2, k * P:(k + 1) * P], ident[:])
                    mm.then_inc(xT_ps, 1)

                def project_qkv(t):
                    pe.wait_ge(xl_ok, b * TILES + t + 1)
                    if t >= 2:
                        pe.wait_ge(qkv_ok, b * TILES + t - 1)
                    three_products(pe, banks[:, 2 + t % 2, 0:QKV],
                                   [(xh[:, k, t * P:(t + 1) * P], xl[:, k, t * P:(t + 1) * P],
                                     wqkv_h[:, k, :], wqkv_l[:, k, :]) for k in range(KC)]).then_inc(qkv_ps, 1)

                turn_x(0)
                turn_x(1)
                pe.wait_ge(wa_ok, 2)
                project_qkv(0)
                turn_x(2)
                project_qkv(1)
                turn_x(3)
                project_qkv(2)
                project_qkv(3)
                pe.wait_ge(hl_ok, b + 1)
                pe.wait_ge(kswap_ok, 2 * b + 2)
                for t in range(TILES):
                    if t >= 2:
                        pe.wait_ge(even_ok, b * TILES + t - 1)
                        pe.wait_ge(odd_ok, b * TILES + t - 1)
                    r = 4 + 2 * (t % 2)
                    h0 = t * QKH
                    for i in range(NH // 2):
                        pe.transpose(banks[:, r + i // 4, (i % 4) * P:(i % 4 + 1) * P],
                                     hl[:, h0 + 2 * i:h0 + 2 * i + 2].rearrange("p h c d -> p (h c d)").bitcast(F32),
                                     ident[:])
                    for i in range(NKV // 2):
                        mm = pe.transpose(banks[:, t % 2, i * P:(i + 1) * P],
                                          hl[:, h0 + NH + 2 * i:h0 + NH + 2 * i + 2]
                                          .rearrange("p h c d -> p (h c d)").bitcast(F32), ident[:])
                    mm.then_inc(qkT_ps, 1)
                pe.wait_ge(even_ok, (b + 1) * TILES)
                pe.wait_ge(odd_ok, (b + 1) * TILES)

                def scores(n):
                    t, g = n // NKV, n % NKV
                    for j, kt in ((0, t - 1), (1, t)):
                        if kt >= 0:
                            mm = pe.matmul(banks[:, 4 + 2 * (n % 2) + j, :], kT[:, g, kt * P:(kt + 1) * P],
                                           qT[:, REP * g:REP * (g + 1), t * P:(t + 1) * P], start=True, stop=True)
                    mm.then_inc(s_ps, 1)

                def weigh(n):
                    t, g = n // NKV, n % NKV
                    pe.wait_ge(mcur_ok, b * UNITS + n + 1)
                    if t:
                        pe.wait_ge(mprev_ok, b * (UNITS - NKV) + prev_masks(n) + 1)
                    for r in range(REP):
                        h = REP * g + r
                        for j, kt in ((0, t - 1), (1, t)):
                            if kt >= 0:
                                mm = pe.matmul(banks[:, t % 2, h * OSTEP:h * OSTEP + VW], E[:, n % 2, j, r, :],
                                               va[:, kt, g, :], start=(j == 0 or t == 0), stop=(j == 1))
                    mm.then_inc(pv_done, 1)

                def turn_y(t):
                    pe.wait_ge(y_ok, b * TILES + t + 1)
                    for k in range(KC):
                        mm = pe.transpose(banks[:, 2, k * P:(k + 1) * P], y[:, t % 2, k * P:(k + 1) * P], ident[:])
                    mm.then_inc(yT_ps, 1)

                def project_y(t):
                    pe.wait_ge(yl_ok, b * TILES + t + 1)
                    if t:
                        pe.wait_ge(x1_ok, b * TILES + t)
                    three_products(pe, banks[:, 3, 0:C],
                                   [(yh[:, k, :], yl[:, k, :], wp_h[:, k, :], wp_l[:, k, :]) for k in range(KC)])\
                        .then_inc(proj_ps, 1)

                scores(0)
                for n in range(UNITS):
                    if n + 1 < UNITS:
                        scores(n + 1)
                    weigh(n)
                    if n >= NKV and n % NKV == 0:
                        turn_y(n // NKV - 1)
                    if n >= NKV and n % NKV == 1:
                        project_y(n // NKV - 1)
                turn_y(TILES - 1)
                project_y(TILES - 1)

            pe.wait_ge(x1_ok, NT)

            def turn(i, xn_sem, ps, lo):
                for j in range(2):
                    pe.wait_ge(xn_sem, i * 2 + j + 1)
                    pe.wait_ge(lo, i * 2 + j + 1)
                    for k in range(KC):
                        mm = pe.transpose(banks[:, j, k * P:(k + 1) * P], xn[:, j, k * P:(k + 1) * P], ident[:])
                    mm.then_inc(ps, 1)

            with pe.Fori(0, NT // 2) as i:
                turn(i, xn2_ok, nT2_ps, nTl2_ok)

            def begin(job):
                if not (isinstance(job, int) and job == 0):
                    pe.wait_ge(misc_out, job)

            def k_job(job, unit, s_, c, batch):
                begin(job)
                pe.wait_ge(wk_ok, unit + 1)
                src = bass.ds(batch * M + c * 512, 512)
                three_products(pe, banks[:, MISC], [(wk_h[:, s_], wk_l[:, s_], ctx_h[:, src], ctx_l[:, src])])\
                    .then_inc(misc_ps, 1)

            def q_job(job, unit, s_, batch):
                begin(job)
                pe.wait_ge(wq_ok, unit * 2 + s_ + 1)
                src = bass.ds(batch * T, T)
                three_products(pe, banks[:, MISC], [(wq_h[:, s_, k], wq_l[:, s_, k], nT_h[:, k, src], nT_l[:, k, src])
                                                    for k in range(KC)]).then_inc(misc_ps, 1)

            def v_job(job, unit, c, batch):
                begin(job)
                pe.wait_ge(wv_ok, unit + 1)
                src = bass.ds(batch * M + c * 512, 512)
                three_products(pe, banks[:, MISC], [(wv_h[:], wv_l[:], ctx_h[:, src], ctx_l[:, src])])\
                    .then_inc(misc_ps, 1)

            def turn_v(job, s_):
                begin(job)
                pe.sem_inc(pe_go, 1)
                for kb in range(KB):
                    mm = pe.transpose(banks[:, MISC, kb * XD:(kb + 1) * XD], vT[64 * s_:64 * s_ + 64, kb * P:(kb + 1) * P],
                                      ident[64 * s_:64 * s_ + 64, 64 * s_:64 * s_ + 64])
                mm.then_inc(misc_ps, 1)

            def score(head, s_, q, prologue=False):
                if q == 0:
                    pe.wait_ge(k_ok, head + 1)
                    pe.wait_ge(q_ok, head + 1)
                if not prologue or q >= 2:
                    pe.wait_ge(ex_ok, head * QB + q - 1)
                for c in range(2):
                    dst = banks[:, S_BANK + 2 * (q % 2) + c]
                    keys = k_st[:, s_, c * 512:(c + 1) * 512]
                    pe.matmul(dst, q_hh[:, s_, q * P:(q + 1) * P], keys, start=True, stop=False)
                    mm = pe.matmul(dst, q_ll[:, s_, q * P:(q + 1) * P], keys, start=False, stop=True)
                mm.then_inc(sx_ps, 1)

            def turn_p(head, s_, kb):
                if kb == 0:
                    pe.wait_ge(ex_ok, (head + 1) * QB)
                for q in range(QB):
                    mm = pe.transpose(banks[:, PT_BANK + kb % 2, q * P:(q + 1) * P],
                                      probs[:, s_, q, kb * P:(kb + 1) * P], ident[:])
                mm.then_inc(pT_ps, 1)

            def weigh_x(head, s_, kb):
                pe.wait_ge(pTl_ok, head * KB + kb + 1)
                if kb == 0:
                    pe.wait_ge(v_ok, head + 1)
                    pe.wait_ge(o_free, head + 1)
                v = v_hl[:, s_, kb].rearrange("p r d -> p (r d)")
                pe.matmul(banks[:, O_BANK], v, pT_h[:, kb % 4], start=(kb == 0), stop=False)
                mm = pe.matmul(banks[:, O_BANK], v, pT_l[:, kb % 4], start=False, stop=(kb == KB - 1))
                if kb == KB - 1:
                    mm.then_inc(o_ps, 1)

            pe.wait_ge(ctx_ok, 1)
            k_job(0, 0, 0, 0, 0)
            k_job(1, 0, 0, 1, 0)
            pe.wait_ge(nTl2_ok, NT + 2)
            q_job(2, 0, 0, 0)
            k_job(3, 0, 1, 0, 0)
            k_job(4, 0, 1, 1, 0)
            v_job(5, 0, 0, 0)
            v_job(6, 0, 1, 0)
            q_job(7, 0, 1, 0)
            turn_v(8, 0)
            for q in range(QB):
                score(0, 0, q, prologue=True)
            with pe.Fori(0, UNITS_X - 1) as u:
                job = u * JOBS + JOBS - 1
                nb = (u + 1) // PAIRS
                h, H = u * 2, u * 2 + 1
                score(H, 1, 0)
                turn_p(h, 0, 0)
                turn_p(h, 0, 1)
                k_job(job, u + 1, 0, 0, nb)
                score(H, 1, 1)
                weigh_x(h, 0, 0)
                turn_p(h, 0, 2)
                weigh_x(h, 0, 1)
                turn_p(h, 0, 3)
                k_job(job + 1, u + 1, 0, 1, nb)
                score(H, 1, 2)
                weigh_x(h, 0, 2)
                turn_p(h, 0, 4)
                weigh_x(h, 0, 3)
                turn_p(h, 0, 5)
                q_job(job + 2, u + 1, 0, nb)
                score(H, 1, 3)
                weigh_x(h, 0, 4)
                turn_p(h, 0, 6)
                weigh_x(h, 0, 5)
                turn_p(h, 0, 7)
                turn_v(job + 3, 1)
                weigh_x(h, 0, 6)
                weigh_x(h, 0, 7)
                h, H = u * 2 + 1, u * 2 + 2
                score(H, 0, 0)
                turn_p(h, 1, 0)
                turn_p(h, 1, 1)
                k_job(job + 4, u + 1, 1, 0, nb)
                score(H, 0, 1)
                k_job(job + 5, u + 1, 1, 1, nb)
                weigh_x(h, 1, 0)
                turn_p(h, 1, 2)
                weigh_x(h, 1, 1)
                turn_p(h, 1, 3)
                v_job(job + 6, u + 1, 0, nb)
                score(H, 0, 2)
                v_job(job + 7, u + 1, 1, nb)
                weigh_x(h, 1, 2)
                turn_p(h, 1, 4)
                weigh_x(h, 1, 3)
                turn_p(h, 1, 5)
                q_job(job + 8, u + 1, 1, nb)
                score(H, 0, 3)
                weigh_x(h, 1, 4)
                turn_p(h, 1, 6)
                weigh_x(h, 1, 5)
                turn_p(h, 1, 7)
                turn_v(job + 9, 0)
                weigh_x(h, 1, 6)
                weigh_x(h, 1, 7)
            h, H = 2 * UNITS_X - 2, 2 * UNITS_X - 1
            score(H, 1, 0)
            turn_p(h, 0, 0)
            turn_p(h, 0, 1)
            for q in range(1, QB):
                score(H, 1, q)
                weigh_x(h, 0, 2 * q - 2)
                turn_p(h, 0, 2 * q)
                weigh_x(h, 0, 2 * q - 1)
                turn_p(h, 0, 2 * q + 1)
            turn_v(JOBS * UNITS_X - 1, 1)
            weigh_x(h, 0, 6)
            weigh_x(h, 0, 7)
            turn_p(H, 1, 0)
            turn_p(H, 1, 1)
            for q in range(1, QB):
                weigh_x(H, 1, 2 * q - 2)
                turn_p(H, 1, 2 * q)
                weigh_x(H, 1, 2 * q - 1)
                turn_p(H, 1, 2 * q + 1)
            weigh_x(H, 1, 6)
            weigh_x(H, 1, 7)

            pe.wait_ge(wo_ok, 1)
            pe.wait_ge(ones_ok, 2)
            with pe.Fori(0, B) as b:
                for c in range(2):
                    pe.matmul(banks[:, Y_BANK + c], ones1[:], bo2[:], start=True, stop=False, skip_group_check=True)
                with pe.Fori(0, PAIRS // 2) as i:
                    for j in range(2):
                        unit = b * PAIRS + i * 2 + j
                        pe.wait_ge(rexp_ok, unit + 1)
                        for q in range(QB):
                            mm = pe.transpose(banks[:, R_BANK + j, q * P:(q + 1) * P], rexp[:, j, q], ident[:])
                        mm.then_inc(rT_ps, 1)
                    for j in range(2):
                        unit = b * PAIRS + i * 2 + j
                        pe.wait_ge(onl_ok, unit + 1)
                        pair = bass.ds(i * 2 + j, 1)
                        wh = wo_h[:, pair, :].rearrange("p o n -> p (o n)")
                        wl = wo_l[:, pair, :].rearrange("p o n -> p (o n)")
                        for q in range(QB):
                            dst = banks[:, Y_BANK + q // 2, (q % 2) * C:(q % 2 + 1) * C]
                            oh, ol = on_h[:, j, q * P:(q + 1) * P], on_l[:, j, q * P:(q + 1) * P]
                            pe.matmul(dst, oh, wh, start=False, stop=False, skip_group_check=True)
                            pe.matmul(dst, oh, wl, start=False, stop=False, skip_group_check=True)
                            mm = pe.matmul(dst, ol, wh, start=False, stop=False, skip_group_check=True)
                        mm.then_inc(y_used, 1)
                pe.wait_ge(x2_ok, b + 1)

            with pe.Fori(0, NT // 2) as i:
                turn(i, xn3_ok, nT3_ps, nTl3_ok)
            pe.wait_ge(nTl3_ok, NT + 2)
            pe.wait_ge(wg_ok, 1)
            for c in range(2):
                src = slice(c * 512, (c + 1) * 512)
                for k in range(KC):
                    for a in range(2):
                        for w in (wg_h, wg_l):
                            mm = pe.matmul(banks[0:NE, 2 + c], w[:, k], (nT_h if a == 0 else nT_l)[:, k, src],
                                           start=(k == 0 and a == 0 and w is wg_h),
                                           stop=(k == KC - 1 and a == 1 and w is wg_l))
                mm.then_inc(lg_ps, 1)
            pe.wait_ge(lgT_ok, 1)
            for t in range(NT):
                mm = pe.transpose(banks[:, 4, t * NE:(t + 1) * NE], lgT[:, t * P:(t + 1) * P], ident[0:NE, 0:NE])
            mm.then_inc(lgN_ps, 1)
            pe.wait_ge(f_const, 3)
            for r in range(4):
                pe.matmul(banks[:, YF_BANK + r], zrow[:, 0:P], zrow[:], start=True, stop=False, skip_group_check=True)
            pe.wait_ge(parts_ok, 1)
            for t in range(NT):
                mm = pe.transpose(banks[0:PARTS * EXPERTS, 5, t * 64:(t + 1) * 64].bitcast(BF16),
                                  parts[:, t].rearrange("p r e -> p (r e)"), identb[:])
            mm.then_inc(combT_ps, 1)
            pe.wait_ge(combT_ok, 1)

            def gate_up(n, j, c, e, first_step=False):
                src = slice(c * 512, (c + 1) * 512)
                if c == 0:
                    pe.wait_ge(wf_ok, e + 1)

                def product(bank, off):
                    return three_products(pe, banks[:, bank], [
                        (wf_h[:, j, k * 2 * NI + off:k * 2 * NI + off + NI],
                         wf_l[:, j, k * 2 * NI + off:k * 2 * NI + off + NI],
                         nT_h[:, k, src], nT_l[:, k, src]) for k in range(KC)])

                product(G_BANK + c, 0).then_inc(g_ps, 1)
                if not first_step:
                    pe.wait_ge(gc_ok, n)
                pe.matmul(banks[:, C_BANK], sel[:, bass.ds(e * P, P)], combT[:, src], start=True, stop=True)\
                    .then_inc(c_ps, 1)
                if not first_step:
                    pe.wait_ge(hid_ok, n)
                product(U_BANK, NI).then_inc(u_ps, 1)

            def down(n, j, c):
                pe.wait_ge(hlo_ok, n + 1)
                off = KC * 2 * NI
                for f in range(KC):
                    dst = banks[:, YF_BANK + 2 * c + f]
                    wh = wf_h[:, j, off + f * P:off + (f + 1) * P]
                    wl = wf_l[:, j, off + f * P:off + (f + 1) * P]
                    pe.matmul(dst, wh, hid_h[:, c], start=False, stop=False, skip_group_check=True)
                    pe.matmul(dst, wh, hid_l[:, c], start=False, stop=False, skip_group_check=True)
                    mm = pe.matmul(dst, wl, hid_h[:, c], start=False, stop=False, skip_group_check=True)
                mm.then_inc(d_ps, 1)

            gate_up(0, 0, 0, 0, first_step=True)
            with pe.Fori(0, EXPERTS // 2 - 1) as i:
                for m in range(4):
                    m1 = m + 1
                    gate_up(i * 4 + m1, (m1 // 2) % 2, m1 % 2, i * 2 + m1 // 2)
                    down(i * 4 + m, m // 2, m % 2)
            for m in range(4):
                n = 2 * EXPERTS - 4 + m
                if m < 3:
                    gate_up(n + 1, (m + 1) // 2, (m + 1) % 2, EXPERTS - 2 + (m + 1) // 2)
                down(n, m // 2, m % 2)
            for r in range(NT // 2):
                c = r // 2
                if r % 2 == 0:
                    pe.wait_ge(yT_a if c == 0 else yT_d, 2)
                for tt in range(2):
                    for f in range(KC):
                        tok = ((2 * r + tt) * P) % 512
                        mm = pe.transpose(banks[:, 4 + r, tt * C + f * P:tt * C + (f + 1) * P],
                                          yT[:, 2 * c + f, tok:tok + P], ident[:])
                mm.then_inc(yN_ps, 1)


def three_products(pe, dst, parts):
    n = len(parts)
    for k, (ah, al, bh, bl) in enumerate(parts):
        pe.matmul(dst, ah, bh, start=(k == 0), stop=False)
        pe.matmul(dst, ah, bl, start=False, stop=False)
        mm = pe.matmul(dst, al, bh, start=False, stop=(k == n - 1))
    return mm


def rope_table():
    theta = (1.0 / 10000.0 ** (np.arange(0, HD, 2, dtype=np.float32) / np.float32(HD))).astype(np.float32)
    freqs = np.outer(np.arange(T, dtype=np.float32), theta).astype(np.float32)
    cos, sin = np.cos(freqs), np.sin(freqs)
    return (np.concatenate([cos, cos], axis=1).astype(np.float32),
            np.concatenate([-sin, sin], axis=1).astype(np.float32))


def band_mask():
    key, query = np.arange(P)[:, None], np.arange(P)[None, :]
    return np.stack([key > query, key <= query], axis=1).astype(np.float32)


def pair_weights(wq, wk, wv):
    q = wq.reshape(KC, P, PAIRS, P).transpose(2, 1, 0, 3).reshape(PAIRS, P, KC * P)
    k = wk.reshape(P, PAIRS, P).transpose(1, 0, 2)
    v = wv.reshape(P, PAIRS, P).transpose(1, 0, 2)
    return np.concatenate([q, k, v], axis=2)


def expert_weights(gate_up, down, sh_gate, sh_up, sh_down):
    g = np.concatenate([gate_up[:, :NI], sh_gate.reshape(SHARED, NI, C)])
    u = np.concatenate([gate_up[:, NI:], sh_up.reshape(SHARED, NI, C)])
    d = np.concatenate([down, sh_down.reshape(C, SHARED, NI).transpose(1, 0, 2)])
    gu = np.concatenate([g, u], axis=1).transpose(0, 2, 1).reshape(EXPERTS, KC, P, 2 * NI).transpose(0, 2, 1, 3)
    return np.concatenate([gu.reshape(EXPERTS, P, KC * 2 * NI), d.transpose(0, 2, 1)], axis=2)


def selectors():
    one = np.equal(np.arange(PARTS * EXPERTS)[:, None] % EXPERTS, np.arange(EXPERTS)[None, :])
    return np.repeat(one, P, axis=1).astype(np.dtype("bfloat16"))


def kernel(**inputs):
    import concourse.bacc as bacc
    from concourse.bass_utils import run_bass_kernel_spmd

    a = {k: np.asarray(v) for k, v in inputs.items()}
    cosv, sinv = rope_table()
    arrays = {
        "x": a["x"],
        "wqkv": np.concatenate([a["L0_attn_Wq"], a["L0_attn_Wkv"]], axis=0).T,
        "wp": a["L0_attn_Wproj"].T,
        "ctxT": a["ctx_512"].reshape(B * M, CD).T,
        "wx": pair_weights(a["L0_xattn_Wq"], a["L0_xattn_Wk"], a["L0_xattn_Wv"]),
        "wo": a["L0_xattn_Wo"],
        "bo2": np.concatenate([a["L0_xattn_bo"], a["L0_xattn_bo"]])[None, :],
        "wf": expert_weights(a["L0_ffn_experts_gate_up"], a["L0_ffn_experts_down"], a["L0_ffn_shared_gate_w"],
                             a["L0_ffn_shared_up_w"], a["L0_ffn_shared_down_w"]),
        "wg": a["L0_ffn_gate_weight"].T,
        "ebias": a["L0_ffn_e_score_correction_bias"],
        "sel": selectors(),
        "cosv": cosv, "sinv": sinv, "mask": band_mask(),
    }
    arrays = {k: np.ascontiguousarray(v) for k, v in arrays.items()}
    nc = bacc.Bacc("TRN2", target_bir_lowering=False, num_devices=1)
    ins = {k: nc.dram_tensor(f"{k}_dram", v.shape, mybir.dt.from_np(v.dtype), kind="ExternalInput").ap()
           for k, v in arrays.items()}
    out = nc.dram_tensor("out_dram", (B, T, C), F32, kind="ExternalOutput").ap()
    mk_decoder(nc, ins, out)
    r = run_bass_kernel_spmd(nc, [{f"{k}_dram": v for k, v in arrays.items()}], core_ids=[0])
    return r.results[0]["out_dram"]
```

```python
from contextlib import ExitStack

import numpy as np

import concourse.bass as bass
from concourse import mybir

ACT = mybir.ActivationFunctionType
ALU = mybir.AluOpType
AX = mybir.AxisListType
F32 = mybir.dt.float32
F32R = mybir.dt.float32r
BF16 = mybir.dt.bfloat16

P = 128
B, T, C = 2, 512, 256
TILES = T // P
NT = B * TILES
KC = C // P
EPS_LN = 1e-5
EPS_NORM = 1e-6

NH, NKV, HD = 16, 4, 16
REP = NH // NKV
QKH = NH + NKV
QKC = QKH * HD
QKV = QKC + NKV * HD
SCALE_A = HD ** -0.5
GW = REP * HD

XH, XD, M, CD = 16, 64, 1024, 128
SCALE_X = XD ** -0.5
PAIRS = XH // 2
UNITS_X = B * PAIRS
QB = T // P
KB = M // P
QKV_X = (KC + 2) * P
WPAIR = QKV_X + C
CTX_PIECE = B * M // NT
JOBS = 5

NE, NI, GROUPS, TOP_GROUPS, TOP_K, ROUTE_SCALE, SHARED = 32, 128, 8, 4, 6, 2.5, 2
GS = NE // GROUPS
EXPERTS = NE + SHARED
GU = KC * 2 * NI
WEXP = GU + C
PARTS = 3
NONE, TAKEN = -1e30, 1e30


def mk_decoder(nc, ins, out):
    ctx = ExitStack()
    stage_a = ExitStack()
    with ctx:
        def sb(name, shape, dt, stack=ctx):
            return stack.enter_context(nc.sbuf_tensor(name, shape, dt))

        def sem(name):
            return ctx.enter_context(nc.semaphore(name))

        banks = ctx.enter_context(nc.psum_tensor("banks", [P, 8, 512], F32))

        ident = sb("ident", [P, P], F32)
        identb = sb("identb", [P, P], BF16)
        x_sb = sb("x_sb", [P, NT, C], F32)
        stats = sb("stats", [P, NT, 6], F32)
        mv = sb("mv", [P, NT, 2], F32)
        ve = sb("ve", [P, NT], F32)
        sd = sb("sd", [P, NT], F32)
        sr = sb("sr", [P, NT], F32)
        rstd = sb("rstd", [P, NT], F32)
        xn = sb("xn", [P, 2, C], F32)
        primer = sb("primer", [P, NT], F32)
        nT_h = sb("nT_h", [P, KC, B * T], F32R)
        nT_l = sb("nT_l", [P, KC, B * T], F32R)
        wraw = sb("wraw", [P, 2, WPAIR], F32)
        ctx_h = sb("ctx_h", [P, B * M], F32R)
        ctx_l = sb("ctx_l", [P, B * M], F32R)

        def sa(name, shape, dt):
            return sb(name, shape, dt, stage_a)

        wqkv = sa("wqkv", [P, KC, QKV], F32)
        wqkv_h = sa("wqkv_h", [P, KC, QKV], F32R)
        wqkv_l = sa("wqkv_l", [P, KC, QKV], F32R)
        wp = sa("wp", [P, KC, C], F32)
        wp_h = sa("wp_h", [P, KC, C], F32R)
        wp_l = sa("wp_l", [P, KC, C], F32R)
        cosv = sa("cosv", [P, TILES, HD], F32)
        sinv = sa("sinv", [P, TILES, HD], F32)
        window = sa("window", [P, P], F32)
        causal = sa("causal", [P, P], BF16)
        xh = sa("xh", [P, KC, T], F32R)
        xl = sa("xl", [P, KC, T], F32R)
        qkv = sa("qkv", [P, NT, QKV], F32)
        sq = sa("sq", [P, TILES, QKC], F32)
        ss = sa("ss", [P, NT * QKH], F32)
        s0 = sa("s0", [P, NT * QKH], F32)
        s1 = sa("s1", [P, NT * QKH], F32)
        qn = sa("qn", [P, QKH, HD], F32)
        ra = sa("ra", [P, QKH, HD], F32)
        rb = sa("rb", [P, QKH, HD], F32)
        hl = sa("hl", [P, 2, QKH, 4, HD], F32R)
        qT = sa("qT", [64, 2, NH, P], F32R)
        kT = sa("kT", [64, TILES, NKV, P], F32R)
        va = sa("va", [P, TILES, NKV, REP, 2 * GW], F32)
        E = sa("E", [P, 2, 2, REP, P], F32)
        y = sa("y", [P, 2, KC, P], F32)
        rowsum = sa("rowsum", [P, 2, KC, P], F32)
        yh = sa("yh", [P, KC, P], F32R)
        yl = sa("yl", [P, KC, P], F32R)

        ctxT = sa("ctxT", [P, B * M], F32)
        stage_a.close()

        stage_b = ExitStack()

        def sx(name, shape, dt):
            return sb(name, shape, dt, stage_b)

        wx_h = sx("wx_h", [P, QKV_X], F32R)
        wx_l = sx("wx_l", [P, QKV_X], F32R)
        k_st = sx("k_st", [P, B, 2, M], F32R)
        q_hh = sx("q_hh", [P, B, 2, T], F32R)
        q_ll = sx("q_ll", [P, B, 2, T], F32R)
        v_raw = sx("v_raw", [P, 2, 512], F32)
        v_hl = sx("v_hl", [P, B, KB, 2, 2, XD], F32R)
        nmax = sx("nmax", [P, 2 * QB], F32)
        pT_h = sx("pT_h", [P, 4, T], F32R)
        pT_l = sx("pT_l", [P, 4, T], F32R)
        o_low = sx("o_low", [P, T], F32)
        o_all = sx("o_all", [P, UNITS_X, T], F32)
        sums = sx("sums", [P, 2 * UNITS_X * QB], F32)
        rsum = sx("rsum", [P, UNITS_X, 2, QB], F32)
        wo_h = sx("wo_h", [P, PAIRS, C], F32R)
        wo_l = sx("wo_l", [P, PAIRS, C], F32R)
        bo2 = sx("bo2", [1, 2 * C], F32)
        ones1 = sx("ones1", [1, P], F32)
        heads = ExitStack()
        probs = sb("probs", [P, 2, QB, M], F32, heads)
        heads.close()
        before = ExitStack()
        xn2 = sb("xn2", [P, 4, C], F32, before)
        before.close()
        rexp = sx("rexp", [P, 4, QB, P], F32)
        on = sx("on", [P, 4, T], F32)
        on_h = sx("on_h", [P, 4, T], F32R)
        on_l = sx("on_l", [P, 4, T], F32R)
        stage_b.close()

        stage_f = ExitStack()

        def sf(name, shape, dt):
            return sb(name, shape, dt, stage_f)

        xn3 = sf("xn3", [P, 4, C], F32)
        wf_raw = sf("wf_raw", [P, 2, WEXP], F32)
        wf_h = sf("wf_h", [P, 2, WEXP], F32R)
        wf_l = sf("wf_l", [P, 2, WEXP], F32R)
        sel = sf("sel", [PARTS * NE, NE * P], BF16)
        wg = sf("wg", [P, KC, NE], F32)
        wg_h = sf("wg_h", [P, KC, NE], F32R)
        wg_l = sf("wg_l", [P, KC, NE], F32R)
        ebias = sf("ebias", [P, NE], F32)
        zrow = sf("zrow", [1, 512], F32)
        lgT = sf("lgT", [NE, B * T], F32)
        sc = sf("sc", [P, NT, NE], F32)
        sfc = sf("sfc", [P, NT, NE], F32)
        gval = sf("gval", [P, NT, GROUPS + 8], F32)
        gtop = sf("gtop", [P, NT, 8], F32)
        gout = sf("gout", [P, NT, GROUPS + 8], F32)
        gmask = sf("gmask", [P, NT, GROUPS], F32)
        evalue = sf("evalue", [P, NT, NE + 8], F32)
        etop = sf("etop", [P, NT, 8], F32)
        eout = sf("eout", [P, NT, NE + 8], F32)
        tw = sf("tw", [P, NT, NE], F32)
        tsum = sf("tsum", [P, NT], F32)
        comb = sf("comb", [P, NT, NE], F32)
        cres = sf("cres", [P, NT, NE], F32)
        parts = sf("parts", [P, NT, PARTS, NE], BF16)
        combT = sf("combT", [PARTS * NE, B * T], BF16)
        sg = sf("sg", [P, 2, 512], F32)
        gc = sf("gc", [P, 2, 512], F32)
        hid = sf("hid", [P, 2, 512], F32)
        hid_h = sf("hid_h", [P, 2, 512], F32R)
        hid_l = sf("hid_l", [P, 2, 512], F32R)
        yT = sf("yT", [P, 4, 512], F32)
        y_out = sf("y_out", [P, NT, C], F32)
        stage_f.close()

        YF_BANK, G_BANK, C_BANK, U_BANK = 0, 4, 6, 7
        L_BANKS = (C_BANK, G_BANK + 1)

        S_BANK, PT_BANK, O_BANK, MISC = 0, 4, 6, 7
        Y_BANK, R_BANK = 0, 4

        ctx_in = sem("ctx_in")
        ctx_hi = sem("ctx_hi")
        ctx_ok = sem("ctx_ok")
        wx_in = sem("wx_in")
        bo_in = sem("bo_in")
        wo_ok = sem("wo_ok")
        wx_used = sem("wx_used")
        wqk_ok = sem("wqk_ok")
        wv_ok = sem("wv_ok")
        pool_step = sem("pool_step")
        pool_go = sem("pool_go")
        pe_go = sem("pe_go")
        misc_ps = sem("misc_ps")
        misc_out = sem("misc_out")
        half_out = sem("half_out")
        mh_ok = sem("mh_ok")
        qlo_ok = sem("qlo_ok")
        q_low = sem("q_low")
        q_ok = sem("q_ok")
        v_ok = sem("v_ok")
        sx_ps = sem("sx_ps")
        max_ok = sem("max_ok")
        ex_ok = sem("ex_ok")
        pT_ps = sem("pT_ps")
        pTh_ok = sem("pTh_ok")
        pTl_ok = sem("pTl_ok")
        o_ps = sem("o_ps")
        o_sum = sem("o_sum")
        o_free = sem("o_free")
        rs_ok = sem("rs_ok")
        rexp_ok = sem("rexp_ok")
        rT_ps = sem("rT_ps")
        on_ok = sem("on_ok")
        onh_ok = sem("onh_ok")
        onl_ok = sem("onl_ok")
        y_used = sem("y_used")
        bias_ok = sem("bias_ok")
        var2_ok = sem("var2_ok")
        sqrt2_ok = sem("sqrt2_ok")
        xn2_ok = sem("xn2_ok")
        nT2_ps = sem("nT2_ps")
        nTh2_ok = sem("nTh2_ok")
        nTl2_ok = sem("nTl2_ok")
        x2_ok = sem("x2_ok")

        var3_ok = sem("var3_ok")
        sqrt3_ok = sem("sqrt3_ok")
        xn3_ok = sem("xn3_ok")
        nT3_ps = sem("nT3_ps")
        nTh3_ok = sem("nTh3_ok")
        nTl3_ok = sem("nTl3_ok")
        gate_in = sem("gate_in")
        f_const = sem("f_const")
        wg_hi = sem("wg_hi")
        wg_ok = sem("wg_ok")
        lg_ps = sem("lg_ps")
        lgT_ok = sem("lgT_ok")
        lgN_ps = sem("lgN_ps")
        sc_ok = sem("sc_ok")
        parts_ok = sem("parts_ok")
        combT_ps = sem("combT_ps")
        combT_ok = sem("combT_ok")
        wf_in = [sem("wf_in0"), sem("wf_in1")]
        wf_step = sem("wf_step")
        wgu_ok = sem("wgu_ok")
        wdn_ok = sem("wdn_ok")
        g_ps = sem("g_ps")
        c_ps = sem("c_ps")
        u_ps = sem("u_ps")
        d_ps = sem("d_ps")
        sg_ok = sem("sg_ok")
        gc_ok = sem("gc_ok")
        hid_ok = sem("hid_ok")
        hh_ok = sem("hh_ok")
        hlo_ok = sem("hlo_ok")
        yT_a = sem("yT_a")
        yT_d = sem("yT_d")
        yN_ps = sem("yN_ps")
        y_fin = sem("y_fin")

        x_in = sem("x_in")
        wa_in = sem("wa_in")
        wp_in = sem("wp_in")
        const_in = sem("const_in")
        ident_ok = sem("ident_ok")
        ones_ok = sem("ones_ok")
        wa_hi = sem("wa_hi")
        wa_ok = sem("wa_ok")
        wp_ok = sem("wp_ok")
        ra_ok = sem("ra_ok")
        v_placed = sem("v_placed")
        rec_ok = sem("rec_ok")
        yn_ok = sem("yn_ok")
        var_ok = sem("var_ok")
        sqrt_ok = sem("sqrt_ok")
        rope_b = sem("rope_b")
        dve_step = sem("dve_step")
        xn_ok = sem("xn_ok")
        xT_ps = sem("xT_ps")
        xh_ok = sem("xh_ok")
        xl_ok = sem("xl_ok")
        qkv_ps = sem("qkv_ps")
        qkv_ok = sem("qkv_ok")
        ss_ok = sem("ss_ok")
        s0_ok = sem("s0_ok")
        qn_ok = sem("qn_ok")
        r_ok = sem("r_ok")
        hi_ok = sem("hi_ok")
        hl_ok = sem("hl_ok")
        qkT_ps = sem("qkT_ps")
        even_ok = sem("even_ok")
        odd_ok = sem("odd_ok")
        s_ps = sem("s_ps")
        exp_ok = sem("exp_ok")
        mask_ok = sem("mask_ok")
        pv_done = sem("pv_done")
        y_ok = sem("y_ok")
        yh_ok = sem("yh_ok")
        yl_ok = sem("yl_ok")
        proj_ps = sem("proj_ps")
        x1_ok = sem("x1_ok")
        stats_ok = sem("stats_ok")
        out_done = sem("out_done")

        UNITS = TILES * NKV
        def ahead(b, t):
            return b * TILES + t + 2 if t + 2 < TILES else (b + 1) % B * TILES + t + 2 - TILES

        def place(unit, name):
            order = ("k0", "k1", "q", "v0", "v1") if isinstance(unit, int) and unit == 0 else ("q", "k0", "k1", "v0", "v1")
            return unit * JOBS + order.index(name)

        def halves(unit, name):
            order = {"k0": 0, "k1": 2, "q": 4} if isinstance(unit, int) and unit == 0 else {"q": 0, "k0": 4, "k1": 6}
            return unit * 8 + order[name]

        block = ctx.enter_context(nc.Block())

        @block.sync
        def _(sp):
            sp.dma_start(x_sb[:], ins["x"].rearrange("b (t p) c -> p (b t) c", p=P)).then_inc(x_in, 16)
            sp.dma_start(wqkv[:], ins["wqkv"].rearrange("(k p) n -> p k n", p=P)).then_inc(wa_in, 16)
            sp.dma_start(wp[:], ins["wp"].rearrange("(k p) n -> p k n", p=P)).then_inc(wp_in, 16)
            sp.dma_start(cosv[:], ins["cosv"].rearrange("(t p) d -> p t d", p=P)).then_inc(const_in, 16)
            sp.dma_start(sinv[:], ins["sinv"].rearrange("(t p) d -> p t d", p=P)).then_inc(const_in, 16)
            sp.dma_start(window[:], ins["window"]).then_inc(const_in, 16)
            sp.dma_start(causal[:], ins["causal"]).then_inc(const_in, 16)
            sp.sem_inc(o_free, 1)
            sp.sem_inc(o_sum, 2)
            sp.sem_inc(ss_ok, TILES)
            sp.sem_inc(pv_done, 2)
            sp.sem_inc(y_ok, 2)
            sp.sem_inc(nTl2_ok, 4)
            sp.dma_start(ctxT[:], ins["ctxT"]).then_inc(ctx_in, 16)

            def load_pair(pair):
                sp.dma_start(wraw[:, bass.ds(pair % 2, 1), :].rearrange("p o n -> p (o n)"),
                             ins["wx"][bass.ds(pair, 1)].rearrange("o p n -> p (o n)")).then_inc(wx_in, 16)

            sp.dma_start(wraw[:, 0], ins["wx"][0]).then_inc(wx_in, 16)
            sp.wait_ge(wx_in, 16)
            sp.dma_start(wraw[:, 1], ins["wx"][1]).then_inc(wx_in, 16)
            sp.wait_ge(x1_ok, NT)
            sp.dma_start(bo2[:], ins["bo2"]).then_inc(bo_in, 16)
            with sp.Fori(0, PAIRS - 2) as p:
                sp.wait_ge(wx_used, p + 1)
                sp.wait_ge(wx_in, p * 16 + 32)
                load_pair(p + 2)
            sp.wait_ge(o_free, 2 * UNITS_X + 1)
            sp.dma_start(wg[:], ins["wg"].rearrange("(k p) e -> p k e", p=P)).then_inc(gate_in, 16)
            sp.dma_start(ebias[:], ins["ebias"].partition_broadcast(P)).then_inc(gate_in, 16)
            sp.dma_start(sel[:], ins["sel"]).then_inc(gate_in, 16)
            for j in range(2):
                sp.dma_start(wf_raw[:, j], ins["wf"][j]).then_inc(wf_in[j], 16)
            with sp.Fori(1, EXPERTS // 2) as i:
                for j in range(2):
                    sp.wait_ge(wdn_ok, i * 2 + j - 1)
                    sp.dma_start(wf_raw[:, j], ins["wf"][bass.ds(i * 2 + j, 1)].rearrange("o p n -> p (o n)"))\
                        .then_inc(wf_in[j], 16)
            o_v = out.rearrange("b (t p) c -> p (b t) c", p=P)
            for r in range(NT // 2):
                sp.wait_ge(y_fin, r + 1)
                sp.dma_start(o_v[:, 2 * r:2 * r + 2], y_out[:, 2 * r:2 * r + 2]).then_inc(out_done, 16)
            sp.wait_ge(out_done, 16 * (NT // 2))

        @block.gpsimd
        def _(pool):
            pool.memset(ident[:], 0.0).then_inc(ident_ok, 1)
            pool.wait_ge(ident_ok, 1)
            pool.affine_select(out=ident[:], in_=ident[:], compare_op=ALU.not_equal, fill=1.0, base=0,
                               pattern=[[-1, P]], channel_multiplier=1).then_inc(ident_ok, 1)
            pool.memset(identb[:], 0.0).then_inc(ident_ok, 1)
            pool.wait_ge(ident_ok, 3)
            pool.affine_select(out=identb[:], in_=identb[:], compare_op=ALU.not_equal, fill=1.0, base=0,
                               pattern=[[-1, P]], channel_multiplier=1).then_inc(ident_ok, 1)
            pool.wait_ge(wa_in, 16)
            pool.tensor_copy(wqkv_h[:], wqkv[:]).then_inc(wa_hi, 1)
            pool.wait_ge(wa_hi, 1)
            pool.tensor_tensor(wqkv_l[:], wqkv[:], wqkv_h[:].bitcast(F32), ALU.subtract).then_inc(wa_ok, 1)
            pool.memset(va[:], 0.0).then_inc(ones_ok, 1)
            pool.wait_ge(ones_ok, 1)
            for r in range(REP):
                pool.memset(va[:, :, :, r, GW + r * HD:GW + (r + 1) * HD], 1.0).then_inc(ones_ok, 1)
            pool.wait_ge(wp_in, 16)
            pool.tensor_copy(wp_h[:], wp[:]).then_inc(wa_hi, 1)
            pool.wait_ge(wa_hi, 2)
            pool.tensor_tensor(wp_l[:], wp[:], wp_h[:].bitcast(F32), ALU.subtract).then_inc(wp_ok, 1)
            pool.wait_ge(const_in, 64)

            def rotate(f, t):
                if not (isinstance(f, int) and f == 0):
                    pool.wait_ge(hl_ok, f * 2)
                pool.wait_ge(qn_ok, f + 1)
                pool.sem_inc(pool_go, 1)
                for half in range(2):
                    lo, hi = (0, HD // 2) if half == 0 else (HD // 2, HD)
                    src = slice(HD // 2, HD) if half == 0 else slice(0, HD // 2)
                    pool.tensor_tensor(rb[:, :, lo:hi], qn[:, :, src],
                                       sinv[:, t % TILES, lo:hi].unsqueeze(1).broadcast_to([P, QKH, HD // 2]),
                                       ALU.mult).then_inc(rope_b, 1)
                pool.wait_ge(rope_b, f * 2 + 2)
                pool.wait_ge(ra_ok, f + 1)
                pool.tensor_tensor(rb[:], ra[:], rb[:], ALU.add).then_inc(r_ok, 1)
                pool.wait_ge(r_ok, f + 1)
                pool.wait_ge(hi_ok, f + 1)
                for heads_, los, his in ((slice(0, NH), slice(2, 4), slice(0, 2)), (slice(NH, QKH), slice(1, 4, 2), slice(0, 4, 2))):
                    raw = rb[:, heads_].unsqueeze(2).broadcast_to([P, heads_.stop - heads_.start, 2, HD])
                    pool.tensor_tensor(hl[:, t % 2, heads_, los, :], raw, hl[:, t % 2, heads_, his, :].bitcast(F32),
                                       ALU.subtract).then_inc(hl_ok, 1)

            def split_ctx(c):
                cols = bass.ds(c * CTX_PIECE, CTX_PIECE)
                pool.sem_inc(pool_go, 1)
                pool.tensor_copy(ctx_h[:, cols], ctxT[:, cols]).then_inc(ctx_hi, 1)
                pool.wait_ge(ctx_hi, c + 1)
                pool.sem_inc(pool_go, 1)
                pool.tensor_tensor(ctx_l[:, cols], ctxT[:, cols], ctx_h[:, cols].bitcast(F32), ALU.subtract)\
                    .then_inc(ctx_ok, 1)

            rotate(0, 0)
            rotate(1, 1)
            pool.wait_ge(ctx_in, 16)
            with pool.Fori(0, B) as b:
                for t in range(TILES):
                    rotate(b * TILES + t + 2, t + 2)
                    split_ctx(b * TILES + t)

            pool.wait_ge(x1_ok, NT)
            pool.memset(ones1[:], 1.0).then_inc(ones_ok, 1)

            psteps = [0]

            def split(h_out, l_out, raw, base, ready, waits):
                for s_, v_ in waits:
                    pool.wait_ge(s_, v_)
                pool.sem_inc(pool_go, 1)
                psteps[0] += 1
                pool.tensor_copy(h_out, raw).then_inc(pool_step, 1)
                pool.wait_ge(pool_step, base + psteps[0])
                pool.sem_inc(pool_go, 1)
                pool.tensor_tensor(l_out, raw, h_out.bitcast(F32), ALU.subtract).then_inc(*ready)

            def raw_w(pair, lo, hi):
                slot = bass.ds(pair % 2, 1) if not isinstance(pair, int) else slice(pair % 2, pair % 2 + 1)
                return wraw[:, slot, lo:hi].rearrange("p o n -> p (o n)")

            QK = (KC + 1) * P

            def split_wqk(pair, base, waits):
                split(wx_h[:, 0:QK], wx_l[:, 0:QK], raw_w(pair, 0, QK), base, (wqk_ok, 1), waits)

            def split_wv(pair, base, waits):
                split(wx_h[:, QK:], wx_l[:, QK:], raw_w(pair, QK, QKV_X), base, (wv_ok, 1), waits)

            def split_wo(pair, base):
                slot = bass.ds(pair, 1) if not isinstance(pair, int) else slice(pair, pair + 1)
                wh, wl = (w[:, slot, :].rearrange("p o n -> p (o n)") for w in (wo_h, wo_l))
                split(wh, wl, raw_w(pair, QKV_X, WPAIR), base, (wo_ok, 1), [])
                pool.wait_ge(wo_ok, pair + 1)
                pool.sem_inc(wx_used, 1)

            def double_q(unit, b):
                pool.wait_ge(qlo_ok, unit)
                pool.sem_inc(pool_go, 1)
                pool.tensor_copy(q_ll[0:64, b, 1], q_ll[64:P, b, 1].bitcast(F32)).then_inc(q_low, 1)
                pool.wait_ge(q_low, unit)
                pool.sem_inc(pool_go, 1)
                pool.tensor_copy(q_ll[64:P, b, 0], q_ll[0:64, b, 0].bitcast(F32)).then_inc(q_ok, 1)
                pool.wait_ge(q_ok, unit + 1)

            def split_v(unit, b, a, base):
                half = v_hl[:, b, 4 * a:4 * a + 4]
                split(half[:, :, :, 0], half[:, :, :, 1], v_raw[:, a].rearrange("p (k h d) -> p k h d", k=4, h=2), base,
                      (v_ok, 1), [(misc_out, place(unit, f"v{a}") + 1)])
                if a == 1:
                    pool.wait_ge(v_ok, unit * 2 + 2)

            def add_o(head, h, unit):
                pool.wait_ge(o_free, head + 2)
                pool.sem_inc(pool_go, 1)
                rows = slice(64 * h, 64 * h + 64)
                dst = o_all[rows, bass.ds(unit, 1) if not isinstance(unit, int) else slice(unit, unit + 1), :]\
                    .rearrange("p o n -> p (o n)")
                pool.tensor_tensor(dst, dst, o_low[rows], ALU.add).then_inc(o_sum, 1)
                pool.wait_ge(o_sum, head + 3)

            split_wqk(0, 0, [(wx_in, 16)])
            split_wv(0, 0, [])
            for a in range(2):
                split_v(0, 0, a, 0)
            split_wo(0, 0)
            first_split = psteps[0]
            PER_PAIR = 7
            with pool.Fori(0, PAIRS - 1) as p:
                psteps[0] = 0
                base = p * PER_PAIR + first_split
                for b in range(B):
                    unit, nu = p * 2 + b, p * 2 + b + 1
                    double_q(nu, 1 - b)
                    if b == 0:
                        split_wqk(p + 1, base, [(wx_in, p * 16 + 32), (misc_ps, nu * JOBS + 3)])
                    add_o(unit * 2, 0, unit)
                    for a in range(2):
                        split_v(nu, 1 - b, a, base)
                    if b == 0:
                        split_wv(p + 1, base, [(misc_ps, nu * JOBS + 5)])
                        split_wo(p + 1, base)
                    add_o(unit * 2 + 1, 1, unit)
                assert psteps[0] == PER_PAIR
            psteps[0] = 0
            end_base = first_split + (PAIRS - 1) * PER_PAIR
            unit = UNITS_X - 2
            double_q(unit + 1, 1)
            add_o(unit * 2, 0, unit)
            for a in range(2):
                split_v(unit + 1, 1, a, end_base)
            add_o(unit * 2 + 1, 1, unit)
            for h in range(2):
                add_o(unit * 2 + 2 + h, h, unit + 1)

            def low_on(v, j):
                pool.wait_ge(onh_ok, v + 1)
                pool.tensor_tensor(on_l[:, j], on[:, j], on_h[:, j].bitcast(F32), ALU.subtract).then_inc(onl_ok, 1)

            with pool.Fori(0, PAIRS // 4) as i:
                for j in range(4):
                    low_on(i * 4 + j, j)
            pool.memset(zrow[:], 0.0).then_inc(f_const, 1)

            def split_part(j, e, cols, first_step, ready):
                pool.tensor_copy(wf_h[:, j, cols], wf_raw[:, j, cols]).then_inc(wf_step, 1)
                pool.wait_ge(wf_step, e * 2 + first_step)
                pool.sem_inc(pool_go, 1)
                pool.tensor_tensor(wf_l[:, j, cols], wf_raw[:, j, cols], wf_h[:, j, cols].bitcast(F32), ALU.subtract)\
                    .then_inc(ready, 1)

            for v in range(PAIRS):
                low_on(PAIRS + v, v % 4)
                if v == 1:
                    pool.wait_ge(gate_in, 48)
                    pool.tensor_copy(wg_h[:], wg[:]).then_inc(wg_hi, 1)
                    pool.wait_ge(wg_hi, 1)
                    pool.tensor_tensor(wg_l[:], wg[:], wg_h[:].bitcast(F32), ALU.subtract).then_inc(wg_ok, 1)
                if v == 3:
                    pool.wait_ge(wf_in[0], 16)
                    split_part(0, 0, slice(0, GU), 1, wgu_ok)
                if v == 5:
                    split_part(0, 0, slice(GU, WEXP), 2, wdn_ok)
            pool.wait_ge(wf_in[1], 16)
            split_part(1, 1, slice(0, GU), 1, wgu_ok)
            split_part(1, 1, slice(GU, WEXP), 2, wdn_ok)
            with pool.Fori(1, EXPERTS // 2) as i:
                for j in range(2):
                    e = i * 2 + j
                    pool.wait_ge(wf_in[j], i * 16 + 16)
                    pool.wait_ge(u_ps, i * 4 + 2 * j - 2)
                    pool.sem_inc(pool_go, 1)
                    split_part(j, e, slice(0, GU), 1, wgu_ok)
                    pool.wait_ge(d_ps, i * 4 + 2 * j - 2)
                    pool.sem_inc(pool_go, 1)
                    split_part(j, e, slice(GU, WEXP), 2, wdn_ok)

        @block.scalar
        def _(act):
            def copy_yh(b, t):
                act.wait_ge(yn_ok, (b * TILES + t + 1) * KC)
                if t:
                    act.wait_ge(proj_ps, b * TILES + t)
                act.activation(yh[:], y[:, t % 2], ACT.Copy).then_inc(yh_ok, 1)

            act.wait_ge(var_ok, 1)
            act.activation(sd[:], ve[:], ACT.Sqrt).then_inc(sqrt_ok, 1)
            with act.Fori(0, B) as b:
                def copy_xh(t):
                    act.wait_ge(xT_ps, b * TILES + t + 1)
                    act.activation(xh[:, :, t * P:(t + 1) * P],
                                   banks[:, t % 2, 0:C].rearrange("p (k n) -> p k n", k=KC),
                                   ACT.Copy).then_inc(xh_ok, 1)

                def copy_qkv(t):
                    act.wait_ge(qkv_ps, b * TILES + t + 1)
                    act.activation(qkv[:, bass.ds(b * TILES + t, 1), :].rearrange("p o n -> p (o n)"),
                                   banks[:, 2 + t % 2, 0:QKV], ACT.Copy)
                    act.wait_ge(ss_ok, b * TILES + t + 1)
                    act.activation(sq[:, t], banks[:, 2 + t % 2, 0:QKC], ACT.Square).then_inc(qkv_ok, 1)

                copy_xh(0)
                copy_xh(1)
                copy_qkv(0)
                copy_xh(2)
                copy_qkv(1)
                copy_xh(3)
                copy_qkv(2)
                copy_qkv(3)
            act.wait_ge(ss_ok, NT + TILES)
            act.activation(s0[:], ss[:], ACT.Sqrt).then_inc(s0_ok, 1)
            act.activation(primer[:], sd[:], ACT.Exp)

            def high_heads(f, t):
                act.wait_ge(r_ok, f + 1)
                act.activation(hl[:, t % 2, 0:NH, 0:2, :], rb[:, 0:NH].unsqueeze(2).broadcast_to([P, NH, 2, HD]), ACT.Copy)
                act.activation(hl[:, t % 2, NH:QKH, 0:4:2, :], rb[:, NH:QKH].unsqueeze(2).broadcast_to([P, NKV, 2, HD]),
                               ACT.Copy).then_inc(hi_ok, 1)

            def place_v(tile, t):
                tile = slice(tile, tile + 1) if isinstance(tile, int) else bass.ds(tile, 1)
                for r in range(REP):
                    last = act.activation(va[:, t % TILES, :, r, r * HD:(r + 1) * HD],
                                          qkv[:, tile, QKC:QKV].rearrange("p o (g d) -> p (o g) d", g=NKV), ACT.Copy)
                last.then_inc(v_placed, 1)

            def even_heads(f, t, k):
                act.wait_ge(qkT_ps, f * 3 + k + 1)
                src = banks[0:64, 2, :].rearrange("p (h n) -> p h n", n=P)
                if k < 2:
                    act.activation(qT[:, t % 2, 8 * k:8 * k + 8:2], src, ACT.Copy).then_inc(even_ok, 1)
                else:
                    act.activation(kT[:, t % TILES, 0:NKV:2], src[:, 0:NKV // 2], ACT.Copy).then_inc(even_ok, 1)

            def exp_unit(unit, n):
                act.wait_ge(s_ps, unit + 1)
                act.wait_ge(pv_done, unit + 1)
                k0 = 0 if n // NKV else 1
                r = 4 + 2 * (n % 2)
                act.activation(E[:, n % 2, k0:2], banks[:, r + k0:r + 2, :].rearrange("p a (h n) -> p a h n", n=P),
                               ACT.Exp, scale=SCALE_A).then_inc(exp_ok, 1)

            def copy_out(unit, n):
                t, g = n // NKV, n % NKV
                act.wait_ge(pv_done, unit + 3)
                rows = slice(GW * (g % 2), GW * (g % 2) + GW)
                act.activation(rowsum[rows, t % 2, g // 2], banks[GW:2 * GW, n % 2, 0:P], ACT.Copy)
                act.activation(y[rows, t % 2, g // 2], banks[0:GW, n % 2, 0:P], ACT.Copy).then_inc(y_ok, 1)

            act.wait_ge(ones_ok, REP + 1)
            for f in range(2):
                place_v(f, f)
            high_heads(0, 0)
            for k in range(3):
                even_heads(0, 0, k)
            high_heads(1, 1)
            with act.Fori(0, B) as b:
                exp_unit(b * UNITS, 0)
                for n in range(UNITS):
                    t, g = n // NKV, n % NKV
                    if n + 1 < UNITS:
                        exp_unit(b * UNITS + n + 1, n + 1)
                    if g < 3:
                        even_heads(b * TILES + t + 1, t + 1, g)
                    if g == 1:
                        place_v(ahead(b, t), t + 2)
                    if g == 1 and t >= 1:
                        copy_yh(b, t - 1)
                    if g == 3:
                        high_heads(b * TILES + t + 2, t + 2)
                    copy_out(b * UNITS + n, n)
                copy_yh(b, TILES - 1)

            def turn_out(i, ps, ok):
                for j in range(4):
                    act.wait_ge(ps, i * 4 + j + 1)
                    act.activation(nT_h[:, :, bass.ds((i * 4 + j) * P, P)],
                                   banks[:, j, 0:C].rearrange("p (k n) -> p k n", k=KC), ACT.Copy).then_inc(ok, 1)

            def high_q(unit, b):
                act.wait_ge(misc_ps, place(unit, "q") + 1)
                for h in range(2):
                    for rows in (slice(64 * h, 64 * h + 64), slice(64 - 64 * h, P - 64 * h)):
                        act.activation(q_hh[rows, b, h], banks[64 * h:64 * h + 64, MISC], ACT.Copy, scale=SCALE_X)\
                            .then_inc(mh_ok, 1)

            def high_k(unit, b, c):
                act.wait_ge(misc_ps, place(unit, f"k{c}") + 1)
                for h in range(2):
                    rows = slice(64 * h, 64 * h + 64)
                    act.activation(k_st[rows, b, h, c * 512:c * 512 + 512], banks[rows, MISC], ACT.Copy)\
                        .then_inc(mh_ok, 1)

            def copy_v(unit, a):
                act.wait_ge(misc_ps, place(unit, f"v{a}") + 1)
                if not (isinstance(unit, int) and unit == 0):
                    act.wait_ge(v_ok, unit * 2 - 1 + a)
                act.activation(v_raw[:, a], banks[:, MISC], ACT.Copy).then_inc(misc_out, 1)

            def exp_x(head, h, q):
                act.wait_ge(max_ok, head * QB + q + 1)
                act.activation(probs[:, h, q], banks[:, S_BANK + 2 * (q % 2):S_BANK + 2 * (q % 2) + 2]
                               .rearrange("p a n -> p (a n)"), ACT.Exp, bias=nmax[:, h * QB + q:h * QB + q + 1],
                               accum_out=sums[:, bass.ds(head * QB + q, 1)]).then_inc(ex_ok, 1)

            def high_p(head, kb):
                act.wait_ge(pT_ps, head * KB + kb + 1)
                act.activation(pT_h[:, kb % 4], banks[:, PT_BANK + kb % 2], ACT.Copy).then_inc(pTh_ok, 1)

            def copy_o(head, h, unit):
                act.wait_ge(o_ps, head + 1)
                rows = slice(64 * h, 64 * h + 64)
                act.activation(o_all[rows, bass.ds(unit, 1), :].rearrange("p o n -> p (o n)"), banks[0:64, O_BANK], ACT.Copy)
                act.wait_ge(o_sum, head + 1)
                act.activation(o_low[rows], banks[64:P, O_BANK], ACT.Copy).then_inc(o_free, 1)

            def half(unit, b, h, jobs, scored):
                head = unit * 2 + h
                for kb in range(KB):
                    high_p(head, kb)
                    if jobs and h == 0 and kb in (1, 3, 5):
                        if kb == 1:
                            high_q(unit + 1, 1 - b)
                        else:
                            high_k(unit + 1, 1 - b, kb // 2 - 1)
                    if jobs and h == 1 and kb in (1, 3):
                        copy_v(unit + 1, kb // 2)
                    if kb % 2 == 1 and scored:
                        exp_x(head + 1, 1 - h, kb // 2)
                copy_o(head, h, unit)

            act.wait_ge(var2_ok, 1)
            act.activation(sd[:], ve[:], ACT.Sqrt).then_inc(sqrt2_ok, 1)
            high_k(0, 0, 0)
            with act.Fori(0, NT // 4) as i:
                turn_out(i, nT2_ps, nTh2_ok)

            high_k(0, 0, 1)
            high_q(0, 0)
            for q in range(QB):
                exp_x(0, 0, q)
                if q % 2 == 1:
                    copy_v(0, q // 2)
            with act.Fori(0, PAIRS - 1) as p:
                for b in range(B):
                    for h in range(2):
                        half(p * 2 + b, b, h, True, True)
            for b in range(B):
                for h in range(2):
                    half(UNITS_X - 2 + b, b, h, b == 0, b + h < 2)
            act.wait_ge(rs_ok, 1)

            def spread_sums(unit, j):
                act.activation(rexp[:, j].rearrange("p q (h d) -> p q h d", h=2),
                               rsum[:, bass.ds(unit, 1)].rearrange("p o h q -> p q (o h)").unsqueeze(3)
                               .broadcast_to([P, QB, 2, XD]), ACT.Copy).then_inc(rexp_ok, 1)

            def high_on(unit, j):
                act.wait_ge(on_ok, unit + 1)
                act.activation(on_h[:, j], on[:, j], ACT.Copy).then_inc(onh_ok, 1)

            for j in range(4):
                spread_sums(2 * j, j)
            with act.Fori(0, PAIRS // 4) as i:
                for j in range(4):
                    high_on(i * 4 + j, j)
                    spread_sums((i + 1) % 2 * 8 + i + 2 * j, j)

            def root3(b):
                act.wait_ge(var3_ok, b + 1)
                act.activation(sd[:, b * TILES:(b + 1) * TILES], ve[:, b * TILES:(b + 1) * TILES], ACT.Sqrt)\
                    .then_inc(sqrt3_ok, 1)

            def high_n(b, k):
                act.wait_ge(nT3_ps, b * 2 + k + 1)
                act.activation(nT_h[:, :, b * T + k * 2 * P:b * T + (k + 1) * 2 * P].rearrange("p k (t n) -> p t k n", n=P),
                               banks[:, 2 * b + k].rearrange("p (t k n) -> p t k n", t=2, k=KC), ACT.Copy)\
                    .then_inc(nTh3_ok, 1)

            for v in range(PAIRS):
                high_on(PAIRS + v, v % 4)
                if v < 4:
                    spread_sums(9 + 2 * v, v)
                if v == 3:
                    root3(0)
                if v == 6:
                    for k in range(2):
                        high_n(0, k)

            root3(1)
            act.wait_ge(lg_ps, 1)
            act.activation(lgT[:, 0:512], banks[0:NE, L_BANKS[0]], ACT.Copy).then_inc(lgT_ok, 1)
            for k in range(2):
                high_n(1, k)
            act.wait_ge(lg_ps, 2)
            act.activation(lgT[:, 512:], banks[0:NE, L_BANKS[1]], ACT.Copy).then_inc(lgT_ok, 1)

            def silu(n, c):
                act.wait_ge(g_ps, n + 1)
                act.activation(sg[:, c], banks[:, G_BANK + c], ACT.Silu).then_inc(sg_ok, 1)

            def high_h(n, c):
                act.wait_ge(hid_ok, n + 1)
                act.activation(hid_h[:, c], hid[:, c], ACT.Copy).then_inc(hh_ok, 1)

            act.wait_ge(lgN_ps, 1)
            act.activation(sc[:], banks[:, C_BANK, 0:NT * NE].rearrange("p (t e) -> p t e", e=NE), ACT.Sigmoid)\
                .then_inc(sc_ok, 1)
            silu(0, 0)
            for m in range(4):
                high_h(m, m % 2)
                if m < 3:
                    silu(m + 1, (m + 1) % 2)
                if m == 3:
                    act.wait_ge(combT_ps, 1)
                    act.activation(combT[:], banks[0:PARTS * NE, C_BANK].bitcast(BF16), ACT.Copy).then_inc(combT_ok, 1)
                    silu(4, 0)
            with act.Fori(1, EXPERTS // 2 - 1) as i:
                for m in range(4):
                    high_h(i * 4 + m, m % 2)
                    silu(i * 4 + m + 1, (m + 1) % 2)
            last_n = 2 * EXPERTS - 4
            for m in range(4):
                high_h(last_n + m, m % 2)
                if m < 3:
                    silu(last_n + m + 1, (m + 1) % 2)
            act.wait_ge(d_ps, 2 * EXPERTS)
            for r in range(2):
                act.activation(yT[:, r], banks[:, YF_BANK + r], ACT.Copy).then_inc(yT_a, 1)

        @block.vector
        def _(dve):
            def add_x1(dve, b, t):
                dve.wait_ge(proj_ps, b * TILES + t + 1)
                xt = x_sb[:, bass.ds(b * TILES + t, 1), :].rearrange("p o c -> p (o c)")
                dve.tensor_tensor(xt, banks[:, 3, 0:C], xt, ALU.add).then_inc(x1_ok, 1)

            steps = [0]

            def step(ins_, base=0):
                steps[0] += 1
                ins_.then_inc(dve_step, 1)
                dve.wait_ge(dve_step, base + steps[0])

            dve.wait_ge(x_in, 16)
            for t in range(NT):
                last = dve.bn_stats(stats[:, t, :], x_sb[:, t, :])
            step(last)
            for t in range(NT):
                last = dve.bn_aggr(mv[:, t, :], stats[:, t, :])
            step(last)
            dve.tensor_scalar(ve[:], mv[:, :, 1], EPS_LN, None, ALU.add).then_inc(var_ok, 1)
            dve.wait_ge(sqrt_ok, 1)
            step(dve.reciprocal(sr[:], sd[:]))
            step(dve.tensor_tensor(sr[:], sr[:], ve[:], ALU.mult))
            step(dve.tensor_tensor(sd[:], sd[:], sr[:], ALU.add))
            step(dve.tensor_scalar(sd[:], sd[:], 0.5, None, ALU.mult))
            step(dve.reciprocal(rstd[:], sd[:]))
            first = steps[0]
            with dve.Fori(0, B) as b:
                def norm_x(t):
                    dve.tensor_scalar(xn[:, t % 2], x_sb[:, bass.ds(b * TILES + t, 1), :].rearrange("p o c -> p (o c)"),
                                      mv[:, bass.ds(b * TILES + t, 1), 0], rstd[:, bass.ds(b * TILES + t, 1)],
                                      ALU.subtract, ALU.mult).then_inc(xn_ok, 1)

                def low_x(t):
                    dve.wait_ge(xh_ok, b * TILES + t + 1)
                    dve.tensor_tensor(xl[:, :, t * P:(t + 1) * P],
                                      banks[:, t % 2, 0:C].rearrange("p (k n) -> p k n", k=KC),
                                      xh[:, :, t * P:(t + 1) * P].bitcast(F32), ALU.subtract).then_inc(xl_ok, 1)

                def sum_squares(t):
                    dve.wait_ge(qkv_ok, b * TILES + t + 1)
                    dve.tensor_reduce(ss[:, bass.ds((b * TILES + t) * QKH, QKH)],
                                      sq[:, t].rearrange("p (h d) -> p h d", d=HD), AX.X, ALU.add).then_inc(ss_ok, 1)

                norm_x(0)
                norm_x(1)
                low_x(0)
                norm_x(2)
                low_x(1)
                norm_x(3)
                low_x(2)
                sum_squares(0)
                low_x(3)
                for t in range(1, TILES):
                    sum_squares(t)
            dve.wait_ge(ss_ok, NT + TILES)
            dve.wait_ge(s0_ok, 1)
            step(dve.tensor_scalar(s1[:], s0[:], 1e-30, None, ALU.max))
            step(dve.reciprocal(s1[:], s1[:]))
            step(dve.tensor_tensor(s1[:], s1[:], ss[:], ALU.mult))
            step(dve.tensor_tensor(s1[:], s1[:], s0[:], ALU.add))
            step(dve.tensor_scalar(s1[:], s1[:], 0.5, EPS_NORM, ALU.mult, ALU.add))
            step(dve.reciprocal(s0[:], s1[:]))
            dve.wait_ge(const_in, 64)

            def norm_heads(f, tile):
                if not isinstance(f, int) or f:
                    dve.wait_ge(r_ok, f)
                one = slice(tile, tile + 1) if isinstance(tile, int) else bass.ds(tile, 1)
                dve.tensor_tensor(qn[:], qkv[:, one, 0:QKC].rearrange("p o (h d) -> p (o h) d", d=HD),
                                  s0[:, bass.ds(tile * QKH, QKH)].unsqueeze(2).broadcast_to([P, QKH, HD]),
                                  ALU.mult).then_inc(qn_ok, 1)

            def cosine(f, t):
                dve.wait_ge(qn_ok, f + 1)
                dve.tensor_tensor(ra[:], qn[:], cosv[:, t % TILES].unsqueeze(1).broadcast_to([P, QKH, HD]),
                                  ALU.mult).then_inc(ra_ok, 1)

            def odd_heads(f, t, k):
                dve.wait_ge(qkT_ps, f * 3 + k + 1)
                src = banks[64:P, 2, :].rearrange("p (h n) -> p h n", n=P)
                if k < 2:
                    dve.tensor_copy(qT[:, t % 2, 8 * k + 1:8 * k + 8:2], src).then_inc(odd_ok, 1)
                else:
                    dve.tensor_copy(kT[:, t % TILES, 1:NKV:2], src[:, 0:NKV // 2]).then_inc(odd_ok, 1)

            for f in range(2):
                norm_heads(f, f)
                cosine(f, f)
            for k in range(3):
                odd_heads(0, 0, k)
            with dve.Fori(0, B) as b:
                def mask_unit(n):
                    if n >= NKV:
                        dve.wait_ge(exp_ok, b * UNITS + n + 1)
                        dve.tensor_tensor(E[:, n % 2, 0], E[:, n % 2, 0], window[:].unsqueeze(1).broadcast_to([P, REP, P]),
                                          ALU.mult).then_inc(mask_ok, 1)

                def divide(t, k):
                    count = (b * TILES + t) * KC + k + 1
                    dve.wait_ge(y_ok, b * UNITS + t * NKV + 2 * k + 4)
                    dve.reciprocal(rowsum[:, t % 2, k], rowsum[:, t % 2, k]).then_inc(rec_ok, 1)
                    dve.wait_ge(rec_ok, count)
                    dve.tensor_tensor(y[:, t % 2, k], y[:, t % 2, k], rowsum[:, t % 2, k], ALU.mult).then_inc(yn_ok, 1)

                def low_y(t):
                    dve.wait_ge(yh_ok, b * TILES + t + 1)
                    dve.wait_ge(yn_ok, (b * TILES + t + 1) * KC)
                    dve.tensor_tensor(yl[:], y[:, t % 2], yh[:].bitcast(F32), ALU.subtract).then_inc(yl_ok, 1)

                def measure(t):
                    dve.wait_ge(x1_ok, b * TILES + t + 1)
                    tt = b * TILES + t
                    dve.bn_stats(stats[:, bass.ds(tt, 1), :].rearrange("p o s -> p (o s)"),
                                 x_sb[:, bass.ds(tt, 1), :].rearrange("p o c -> p (o c)")).then_inc(stats_ok, 1)

                for n in range(UNITS):
                    t, g = n // NKV, n % NKV
                    if n + 1 < UNITS:
                        mask_unit(n + 1)
                    if g < 3:
                        odd_heads(b * TILES + t + 1, t + 1, g)
                    if g == 0 and t >= 1:
                        divide(t - 1, 1)
                    if g == 2:
                        divide(t, 0)
                    if g == 0:
                        norm_heads(b * TILES + t + 2, ahead(b, t))
                    if g == 1:
                        cosine(b * TILES + t + 2, t + 2)
                    if n >= NKV and n % NKV == 1:
                        low_y(n // NKV - 1)
                        if n >= 2 * NKV:
                            measure(n // NKV - 2)
                    if n >= NKV and n % NKV == 3:
                        add_x1(dve, b, n // NKV - 1)
                divide(TILES - 1, 1)
                low_y(TILES - 1)
                add_x1(dve, b, TILES - 1)
                measure(TILES - 2)
                measure(TILES - 1)

            def invert(part, base):
                s_, r_, v_ = sd[:, part], sr[:, part], ve[:, part]
                step(dve.reciprocal(r_, s_), base)
                step(dve.tensor_tensor(r_, r_, v_, ALU.mult), base)
                step(dve.tensor_tensor(s_, s_, r_, ALU.add), base)
                step(dve.tensor_scalar(s_, s_, 0.5, None, ALU.mult), base)
                step(dve.reciprocal(rstd[:, part], s_), base)

            def spread(done, var_sem, sqrt_sem, base, measured=False):
                for s_, v_ in done:
                    dve.wait_ge(s_, v_)
                if not measured:
                    for t in range(NT):
                        last = dve.bn_stats(stats[:, t, :], x_sb[:, t, :])
                    step(last, base)
                for t in range(NT):
                    last = dve.bn_aggr(mv[:, t, :], stats[:, t, :])
                step(last, base)
                dve.tensor_scalar(ve[:], mv[:, :, 1], EPS_LN, None, ALU.add).then_inc(var_sem, 1)
                dve.wait_ge(sqrt_sem, 1)
                invert(slice(0, NT), base)

            def norm_turn(i, xn_, ok, hi, lo):
                for j in range(4):
                    tt = i * 4 + j
                    dve.tensor_scalar(xn_[:, j], x_sb[:, bass.ds(tt, 1), :].rearrange("p o c -> p (o c)"),
                                      mv[:, bass.ds(tt, 1), 0], rstd[:, bass.ds(tt, 1)],
                                      ALU.subtract, ALU.mult).then_inc(ok, 1)
                for j in range(4):
                    tt = i * 4 + j
                    dve.wait_ge(hi, tt + 1)
                    dve.tensor_tensor(nT_l[:, :, bass.ds(tt * P, P)],
                                      banks[:, j, 0:C].rearrange("p (k n) -> p k n", k=KC),
                                      nT_h[:, :, bass.ds(tt * P, P)].bitcast(F32), ALU.subtract).then_inc(lo, 1)

            def low_q(unit, b, doubled=False):
                for h in range(2):
                    rows, other = slice(64 * h, 64 * h + 64), slice(64 - 64 * h, P - 64 * h)
                    dve.wait_ge(mh_ok, halves(unit, "q") + 2 * h + 2)
                    if doubled:
                        dve.scalar_tensor_tensor(q_ll[other, b, h], banks[rows, MISC], SCALE_X,
                                                 q_hh[rows, b, h].bitcast(F32), ALU.mult, ALU.subtract)
                    dve.scalar_tensor_tensor(q_ll[rows, b, h], banks[rows, MISC], SCALE_X, q_hh[rows, b, h].bitcast(F32),
                                             ALU.mult, ALU.subtract).then_inc(misc_out if h else half_out, 1)
                dve.wait_ge(misc_out, place(unit, "q") + 1)
                dve.sem_inc(q_ok if doubled else qlo_ok, 1)

            def low_k(unit, b, c):
                cols = slice(c * 512, c * 512 + 512)
                for h in range(2):
                    rows, other = slice(64 * h, 64 * h + 64), slice(64 - 64 * h, P - 64 * h)
                    dve.wait_ge(mh_ok, halves(unit, f"k{c}") + h + 1)
                    last = dve.tensor_tensor(k_st[other, b, h, cols], banks[rows, MISC], k_st[rows, b, h, cols].bitcast(F32),
                                             ALU.subtract)
                last.then_inc(misc_out, 1)

            def max_x(head, h, q):
                dve.wait_ge(sx_ps, head * QB + q + 1)
                dve.tensor_reduce(nmax[:, h * QB + q:h * QB + q + 1],
                                  banks[:, S_BANK + 2 * (q % 2):S_BANK + 2 * (q % 2) + 2]
                                  .rearrange("p a n -> p (a n)"), AX.X, ALU.max, negate=True).then_inc(max_ok, 1)

            def low_p(head, kb):
                dve.wait_ge(pTh_ok, head * KB + kb + 1)
                dve.tensor_tensor(pT_l[:, kb % 4], banks[:, PT_BANK + kb % 2], pT_h[:, kb % 4].bitcast(F32),
                                  ALU.subtract).then_inc(pTl_ok, 1)

            def half(unit, b, h, jobs, scored, begun):
                head = unit * 2 + h
                for kb in range(KB):
                    if kb in (2, 4, 6) and scored:
                        max_x(head + 1, 1 - h, kb // 2)
                    low_p(head, kb)
                    if jobs and h == 0 and kb in (1, 3, 5):
                        if kb == 1:
                            low_q(unit + 1, 1 - b)
                        else:
                            low_k(unit + 1, 1 - b, kb // 2 - 1)
                if begun:
                    max_x(head + 2, h, 0)

            spread([(stats_ok, NT)], var2_ok, sqrt2_ok, 0, measured=True)
            low_k(0, 0, 0)
            with dve.Fori(0, NT // 4) as i:
                norm_turn(i, xn2, xn2_ok, nTh2_ok, nTl2_ok)

            low_k(0, 0, 1)
            low_q(0, 0, doubled=True)
            for q in range(QB):
                max_x(0, 0, q)
            max_x(1, 1, 0)
            with dve.Fori(0, PAIRS - 1) as p:
                for b in range(B):
                    for h in range(2):
                        half(p * 2 + b, b, h, True, True, True)
            for b in range(B):
                for h in range(2):
                    half(UNITS_X - 2 + b, b, h, b == 0, b + h < 2, b == 0)
            dve.wait_ge(ex_ok, 2 * UNITS_X * QB)
            dve.reciprocal(rsum[:].rearrange("p u h q -> p (u h q)"), sums[:]).then_inc(rs_ok, 1)
            dve.wait_ge(o_sum, 2 * UNITS_X + 2)
            def scale_o(v, unit, j):
                dve.wait_ge(rT_ps, v + 1)
                dve.tensor_tensor(on[:, j], banks[:, R_BANK + j], o_all[:, bass.ds(unit, 1), :].rearrange("p o n -> p (o n)"),
                                  ALU.mult).then_inc(on_ok, 1)

            def add_x2(b):
                dve.wait_ge(y_used, PAIRS * (b + 1))
                xt = x_sb[:, b * TILES:(b + 1) * TILES, :].rearrange("p t c -> p (t c)")
                dve.tensor_tensor(xt, banks[:, Y_BANK + 2 * b:Y_BANK + 2 * b + 2].rearrange("p a n -> p (a n)"), xt, ALU.add)\
                    .then_inc(x2_ok, 1)

            def measure3(b):
                dve.wait_ge(x2_ok, b + 1)
                tiles = range(b * TILES, (b + 1) * TILES)
                for t in tiles:
                    last = dve.bn_stats(stats[:, t, :], x_sb[:, t, :])
                step(last)
                for t in tiles:
                    last = dve.bn_aggr(mv[:, t, :], stats[:, t, :])
                step(last)
                part = slice(b * TILES, (b + 1) * TILES)
                dve.tensor_scalar(ve[:, part], mv[:, part, 1], EPS_LN, None, ALU.add).then_inc(var3_ok, 1)

            def norm3(b):
                part = slice(b * TILES, (b + 1) * TILES)
                dve.wait_ge(sqrt3_ok, b + 1)
                invert(part, 0)
                if b:
                    dve.wait_ge(nT3_ps, 2)
                for t in range(TILES):
                    tt = b * TILES + t
                    dve.tensor_scalar(xn3[:, t], x_sb[:, tt, :], mv[:, tt:tt + 1, 0], rstd[:, tt:tt + 1],
                                      ALU.subtract, ALU.mult).then_inc(xn3_ok, 1)

            def low_n(b, k):
                dve.wait_ge(nTh3_ok, b * 2 + k + 1)
                cols = slice(b * T + k * 2 * P, b * T + (k + 1) * 2 * P)
                dve.tensor_tensor(nT_l[:, :, cols].rearrange("p k (t n) -> p t k n", n=P),
                                  banks[:, 2 * b + k].rearrange("p (t k n) -> p t k n", t=2, k=KC),
                                  nT_h[:, :, cols].rearrange("p k (t n) -> p t k n", n=P).bitcast(F32),
                                  ALU.subtract).then_inc(nTl3_ok, 1)

            with dve.Fori(0, PAIRS // 4) as i:
                for j in range(4):
                    scale_o(i * 4 + j, i * 8 + 2 * j, j)
            for v in range(PAIRS):
                scale_o(PAIRS + v, 2 * v + 1, v % 4)
                if v == 1:
                    add_x2(0)
                if v == 2:
                    measure3(0)
                if v == 4:
                    norm3(0)
                if v == 6:
                    for k in range(2):
                        low_n(0, k)
            add_x2(1)
            measure3(1)
            norm3(1)
            for k in range(2):
                low_n(1, k)
            base_f = 0
            def weigh_gate(n, c):
                dve.wait_ge(sg_ok, n + 1)
                dve.wait_ge(c_ps, n + 1 - 2 * SHARED)
                dve.tensor_tensor(gc[:, c], banks[:, C_BANK], sg[:, c], ALU.mult).then_inc(gc_ok, 1)

            def hidden(n, c):
                dve.wait_ge(u_ps, n + 1)
                if isinstance(n, int) and n < 2 * SHARED:
                    dve.wait_ge(sg_ok, n + 1)
                    dve.tensor_tensor(hid[:, c], banks[:, U_BANK], sg[:, c], ALU.mult).then_inc(hid_ok, 1)
                else:
                    dve.wait_ge(gc_ok, n + 1 - 2 * SHARED)
                    dve.tensor_tensor(hid[:, c], banks[:, U_BANK], gc[:, c], ALU.mult).then_inc(hid_ok, 1)
                dve.wait_ge(hh_ok, n + 1)
                dve.tensor_tensor(hid_l[:, c], hid[:, c], hid_h[:, c].bitcast(F32), ALU.subtract).then_inc(hlo_ok, 1)

            dve.memset(gval[:], NONE)
            step(dve.memset(evalue[:], NONE), base_f)
            dve.wait_ge(sc_ok, 1)
            dve.wait_ge(gate_in, 48)
            step(dve.tensor_tensor(sfc[:], sc[:], ebias[:].unsqueeze(1).broadcast_to([P, NT, NE]), ALU.add), base_f)
            step(dve.tensor_reduce(gval[:, :, 0:GROUPS], sfc[:].rearrange("p t (g s) -> p t g s", s=GS),
                                   AX.X, ALU.max), base_f)
            for t in range(NT):
                last = dve.max(gtop[:, t], gval[:, t, 0:GROUPS])
            step(last, base_f)
            step(dve.memset(gtop[:, :, TOP_GROUPS:8], NONE), base_f)
            for t in range(NT):
                last = dve.match_replace(gout[:, t], gtop[:, t], gval[:, t], TAKEN)
            step(last, base_f)
            hidden(0, 0)
            step(dve.tensor_scalar(gmask[:], gout[:, :, 0:GROUPS], TAKEN, None, ALU.is_ge), base_f)
            step(dve.tensor_tensor(evalue[:, :, 0:NE].rearrange("p t (g s) -> p t g s", s=GS),
                                   sfc[:].rearrange("p t (g s) -> p t g s", s=GS),
                                   gmask[:].unsqueeze(3).broadcast_to([P, NT, GROUPS, GS]), ALU.mult), base_f)
            for t in range(NT):
                last = dve.max(etop[:, t], evalue[:, t, 0:NE])
            step(last, base_f)
            step(dve.memset(etop[:, :, TOP_K:8], NONE), base_f)
            for t in range(NT):
                last = dve.match_replace(eout[:, t], etop[:, t], evalue[:, t], TAKEN)
            step(last, base_f)
            hidden(1, 1)
            step(dve.tensor_scalar(tw[:], eout[:, :, 0:NE], TAKEN, None, ALU.is_ge), base_f)
            step(dve.tensor_tensor(tw[:], tw[:], sc[:], ALU.mult), base_f)
            step(dve.tensor_reduce(tsum[:], tw[:], AX.X, ALU.add), base_f)
            step(dve.tensor_scalar(tsum[:], tsum[:], 1e-20, None, ALU.add), base_f)
            step(dve.reciprocal(tsum[:], tsum[:]), base_f)
            step(dve.tensor_tensor(comb[:], tw[:], tsum[:].unsqueeze(2).broadcast_to([P, NT, NE]),
                                   ALU.mult), base_f)
            step(dve.tensor_scalar(comb[:], comb[:], ROUTE_SCALE, None, ALU.mult), base_f)
            step(dve.tensor_copy(parts[:, :, 0], comb[:]), base_f)
            step(dve.tensor_tensor(cres[:], comb[:], parts[:, :, 0], ALU.subtract), base_f)
            step(dve.tensor_copy(parts[:, :, 1], cres[:]), base_f)
            step(dve.tensor_tensor(comb[:], cres[:], parts[:, :, 1], ALU.subtract), base_f)
            dve.tensor_copy(parts[:, :, 2], comb[:]).then_inc(parts_ok, 1)

            hidden(2, 0)
            hidden(3, 1)
            with dve.Fori(1, EXPERTS // 2) as i:
                for m in range(4):
                    weigh_gate(i * 4 + m, m % 2)
                    hidden(i * 4 + m, m % 2)
            dve.wait_ge(d_ps, 2 * EXPERTS)
            for r in range(2, 4):
                dve.tensor_copy(yT[:, r], banks[:, YF_BANK + r]).then_inc(yT_d, 1)
            for r in range(NT // 2):
                dve.wait_ge(yN_ps, r + 1)
                dve.tensor_tensor(y_out[:, 2 * r:2 * r + 2].rearrange("p t c -> p (t c)"), banks[:, 4 + r],
                                  x_sb[:, 2 * r:2 * r + 2].rearrange("p t c -> p (t c)"), ALU.add).then_inc(y_fin, 1)

        @block.tensor
        def _(pe):
            pe.wait_ge(ident_ok, 2)
            with pe.Fori(0, B) as b:
                def turn_x(t):
                    pe.wait_ge(xn_ok, b * TILES + t + 1)
                    for k in range(KC):
                        mm = pe.transpose(banks[:, t % 2, k * P:(k + 1) * P], xn[:, t % 2, k * P:(k + 1) * P], ident[:])
                    mm.then_inc(xT_ps, 1)

                def project_qkv(t):
                    pe.wait_ge(xl_ok, b * TILES + t + 1)
                    if t >= 2:
                        pe.wait_ge(qkv_ok, b * TILES + t - 1)
                    three_products(pe, banks[:, 2 + t % 2, 0:QKV],
                                   [(xh[:, k, t * P:(t + 1) * P], xl[:, k, t * P:(t + 1) * P],
                                     wqkv_h[:, k, :], wqkv_l[:, k, :]) for k in range(KC)]).then_inc(qkv_ps, 1)

                turn_x(0)
                turn_x(1)
                pe.wait_ge(wa_ok, 1)
                project_qkv(0)
                turn_x(2)
                project_qkv(1)
                turn_x(3)
                project_qkv(2)
                project_qkv(3)

            def turn_heads(f, t, k):
                if k == 0:
                    pe.wait_ge(hl_ok, f * 2 + 2)
                if not (isinstance(f, int) and f * 3 + k == 0):
                    pe.wait_ge(even_ok, f * 3 + k)
                    pe.wait_ge(odd_ok, f * 3 + k)
                for i in range(4 if k < 2 else NKV // 2):
                    h0 = 8 * k + 2 * i
                    mm = pe.transpose(banks[:, 2, i * P:(i + 1) * P],
                                      hl[:, t % 2, h0:h0 + 2].rearrange("p h c d -> p (h c d)").bitcast(F32), ident[:])
                mm.then_inc(qkT_ps, 1)

            def scores(f, t, g):
                if g == 0:
                    pe.wait_ge(even_ok, f * 3 + 3)
                    pe.wait_ge(odd_ok, f * 3 + 3)
                if t:
                    pe.matmul(banks[:, 4 + 2 * (g % 2), :], kT[:, t - 1, g], qT[:, t % 2, REP * g:REP * (g + 1)],
                              start=True, stop=True)
                own = banks[:, 5 + 2 * (g % 2), :]
                pe.matmul(own, kT[:, t, g], qT[:, t % 2, REP * g:REP * (g + 1)], start=True, stop=False)
                pe.matmul(own, identb[:], causal[:].unsqueeze(1).broadcast_to([P, REP, P]), start=False, stop=True)\
                    .then_inc(s_ps, 1)

            def weigh(b, n):
                t, g = n // NKV, n % NKV
                pe.wait_ge(exp_ok, b * UNITS + n + 1)
                pe.wait_ge(y_ok, b * UNITS + n + 1)
                for r in range(REP):
                    mm = pe.matmul(banks[:, n % 2, 0:P], va[:, t, g, r], E[:, n % 2, 1, r, :], start=(r == 0),
                                   stop=(t == 0 and r == REP - 1))
                if t:
                    pe.wait_ge(mask_ok, b * (UNITS - NKV) + n - NKV + 1)
                    for r in range(REP):
                        mm = pe.matmul(banks[:, n % 2, 0:P], va[:, t - 1, g, r], E[:, n % 2, 0, r, :], start=False,
                                       stop=(r == REP - 1))
                mm.then_inc(pv_done, 1)

            def project_y(b, t):
                pe.wait_ge(yl_ok, b * TILES + t + 1)
                if t:
                    pe.wait_ge(x1_ok, b * TILES + t)
                three_products(pe, banks[:, 3, 0:C],
                               [(yh[:, k, :], yl[:, k, :], wp_h[:, k, :], wp_l[:, k, :]) for k in range(KC)])\
                    .then_inc(proj_ps, 1)

            for k in range(3):
                turn_heads(0, 0, k)
            pe.wait_ge(v_placed, 2)
            pe.wait_ge(ident_ok, 4)
            pe.wait_ge(const_in, 64)
            pe.wait_ge(wp_ok, 1)
            scores(0, 0, 0)
            with pe.Fori(0, B) as b:
                for n in range(UNITS):
                    t, g = n // NKV, n % NKV
                    f = b * TILES + t
                    if g < 3:
                        scores(f, t, g + 1)
                        turn_heads(f + 1, t + 1, g)
                    else:
                        scores(f + 1, (t + 1) % TILES, 0)
                    if g == 0:
                        pe.wait_ge(v_placed, f + 1)
                    weigh(b, n)
                    if n >= NKV and g == 2:
                        project_y(b, t - 1)
                project_y(b, TILES - 1)

            pe.wait_ge(x1_ok, NT)

            def turn(i, xn_, xn_sem, ps, lo):
                for j in range(4):
                    pe.wait_ge(xn_sem, i * 4 + j + 1)
                    pe.wait_ge(lo, i * 4 + j + 1)
                    for k in range(KC):
                        mm = pe.transpose(banks[:, j, k * P:(k + 1) * P], xn_[:, j, k * P:(k + 1) * P], ident[:])
                    mm.then_inc(ps, 1)

            def begin(job):
                if not (isinstance(job, int) and job == 0):
                    pe.wait_ge(misc_out, job)

            def pair_cols(block):
                return slice(block * P, (block + 1) * P)

            def q_job(unit, pair, b):
                begin(place(unit, "q"))
                pe.wait_ge(wqk_ok, pair + 1)
                src = slice(b * T, (b + 1) * T)
                three_products(pe, banks[:, MISC], [(wx_h[:, pair_cols(k)], wx_l[:, pair_cols(k)], nT_h[:, k, src],
                                                     nT_l[:, k, src]) for k in range(KC)]).then_inc(misc_ps, 1)

            def k_job(unit, b, c):
                begin(place(unit, f"k{c}"))
                pe.wait_ge(wqk_ok, 1)
                src = slice(b * M + c * 512, b * M + c * 512 + 512)
                wk = pair_cols(KC)
                three_products(pe, banks[:, MISC], [(wx_h[:, wk], wx_l[:, wk], ctx_h[:, src], ctx_l[:, src])])\
                    .then_inc(misc_ps, 1)

            def v_job(unit, pair, b, a):
                begin(place(unit, f"v{a}"))
                pe.wait_ge(wv_ok, pair + 1)
                wv = pair_cols(KC + 1)
                for t in range(4):
                    src = slice(b * M + (4 * a + t) * P, b * M + (4 * a + t + 1) * P)
                    mm = three_products(pe, banks[:, MISC, t * P:(t + 1) * P],
                                        [(ctx_h[:, src], ctx_l[:, src], wx_h[:, wv], wx_l[:, wv])])
                mm.then_inc(misc_ps, 1)

            def score(head, unit, b, h, q, prologue=False):
                if q == 0:
                    pe.wait_ge(misc_out, unit * JOBS + 3)
                    pe.wait_ge(q_ok, unit + 1)
                if not prologue or q >= 2:
                    pe.wait_ge(ex_ok, head * QB + q - 1)
                for c in range(2):
                    dst = banks[:, S_BANK + 2 * (q % 2) + c]
                    keys = k_st[:, b, h, c * 512:(c + 1) * 512]
                    pe.matmul(dst, q_hh[:, b, h, q * P:(q + 1) * P], keys, start=True, stop=False)
                    mm = pe.matmul(dst, q_ll[:, b, h, q * P:(q + 1) * P], keys, start=False, stop=True)
                mm.then_inc(sx_ps, 1)

            def turn_p(head, h, kb):
                if kb == 0:
                    pe.wait_ge(ex_ok, (head + 1) * QB)
                for q in range(QB):
                    mm = pe.transpose(banks[:, PT_BANK + kb % 2, q * P:(q + 1) * P],
                                      probs[:, h, q, kb * P:(kb + 1) * P], ident[:])
                mm.then_inc(pT_ps, 1)

            def weigh_x(head, unit, b, h, kb):
                pe.wait_ge(pTl_ok, head * KB + kb + 1)
                if kb == 0:
                    pe.wait_ge(o_free, head + 1)
                if kb % 4 == 0 and h == 0:
                    pe.wait_ge(v_ok, unit * 2 + 1 + kb // 4)
                v = v_hl[:, b, kb, h].rearrange("p r d -> p (r d)")
                pe.matmul(banks[:, O_BANK], v, pT_h[:, kb % 4], start=(kb == 0), stop=False)
                mm = pe.matmul(banks[:, O_BANK], v, pT_l[:, kb % 4], start=False, stop=(kb == KB - 1))
                if kb == KB - 1:
                    mm.then_inc(o_ps, 1)

            def half(unit, pair, b, h, jobs, scored, begun):
                head = unit * 2 + h
                nb = 1 - b

                def score_next(q):
                    if scored:
                        score(head + 1, unit + h, b if h == 0 else nb, 1 - h, q)

                def job(i):
                    if jobs and h == 0:
                        q_job(unit + 1, pair + b, nb) if i == 0 else k_job(unit + 1, nb, i - 1)
                    if jobs and h == 1 and i < 2:
                        v_job(unit + 1, pair + b, nb, i)

                turn_p(head, h, 0)
                turn_p(head, h, 1)
                for q in range(1, QB):
                    job(q - 1)
                    score_next(q)
                    weigh_x(head, unit, b, h, 2 * q - 2)
                    turn_p(head, h, 2 * q)
                    weigh_x(head, unit, b, h, 2 * q - 1)
                    turn_p(head, h, 2 * q + 1)
                if begun:
                    score(head + 2, unit + 1, nb, h, 0)
                weigh_x(head, unit, b, h, 6)
                weigh_x(head, unit, b, h, 7)

            pe.wait_ge(ctx_ok, NT)
            k_job(0, 0, 0)
            with pe.Fori(0, NT // 4) as i:
                turn(i, xn2, xn2_ok, nT2_ps, nTl2_ok)
            k_job(0, 0, 1)
            pe.wait_ge(nTl2_ok, NT + 4)
            q_job(0, 0, 0)
            for q in range(QB):
                score(0, 0, 0, 0, q, prologue=True)
                if q % 2 == 1:
                    v_job(0, 0, 0, q // 2)
            score(1, 0, 0, 1, 0)
            with pe.Fori(0, PAIRS - 1) as p:
                for b in range(B):
                    for h in range(2):
                        half(p * 2 + b, p, b, h, True, True, True)
            for b in range(B):
                for h in range(2):
                    half(UNITS_X - 2 + b, PAIRS - 1, b, h, b == 0, b + h < 2, b == 0)

            pe.wait_ge(wo_ok, PAIRS)
            pe.wait_ge(ones_ok, REP + 2)
            pe.wait_ge(bo_in, 16)
            for c in range(2 * B):
                pe.matmul(banks[:, Y_BANK + c], ones1[:], bo2[:], start=True, stop=False, skip_group_check=True)

            def turn_sums(unit, j):
                pe.wait_ge(rexp_ok, unit + 1)
                for q in range(QB):
                    mm = pe.transpose(banks[:, R_BANK + j, q * P:(q + 1) * P], rexp[:, j, q], ident[:])
                mm.then_inc(rT_ps, 1)

            def project_o(v, pair, b, j):
                pe.wait_ge(onl_ok, v + 1)
                wh, wl = (w[:, bass.ds(pair, 1), :].rearrange("p o n -> p (o n)") for w in (wo_h, wo_l))
                for q in range(QB):
                    dst = banks[:, Y_BANK + 2 * b + q // 2, (q % 2) * C:(q % 2 + 1) * C]
                    oh, ol = on_h[:, j, q * P:(q + 1) * P], on_l[:, j, q * P:(q + 1) * P]
                    pe.matmul(dst, oh, wh, start=False, stop=False, skip_group_check=True)
                    pe.matmul(dst, oh, wl, start=False, stop=False, skip_group_check=True)
                    mm = pe.matmul(dst, ol, wh, start=False, stop=False, skip_group_check=True)
                mm.then_inc(y_used, 1)

            def turn3(b):
                for k in range(2):
                    pe.wait_ge(xn3_ok, b * TILES + 2 * k + 2)
                    for t in range(2):
                        for f in range(KC):
                            mm = pe.transpose(banks[:, 2 * b + k, (t * KC + f) * P:(t * KC + f + 1) * P],
                                              xn3[:, 2 * k + t, f * P:(f + 1) * P], ident[:])
                    mm.then_inc(nT3_ps, 1)

            def logits(c):
                pe.wait_ge(nTl3_ok, 2 * c + 2)
                src = slice(c * 512, (c + 1) * 512)
                for k in range(KC):
                    for a in range(2):
                        for w in (wg_h, wg_l):
                            mm = pe.matmul(banks[0:NE, L_BANKS[c]], w[:, k], (nT_h if a == 0 else nT_l)[:, k, src],
                                           start=(k == 0 and a == 0 and w is wg_h),
                                           stop=(k == KC - 1 and a == 1 and w is wg_l))
                mm.then_inc(lg_ps, 1)

            for j in range(2):
                turn_sums(j, j)
            with pe.Fori(0, PAIRS // 4) as i:
                for j in range(4):
                    turn_sums(i * 4 + j + 2, (j + 2) % 4)
                    project_o(i * 4 + j, i * 4 + j, 0, j)
            for v in range(PAIRS):
                if v + 2 < PAIRS:
                    turn_sums(PAIRS + v + 2, (v + 2) % 4)
                project_o(PAIRS + v, v, 1, v % 4)
                if v == 5:
                    turn3(0)

            def gate_up(n, j, c, e, first_step=False):
                src = slice(c * 512, (c + 1) * 512)
                if c == 0:
                    pe.wait_ge(wgu_ok, e + 1)

                def product(bank, off):
                    return three_products(pe, banks[:, bank], [
                        (wf_h[:, j, k * 2 * NI + off:k * 2 * NI + off + NI],
                         wf_l[:, j, k * 2 * NI + off:k * 2 * NI + off + NI],
                         nT_h[:, k, src], nT_l[:, k, src]) for k in range(KC)])

                product(G_BANK + c, 0).then_inc(g_ps, 1)
                if not (isinstance(n, int) and n < 2 * SHARED):
                    if isinstance(n, int) and n == 2 * SHARED:
                        pe.wait_ge(combT_ok, 1)
                    else:
                        pe.wait_ge(gc_ok, n - 2 * SHARED)
                    pe.matmul(banks[:, C_BANK], sel[:, bass.ds((e - SHARED) * P, P)], combT[:, src],
                              start=True, stop=True).then_inc(c_ps, 1)
                if not first_step:
                    pe.wait_ge(hid_ok, n)
                product(U_BANK, NI).then_inc(u_ps, 1)

            pe.wait_ge(wg_ok, 1)
            logits(0)
            gate_up(0, 0, 0, 0, first_step=True)
            turn3(1)
            logits(1)
            pe.wait_ge(f_const, 1)
            pe.wait_ge(nTl3_ok, 4)
            for r in range(4):
                pe.matmul(banks[:, YF_BANK + r], zrow[:, 0:P], zrow[:], start=True, stop=False, skip_group_check=True)

            def turn_logits():
                for t in range(NT):
                    mm = pe.transpose(banks[:, C_BANK, t * NE:(t + 1) * NE], lgT[:, t * P:(t + 1) * P],
                                      ident[0:NE, 0:NE])
                mm.then_inc(lgN_ps, 1)

            def turn_weights():
                pe.wait_ge(parts_ok, 1)
                for t in range(NT):
                    mm = pe.transpose(banks[0:PARTS * NE, C_BANK, t * 64:(t + 1) * 64].bitcast(BF16),
                                      parts[:, t].rearrange("p r e -> p (r e)"), identb[:])
                mm.then_inc(combT_ps, 1)

            def down(n, j, c, e):
                pe.wait_ge(hlo_ok, n + 1)
                if c == 0:
                    pe.wait_ge(wdn_ok, e + 1)
                off = GU
                for f in range(KC):
                    dst = banks[:, YF_BANK + 2 * c + f]
                    wh = wf_h[:, j, off + f * P:off + (f + 1) * P]
                    wl = wf_l[:, j, off + f * P:off + (f + 1) * P]
                    pe.matmul(dst, wh, hid_h[:, c], start=False, stop=False, skip_group_check=True)
                    pe.matmul(dst, wh, hid_l[:, c], start=False, stop=False, skip_group_check=True)
                    mm = pe.matmul(dst, wl, hid_h[:, c], start=False, stop=False, skip_group_check=True)
                mm.then_inc(d_ps, 1)

            pe.wait_ge(lgT_ok, 2)
            turn_logits()
            for m in range(4):
                m1 = m + 1
                if m1 == 2 * SHARED:
                    turn_weights()
                gate_up(m1, (m1 // 2) % 2, m1 % 2, m1 // 2)
                down(m, m // 2, m % 2, m // 2)
            with pe.Fori(1, EXPERTS // 2 - 1) as i:
                for m in range(4):
                    m1 = m + 1
                    gate_up(i * 4 + m1, (m1 // 2) % 2, m1 % 2, i * 2 + m1 // 2)
                    down(i * 4 + m, m // 2, m % 2, i * 2 + m // 2)
            for m in range(4):
                n = 2 * EXPERTS - 4 + m
                if m < 3:
                    gate_up(n + 1, (m + 1) // 2, (m + 1) % 2, EXPERTS - 2 + (m + 1) // 2)
                down(n, m // 2, m % 2, EXPERTS - 2 + m // 2)
            for r in range(NT // 2):
                c = r // 2
                if r % 2 == 0:
                    pe.wait_ge(yT_a if c == 0 else yT_d, 2)
                for tt in range(2):
                    for f in range(KC):
                        tok = ((2 * r + tt) * P) % 512
                        mm = pe.transpose(banks[:, 4 + r, tt * C + f * P:tt * C + (f + 1) * P],
                                          yT[:, 2 * c + f, tok:tok + P], ident[:])
                mm.then_inc(yN_ps, 1)


def three_products(pe, dst, parts):
    n = len(parts)
    for k, (ah, al, bh, bl) in enumerate(parts):
        pe.matmul(dst, ah, bh, start=(k == 0), stop=False)
        pe.matmul(dst, ah, bl, start=False, stop=False)
        mm = pe.matmul(dst, al, bh, start=False, stop=(k == n - 1))
    return mm


def rope_table():
    theta = (1.0 / 10000.0 ** (np.arange(0, HD, 2, dtype=np.float32) / np.float32(HD))).astype(np.float32)
    freqs = np.outer(np.arange(T, dtype=np.float32), theta).astype(np.float32)
    cos, sin = np.cos(freqs), np.sin(freqs)
    return (np.concatenate([cos, cos], axis=1).astype(np.float32),
            np.concatenate([-sin, sin], axis=1).astype(np.float32))


def band_masks():
    key, query = np.arange(P)[:, None], np.arange(P)[None, :]
    return (key > query).astype(np.float32), np.where(key <= query, 0.0, NONE).astype(np.dtype("bfloat16"))


def pair_weights(wq, wk, wv, wo):
    q = wq.reshape(KC, P, PAIRS, P).transpose(2, 1, 0, 3).reshape(PAIRS, P, KC * P)
    k = wk.reshape(P, PAIRS, P).transpose(1, 0, 2)
    v = wv.reshape(P, PAIRS, P).transpose(1, 0, 2)
    return np.concatenate([q, k, v, wo.reshape(PAIRS, P, C)], axis=2)


def expert_weights(gate_up, down, sh_gate, sh_up, sh_down):
    g = np.concatenate([sh_gate.reshape(SHARED, NI, C), gate_up[:, :NI]])
    u = np.concatenate([sh_up.reshape(SHARED, NI, C), gate_up[:, NI:]])
    d = np.concatenate([sh_down.reshape(C, SHARED, NI).transpose(1, 0, 2), down])
    gu = np.concatenate([g, u], axis=1).transpose(0, 2, 1).reshape(EXPERTS, KC, P, 2 * NI).transpose(0, 2, 1, 3)
    return np.concatenate([gu.reshape(EXPERTS, P, KC * 2 * NI), d.transpose(0, 2, 1)], axis=2)


def selectors():
    one = np.equal(np.arange(PARTS * NE)[:, None] % NE, np.arange(NE)[None, :])
    return np.repeat(one, P, axis=1).astype(np.dtype("bfloat16"))


def kernel(**inputs):
    import concourse.bacc as bacc
    from concourse.bass_utils import run_bass_kernel_spmd

    a = {k: np.asarray(v) for k, v in inputs.items()}
    cosv, sinv = rope_table()
    window, causal = band_masks()
    arrays = {
        "x": a["x"],
        "wqkv": np.concatenate([a["L0_attn_Wq"], a["L0_attn_Wkv"]], axis=0).T,
        "wp": a["L0_attn_Wproj"].T,
        "ctxT": a["ctx_512"].reshape(B * M, CD).T,
        "wx": pair_weights(a["L0_xattn_Wq"], a["L0_xattn_Wk"], a["L0_xattn_Wv"],
                           a["L0_xattn_Wo"]),
        "bo2": np.concatenate([a["L0_xattn_bo"], a["L0_xattn_bo"]])[None, :],
        "wf": expert_weights(a["L0_ffn_experts_gate_up"], a["L0_ffn_experts_down"], a["L0_ffn_shared_gate_w"],
                             a["L0_ffn_shared_up_w"], a["L0_ffn_shared_down_w"]),
        "wg": a["L0_ffn_gate_weight"].T,
        "ebias": a["L0_ffn_e_score_correction_bias"],
        "sel": selectors(),
        "cosv": cosv, "sinv": sinv, "window": window, "causal": causal,
    }
    arrays = {k: np.ascontiguousarray(v) for k, v in arrays.items()}
    nc = bacc.Bacc("TRN2", target_bir_lowering=False, num_devices=1)
    ins = {k: nc.dram_tensor(f"{k}_dram", v.shape, mybir.dt.from_np(v.dtype), kind="ExternalInput").ap()
           for k, v in arrays.items()}
    out = nc.dram_tensor("out_dram", (B, T, C), F32, kind="ExternalOutput").ap()
    mk_decoder(nc, ins, out)
    r = run_bass_kernel_spmd(nc, [{f"{k}_dram": v for k, v in arrays.items()}], core_ids=[0])
    return r.results[0]["out_dram"]
```

```python
from contextlib import ExitStack

import numpy as np

import concourse.bass as bass
from concourse import mybir

ACT = mybir.ActivationFunctionType
ALU = mybir.AluOpType
AX = mybir.AxisListType
F32 = mybir.dt.float32
F32R = mybir.dt.float32r
BF16 = mybir.dt.bfloat16

P = 128
B, T, C = 2, 512, 256
TILES = T // P
NT = B * TILES
KC = C // P
EPS_LN = 1e-5
EPS_NORM = 1e-6

NH, NKV, HD = 16, 4, 16
REP = NH // NKV
QKH = NH + NKV
QKC = QKH * HD
QKV = QKC + NKV * HD
SCALE_A = HD ** -0.5
GW = REP * HD

XH, XD, M, CD = 16, 64, 1024, 128
SCALE_X = XD ** -0.5
PAIRS = XH // 2
UNITS_X = B * PAIRS
QB = T // P
KB = M // P
QKV_X = (KC + 2) * P
WPAIR = QKV_X + C
CTX_PIECE = B * M // NT
JOBS = 5

NE, NI, GROUPS, TOP_GROUPS, TOP_K, ROUTE_SCALE, SHARED = 32, 128, 8, 4, 6, 2.5, 2
GS = NE // GROUPS
EXPERTS = NE + SHARED
GU = KC * 2 * NI
WEXP = GU + C
PARTS = 3
NONE, TAKEN = -1e30, 1e30


def mk_decoder(nc, ins, out):
    ctx = ExitStack()
    stage_a = ExitStack()
    with ctx:
        def sb(name, shape, dt, stack=ctx):
            return stack.enter_context(nc.sbuf_tensor(name, shape, dt))

        def sem(name):
            return ctx.enter_context(nc.semaphore(name))

        banks = ctx.enter_context(nc.psum_tensor("banks", [P, 8, 512], F32))

        ident = sb("ident", [P, P], F32)
        identb = sb("identb", [P, P], BF16)
        x_sb = sb("x_sb", [P, NT, C], F32)
        stats = sb("stats", [P, NT, 6], F32)
        mv = sb("mv", [P, NT, 2], F32)
        ve = sb("ve", [P, NT], F32)
        sd = sb("sd", [P, NT], F32)
        sr = sb("sr", [P, NT], F32)
        rstd = sb("rstd", [P, NT], F32)
        xn = sb("xn", [P, 2, C], F32)
        primer = sb("primer", [P, NT], F32)
        nT_h = sb("nT_h", [P, KC, B * T], F32R)
        nT_l = sb("nT_l", [P, KC, B * T], F32R)
        wraw = sb("wraw", [P, 2, WPAIR], F32)
        ctx_h = sb("ctx_h", [P, B * M], F32R)
        ctx_l = sb("ctx_l", [P, B * M], F32R)

        def sa(name, shape, dt):
            return sb(name, shape, dt, stage_a)

        wqkv = sa("wqkv", [P, KC, QKV], F32)
        wqkv_h = sa("wqkv_h", [P, KC, QKV], F32R)
        wqkv_l = sa("wqkv_l", [P, KC, QKV], F32R)
        wp = sa("wp", [P, KC, C], F32)
        wp_h = sa("wp_h", [P, KC, C], F32R)
        wp_l = sa("wp_l", [P, KC, C], F32R)
        cosv = sa("cosv", [P, TILES, HD], F32)
        sinv = sa("sinv", [P, TILES, HD], F32)
        window = sa("window", [P, P], F32)
        causal = sa("causal", [P, P], BF16)
        xh = sa("xh", [P, KC, T], F32R)
        xl = sa("xl", [P, KC, T], F32R)
        qkv = sa("qkv", [P, NT, QKV], F32)
        sq = sa("sq", [P, TILES, QKC], F32)
        ss = sa("ss", [P, NT * QKH], F32)
        s0 = sa("s0", [P, NT * QKH], F32)
        s1 = sa("s1", [P, NT * QKH], F32)
        qn = sa("qn", [P, QKH, HD], F32)
        ra = sa("ra", [P, QKH, HD], F32)
        rb = sa("rb", [P, QKH, HD], F32)
        hl = sa("hl", [P, 2, QKH, 4, HD], F32R)
        qT = sa("qT", [64, 2, NH, P], F32R)
        kT = sa("kT", [64, TILES, NKV, P], F32R)
        va = sa("va", [P, TILES, NKV, REP, 2 * GW], F32)
        E = sa("E", [P, 2, 2, REP, P], F32)
        y = sa("y", [P, 2, KC, P], F32)
        rowsum = sa("rowsum", [P, 2, KC, P], F32)
        yh = sa("yh", [P, KC, P], F32R)
        yl = sa("yl", [P, KC, P], F32R)

        ctxT = sa("ctxT", [P, B * M], F32)
        stage_a.close()

        stage_b = ExitStack()

        def sx(name, shape, dt):
            return sb(name, shape, dt, stage_b)

        wx_h = sx("wx_h", [P, QKV_X], F32R)
        wx_l = sx("wx_l", [P, QKV_X], F32R)
        k_st = sx("k_st", [P, B, 2, M], F32R)
        q_hh = sx("q_hh", [P, B, 2, T], F32R)
        q_ll = sx("q_ll", [P, B, 2, T], F32R)
        v_raw = sx("v_raw", [P, 2, 512], F32)
        v_hl = sx("v_hl", [P, B, KB, 2, 2, XD], F32R)
        nmax = sx("nmax", [P, 2 * QB], F32)
        before = ExitStack()
        xn2 = sb("xn2", [P, NT, C], F32, before)
        before.close()
        pT_h = sx("pT_h", [P, 4, T], F32R)
        pT_l = sx("pT_l", [P, 4, T], F32R)
        o_low = sx("o_low", [P, T], F32)
        o_all = sx("o_all", [P, UNITS_X, T], F32)
        sums = sx("sums", [P, 2 * UNITS_X * QB], F32)
        rsum = sx("rsum", [P, UNITS_X, 2, QB], F32)
        wo_h = sx("wo_h", [P, PAIRS, C], F32R)
        wo_l = sx("wo_l", [P, PAIRS, C], F32R)
        bo2 = sx("bo2", [1, 2 * C], F32)
        ones1 = sx("ones1", [1, P], F32)
        heads = ExitStack()
        probs = sb("probs", [P, 2, QB, M], F32, heads)
        heads.close()
        rexp = sx("rexp", [P, 4, QB, P], F32)
        on = sx("on", [P, 4, T], F32)
        on_h = sx("on_h", [P, 4, T], F32R)
        on_l = sx("on_l", [P, 4, T], F32R)
        stage_b.close()

        stage_f = ExitStack()

        def sf(name, shape, dt):
            return sb(name, shape, dt, stage_f)

        xn3 = sf("xn3", [P, 4, C], F32)
        wf_raw = sf("wf_raw", [P, 2, WEXP], F32)
        wf_h = sf("wf_h", [P, 2, WEXP], F32R)
        wf_l = sf("wf_l", [P, 2, WEXP], F32R)
        sel = sf("sel", [PARTS * NE, NE * P], BF16)
        wg = sf("wg", [P, KC, NE], F32)
        wg_h = sf("wg_h", [P, KC, NE], F32R)
        wg_l = sf("wg_l", [P, KC, NE], F32R)
        ebias = sf("ebias", [P, NE], F32)
        lgT = sf("lgT", [NE, B * T], F32)
        sc = sf("sc", [P, NT, NE], F32)
        sfc = sf("sfc", [P, NT, NE], F32)
        gval = sf("gval", [P, NT, GROUPS + 8], F32)
        gtop = sf("gtop", [P, NT, 8], F32)
        gout = sf("gout", [P, NT, GROUPS + 8], F32)
        gmask = sf("gmask", [P, NT, GROUPS], F32)
        evalue = sf("evalue", [P, NT, NE + 8], F32)
        etop = sf("etop", [P, NT, 8], F32)
        eout = sf("eout", [P, NT, NE + 8], F32)
        tw = sf("tw", [P, NT, NE], F32)
        tsum = sf("tsum", [P, NT], F32)
        comb = sf("comb", [P, NT, NE], F32)
        cres = sf("cres", [P, NT, NE], F32)
        parts = sf("parts", [P, NT, PARTS, NE], BF16)
        combT = sf("combT", [PARTS * NE, B * T], BF16)
        sg = sf("sg", [P, 2, 512], F32)
        gc = sf("gc", [P, 2, 512], F32)
        hid = sf("hid", [P, 2, 512], F32)
        hid_h = sf("hid_h", [P, 2, 512], F32R)
        hid_l = sf("hid_l", [P, 2, 512], F32R)
        yT = sf("yT", [P, 4, 512], F32)
        y_out = sf("y_out", [P, NT, C], F32)
        stage_f.close()

        YF_BANK, G_BANK, C_BANK, U_BANK = 0, 4, 6, 7
        L_BANKS = (C_BANK, G_BANK + 1)

        S_BANK, PT_BANK, O_BANK, MISC = 0, 4, 6, 7
        Y_BANK, R_BANK = 0, 4

        ctx_in = sem("ctx_in")
        ctx_hi = sem("ctx_hi")
        ctx_ok = sem("ctx_ok")
        wx_in = sem("wx_in")
        bo_in = sem("bo_in")
        wo_ok = sem("wo_ok")
        wx_used = sem("wx_used")
        wk_ok = sem("wk_ok")
        wq_ok = sem("wq_ok")
        wv_ok = sem("wv_ok")
        pool_step = sem("pool_step")
        pool_go = sem("pool_go")
        pe_go = sem("pe_go")
        misc_ps = sem("misc_ps")
        misc_out = sem("misc_out")
        half_out = sem("half_out")
        mh_ok = sem("mh_ok")
        qlo_ok = sem("qlo_ok")
        q_low = sem("q_low")
        q_ok = sem("q_ok")
        v_ok = sem("v_ok")
        sx_ps = sem("sx_ps")
        max_ok = sem("max_ok")
        ex_ok = sem("ex_ok")
        pT_ps = sem("pT_ps")
        pTh_ok = sem("pTh_ok")
        pTl_ok = sem("pTl_ok")
        o_ps = sem("o_ps")
        o_sum = sem("o_sum")
        o_free = sem("o_free")
        rs_ok = sem("rs_ok")
        rexp_ok = sem("rexp_ok")
        rT_ps = sem("rT_ps")
        on_ok = sem("on_ok")
        onh_ok = sem("onh_ok")
        onl_ok = sem("onl_ok")
        y_used = sem("y_used")
        bias_ok = sem("bias_ok")
        var2_ok = sem("var2_ok")
        sqrt2_ok = sem("sqrt2_ok")
        xn2_ok = sem("xn2_ok")
        nT2_ps = sem("nT2_ps")
        nTh2_ok = sem("nTh2_ok")
        nTl2_ok = sem("nTl2_ok")
        x2_ok = sem("x2_ok")

        var3_ok = sem("var3_ok")
        sqrt3_ok = sem("sqrt3_ok")
        xn3_ok = sem("xn3_ok")
        nT3_ps = sem("nT3_ps")
        nTh3_ok = sem("nTh3_ok")
        nTl3_ok = sem("nTl3_ok")
        gate_in = sem("gate_in")
        wg_hi = sem("wg_hi")
        wg_ok = sem("wg_ok")
        lg_ps = sem("lg_ps")
        lgT_ok = sem("lgT_ok")
        lgN_ps = sem("lgN_ps")
        sc_ok = sem("sc_ok")
        parts_ok = sem("parts_ok")
        combT_ps = sem("combT_ps")
        combT_ok = sem("combT_ok")
        wf_in = [sem("wf_in0"), sem("wf_in1")]
        wf_step = sem("wf_step")
        wgu_ok = sem("wgu_ok")
        wdn_ok = sem("wdn_ok")
        g_ps = sem("g_ps")
        c_ps = sem("c_ps")
        u_ps = sem("u_ps")
        d_ps = sem("d_ps")
        sg_ok = sem("sg_ok")
        gc_ok = sem("gc_ok")
        hid_ok = sem("hid_ok")
        hh_ok = sem("hh_ok")
        hlo_ok = sem("hlo_ok")
        yT_a = sem("yT_a")
        yT_d = sem("yT_d")
        yN_ps = sem("yN_ps")
        y_fin = sem("y_fin")

        x_in = [sem(f"x_in{b}") for b in range(B)]
        wa_in = sem("wa_in")
        wp_in = sem("wp_in")
        const_in = sem("const_in")
        ident_ok = sem("ident_ok")
        ones_ok = sem("ones_ok")
        wa_hi = sem("wa_hi")
        wa_ok = sem("wa_ok")
        wp_ok = sem("wp_ok")
        ra_ok = sem("ra_ok")
        v_placed = sem("v_placed")
        rec_ok = sem("rec_ok")
        yn_ok = sem("yn_ok")
        var_ok = sem("var_ok")
        sqrt_ok = sem("sqrt_ok")
        rope_b = sem("rope_b")
        dve_step = sem("dve_step")
        xn_ok = sem("xn_ok")
        xT_ps = sem("xT_ps")
        xh_ok = sem("xh_ok")
        xl_ok = sem("xl_ok")
        qkv_ps = sem("qkv_ps")
        qkv_ok = sem("qkv_ok")
        ss_ok = sem("ss_ok")
        s0_ok = sem("s0_ok")
        qn_ok = sem("qn_ok")
        r_ok = sem("r_ok")
        hi_ok = sem("hi_ok")
        hl_ok = sem("hl_ok")
        qkT_ps = sem("qkT_ps")
        even_ok = sem("even_ok")
        odd_ok = sem("odd_ok")
        s_ps = sem("s_ps")
        exp_ok = sem("exp_ok")
        mask_ok = sem("mask_ok")
        pv_done = sem("pv_done")
        y_ok = sem("y_ok")
        yh_ok = sem("yh_ok")
        yl_ok = sem("yl_ok")
        proj_ps = sem("proj_ps")
        x1_ok = sem("x1_ok")
        stats_ok = sem("stats_ok")
        out_done = sem("out_done")

        UNITS = TILES * NKV
        def ahead(b, t):
            return b * TILES + t + 2 if t + 2 < TILES else (b + 1) % B * TILES + t + 2 - TILES

        FIRST_JOBS = ((0, "k0"), (0, "k1"), (0, "q"), (1, "k0"), (0, "v0"), (1, "k1"), (0, "v1"))

        def place(unit, name):
            if isinstance(unit, int) and (unit, name) in FIRST_JOBS:
                return FIRST_JOBS.index((unit, name))
            return unit * JOBS + ("k0", "k1", "q", "v0", "v1").index(name)

        def halves(unit, name):
            if isinstance(unit, int) and (unit, name) in FIRST_JOBS:
                before_ = FIRST_JOBS[:FIRST_JOBS.index((unit, name))]
                return sum({"k": 2, "q": 4, "v": 0}[n[0]] for _, n in before_)
            return unit * 8 + {"k0": 0, "k1": 2, "q": 4}[name]

        block = ctx.enter_context(nc.Block())

        @block.sync
        def _(sp):
            for b in range(B):
                sp.dma_start(x_sb[:, b * TILES:(b + 1) * TILES], ins["x"][b].rearrange("(t p) c -> p t c", p=P))\
                    .then_inc(x_in[b], 16)
            sp.dma_start(wqkv[:], ins["wqkv"].rearrange("(k p) n -> p k n", p=P)).then_inc(wa_in, 16)
            sp.dma_start(wp[:], ins["wp"].rearrange("(k p) n -> p k n", p=P)).then_inc(wp_in, 16)
            sp.dma_start(cosv[:], ins["cosv"].rearrange("(t p) d -> p t d", p=P)).then_inc(const_in, 16)
            sp.dma_start(sinv[:], ins["sinv"].rearrange("(t p) d -> p t d", p=P)).then_inc(const_in, 16)
            sp.dma_start(window[:], ins["window"]).then_inc(const_in, 16)
            sp.dma_start(causal[:], ins["causal"]).then_inc(const_in, 16)
            sp.sem_inc(o_free, 1)
            sp.sem_inc(o_sum, 2)
            sp.sem_inc(ss_ok, TILES)
            sp.sem_inc(pv_done, 2)
            sp.sem_inc(y_ok, 2)
            sp.dma_start(ctxT[:], ins["ctxT"]).then_inc(ctx_in, 16)

            def load_pair(pair):
                sp.dma_start(wraw[:, bass.ds(pair % 2, 1), :].rearrange("p o n -> p (o n)"),
                             ins["wx"][bass.ds(pair, 1)].rearrange("o p n -> p (o n)")).then_inc(wx_in, 16)

            sp.dma_start(wraw[:, 0], ins["wx"][0]).then_inc(wx_in, 16)
            sp.wait_ge(wx_in, 16)
            sp.dma_start(wraw[:, 1], ins["wx"][1]).then_inc(wx_in, 16)
            sp.wait_ge(x1_ok, NT)
            sp.dma_start(bo2[:], ins["bo2"]).then_inc(bo_in, 16)
            with sp.Fori(0, PAIRS - 2) as p:
                sp.wait_ge(wx_used, p + 1)
                sp.wait_ge(wx_in, p * 16 + 32)
                load_pair(p + 2)
            sp.wait_ge(o_free, 2 * UNITS_X + 1)
            sp.dma_start(wg[:], ins["wg"].rearrange("(k p) e -> p k e", p=P)).then_inc(gate_in, 16)
            sp.dma_start(ebias[:], ins["ebias"].partition_broadcast(P)).then_inc(gate_in, 16)
            sp.dma_start(sel[:], ins["sel"]).then_inc(gate_in, 16)
            for j in range(2):
                sp.dma_start(wf_raw[:, j], ins["wf"][j]).then_inc(wf_in[j], 16)
            with sp.Fori(1, EXPERTS // 2) as i:
                for j in range(2):
                    sp.wait_ge(wdn_ok, i * 2 + j - 1)
                    sp.dma_start(wf_raw[:, j], ins["wf"][bass.ds(i * 2 + j, 1)].rearrange("o p n -> p (o n)"))\
                        .then_inc(wf_in[j], 16)
            o_v = out.rearrange("b (t p) c -> p (b t) c", p=P)
            for r in range(NT // 2):
                sp.wait_ge(y_fin, r + 1)
                sp.dma_start(o_v[:, 2 * r:2 * r + 2], y_out[:, 2 * r:2 * r + 2]).then_inc(out_done, 16)
            sp.wait_ge(out_done, 16 * (NT // 2))

        @block.gpsimd
        def _(pool):
            pool.memset(ident[:], 0.0).then_inc(ident_ok, 1)
            pool.wait_ge(ident_ok, 1)
            pool.affine_select(out=ident[:], in_=ident[:], compare_op=ALU.not_equal, fill=1.0, base=0,
                               pattern=[[-1, P]], channel_multiplier=1).then_inc(ident_ok, 1)
            pool.memset(identb[:], 0.0).then_inc(ident_ok, 1)
            pool.wait_ge(ident_ok, 3)
            pool.affine_select(out=identb[:], in_=identb[:], compare_op=ALU.not_equal, fill=1.0, base=0,
                               pattern=[[-1, P]], channel_multiplier=1).then_inc(ident_ok, 1)
            pool.wait_ge(wa_in, 16)
            pool.tensor_copy(wqkv_h[:], wqkv[:]).then_inc(wa_hi, 1)
            pool.wait_ge(wa_hi, 1)
            pool.tensor_tensor(wqkv_l[:], wqkv[:], wqkv_h[:].bitcast(F32), ALU.subtract).then_inc(wa_ok, 1)
            pool.memset(va[:], 0.0).then_inc(ones_ok, 1)
            pool.wait_ge(ones_ok, 1)
            for r in range(REP):
                pool.memset(va[:, :, :, r, GW + r * HD:GW + (r + 1) * HD], 1.0).then_inc(ones_ok, 1)
            pool.wait_ge(wp_in, 16)
            pool.tensor_copy(wp_h[:], wp[:]).then_inc(wa_hi, 1)
            pool.wait_ge(wa_hi, 2)
            pool.tensor_tensor(wp_l[:], wp[:], wp_h[:].bitcast(F32), ALU.subtract).then_inc(wp_ok, 1)
            pool.wait_ge(const_in, 64)

            def rotate(f, t):
                if not (isinstance(f, int) and f == 0):
                    pool.wait_ge(hl_ok, f * 2)
                pool.wait_ge(qn_ok, f + 1)
                pool.sem_inc(pool_go, 1)
                for half in range(2):
                    lo, hi = (0, HD // 2) if half == 0 else (HD // 2, HD)
                    src = slice(HD // 2, HD) if half == 0 else slice(0, HD // 2)
                    pool.tensor_tensor(rb[:, :, lo:hi], qn[:, :, src],
                                       sinv[:, t % TILES, lo:hi].unsqueeze(1).broadcast_to([P, QKH, HD // 2]),
                                       ALU.mult).then_inc(rope_b, 1)
                pool.wait_ge(rope_b, f * 2 + 2)
                pool.wait_ge(ra_ok, f + 1)
                pool.tensor_tensor(rb[:], ra[:], rb[:], ALU.add).then_inc(r_ok, 1)
                pool.wait_ge(r_ok, f + 1)
                pool.wait_ge(hi_ok, f + 1)
                for heads_, los, his in ((slice(0, NH), slice(2, 4), slice(0, 2)), (slice(NH, QKH), slice(1, 4, 2), slice(0, 4, 2))):
                    raw = rb[:, heads_].unsqueeze(2).broadcast_to([P, heads_.stop - heads_.start, 2, HD])
                    pool.tensor_tensor(hl[:, t % 2, heads_, los, :], raw, hl[:, t % 2, heads_, his, :].bitcast(F32),
                                       ALU.subtract).then_inc(hl_ok, 1)

            def split_ctx(c):
                cols = bass.ds(c * CTX_PIECE, CTX_PIECE)
                pool.sem_inc(pool_go, 1)
                pool.tensor_copy(ctx_h[:, cols], ctxT[:, cols]).then_inc(ctx_hi, 1)
                pool.wait_ge(ctx_hi, c + 1)
                pool.sem_inc(pool_go, 1)
                pool.tensor_tensor(ctx_l[:, cols], ctxT[:, cols], ctx_h[:, cols].bitcast(F32), ALU.subtract)\
                    .then_inc(ctx_ok, 1)

            rotate(0, 0)
            rotate(1, 1)
            pool.wait_ge(ctx_in, 16)
            with pool.Fori(0, B) as b:
                for t in range(TILES):
                    rotate(b * TILES + t + 2, t + 2)
                    split_ctx(b * TILES + t)

            pool.wait_ge(x1_ok, NT)
            pool.memset(ones1[:], 1.0).then_inc(ones_ok, 1)

            psteps = [0]

            def split(h_out, l_out, raw, base, ready, waits):
                for s_, v_ in waits:
                    pool.wait_ge(s_, v_)
                pool.sem_inc(pool_go, 1)
                psteps[0] += 1
                pool.tensor_copy(h_out, raw).then_inc(pool_step, 1)
                pool.wait_ge(pool_step, base + psteps[0])
                pool.sem_inc(pool_go, 1)
                pool.tensor_tensor(l_out, raw, h_out.bitcast(F32), ALU.subtract).then_inc(*ready)

            def raw_w(pair, lo, hi):
                slot = bass.ds(pair % 2, 1) if not isinstance(pair, int) else slice(pair % 2, pair % 2 + 1)
                return wraw[:, slot, lo:hi].rearrange("p o n -> p (o n)")

            def split_w(pair, base, blocks, ready, waits):
                cols = slice(blocks[0] * P, blocks[1] * P)
                split(wx_h[:, cols], wx_l[:, cols], raw_w(pair, cols.start, cols.stop), base, (ready, 1), waits)

            WQ, WK, WV = (0, KC), (KC, KC + 1), (KC + 1, KC + 2)

            def split_wo(pair, base):
                slot = bass.ds(pair, 1) if not isinstance(pair, int) else slice(pair, pair + 1)
                wh, wl = (w[:, slot, :].rearrange("p o n -> p (o n)") for w in (wo_h, wo_l))
                split(wh, wl, raw_w(pair, QKV_X, WPAIR), base, (wo_ok, 1), [])
                pool.wait_ge(wo_ok, pair + 1)
                pool.sem_inc(wx_used, 1)

            def double_q(unit, b):
                pool.wait_ge(qlo_ok, unit)
                pool.sem_inc(pool_go, 1)
                pool.tensor_copy(q_ll[0:64, b, 1], q_ll[64:P, b, 1].bitcast(F32)).then_inc(q_low, 1)
                pool.wait_ge(q_low, unit)
                pool.sem_inc(pool_go, 1)
                pool.tensor_copy(q_ll[64:P, b, 0], q_ll[0:64, b, 0].bitcast(F32)).then_inc(q_ok, 1)
                pool.wait_ge(q_ok, unit + 1)

            def split_v(unit, b, a, base):
                half = v_hl[:, b, 4 * a:4 * a + 4]
                split(half[:, :, :, 0], half[:, :, :, 1], v_raw[:, a].rearrange("p (k h d) -> p k h d", k=4, h=2), base,
                      (v_ok, 1), [(misc_out, place(unit, f"v{a}") + 1)])
                if a == 1:
                    pool.wait_ge(v_ok, unit * 2 + 2)

            def add_o(head, h, unit):
                pool.wait_ge(o_free, head + 2)
                pool.sem_inc(pool_go, 1)
                rows = slice(64 * h, 64 * h + 64)
                dst = o_all[rows, bass.ds(unit, 1) if not isinstance(unit, int) else slice(unit, unit + 1), :]\
                    .rearrange("p o n -> p (o n)")
                pool.tensor_tensor(dst, dst, o_low[rows], ALU.add).then_inc(o_sum, 1)
                pool.wait_ge(o_sum, head + 3)

            split_w(0, 0, WK, wk_ok, [(wx_in, 16)])
            split_w(0, 0, WQ, wq_ok, [])
            split_w(0, 0, WV, wv_ok, [])
            for a in range(2):
                split_v(0, 0, a, 0)
            split_wo(0, 0)
            first_split = psteps[0]
            PER_PAIR = 8
            with pool.Fori(0, PAIRS - 1) as p:
                psteps[0] = 0
                base = p * PER_PAIR + first_split
                for b in range(B):
                    unit, nu = p * 2 + b, p * 2 + b + 1
                    double_q(nu, 1 - b)
                    if b == 0:
                        split_w(p + 1, base, WK, wk_ok, [(wx_in, p * 16 + 32), (misc_ps, place(nu, "k1") + 1)])
                    add_o(unit * 2, 0, unit)
                    if b == 0:
                        split_w(p + 1, base, WQ, wq_ok, [(misc_ps, place(nu, "q") + 1)])
                    split_v(nu, 1 - b, 0, base)
                    split_v(nu, 1 - b, 1, base)
                    if b == 0:
                        split_w(p + 1, base, WV, wv_ok, [(misc_ps, place(nu, "v1") + 1)])
                        split_wo(p + 1, base)
                    add_o(unit * 2 + 1, 1, unit)
                assert psteps[0] == PER_PAIR
            psteps[0] = 0
            end_base = first_split + (PAIRS - 1) * PER_PAIR
            unit = UNITS_X - 2
            double_q(unit + 1, 1)
            add_o(unit * 2, 0, unit)
            for a in range(2):
                split_v(unit + 1, 1, a, end_base)
            add_o(unit * 2 + 1, 1, unit)
            for h in range(2):
                add_o(unit * 2 + 2 + h, h, unit + 1)

            def low_on(v, j):
                pool.wait_ge(onh_ok, v + 1)
                pool.tensor_tensor(on_l[:, j], on[:, j], on_h[:, j].bitcast(F32), ALU.subtract).then_inc(onl_ok, 1)

            with pool.Fori(0, PAIRS // 4) as i:
                for j in range(4):
                    low_on(i * 4 + j, j)

            def split_part(j, e, cols, first_step, ready):
                pool.tensor_copy(wf_h[:, j, cols], wf_raw[:, j, cols]).then_inc(wf_step, 1)
                low_part(j, e, cols, first_step, ready)

            def low_part(j, e, cols, first_step, ready):
                pool.wait_ge(wf_step, e * 2 + first_step)
                pool.sem_inc(pool_go, 1)
                pool.tensor_tensor(wf_l[:, j, cols], wf_raw[:, j, cols], wf_h[:, j, cols].bitcast(F32), ALU.subtract)\
                    .then_inc(ready, 1)

            for v in range(PAIRS):
                low_on(PAIRS + v, v % 4)
                if v == 1:
                    pool.wait_ge(wg_hi, 1)
                    pool.tensor_tensor(wg_l[:], wg[:], wg_h[:].bitcast(F32), ALU.subtract).then_inc(wg_ok, 1)
                if v == 3:
                    low_part(0, 0, slice(0, GU), 1, wgu_ok)
                if v == 5:
                    low_part(0, 0, slice(GU, WEXP), 2, wdn_ok)
            low_part(1, 1, slice(0, GU), 1, wgu_ok)
            low_part(1, 1, slice(GU, WEXP), 2, wdn_ok)
            with pool.Fori(1, EXPERTS // 2) as i:
                for j in range(2):
                    e = i * 2 + j
                    pool.wait_ge(wf_in[j], i * 16 + 16)
                    pool.wait_ge(u_ps, i * 4 + 2 * j - 2)
                    pool.sem_inc(pool_go, 1)
                    split_part(j, e, slice(0, GU), 1, wgu_ok)
                    pool.wait_ge(d_ps, i * 4 + 2 * j - 2)
                    pool.sem_inc(pool_go, 1)
                    split_part(j, e, slice(GU, WEXP), 2, wdn_ok)

        @block.scalar
        def _(act):
            def copy_yh(b, t):
                act.wait_ge(yn_ok, (b * TILES + t + 1) * KC)
                if t:
                    act.wait_ge(proj_ps, b * TILES + t)
                act.activation(yh[:], y[:, t % 2], ACT.Copy).then_inc(yh_ok, 1)

            act.wait_ge(var_ok, 1)
            act.activation(sd[:], ve[:], ACT.Sqrt).then_inc(sqrt_ok, 1)
            with act.Fori(0, B) as b:
                def copy_xh(t):
                    act.wait_ge(xT_ps, b * TILES + t + 1)
                    act.activation(xh[:, :, t * P:(t + 1) * P],
                                   banks[:, t % 2, 0:C].rearrange("p (k n) -> p k n", k=KC),
                                   ACT.Copy).then_inc(xh_ok, 1)

                def copy_qkv(t):
                    act.wait_ge(qkv_ps, b * TILES + t + 1)
                    act.activation(qkv[:, bass.ds(b * TILES + t, 1), :].rearrange("p o n -> p (o n)"),
                                   banks[:, 2 + t % 2, 0:QKV], ACT.Copy)
                    act.wait_ge(ss_ok, b * TILES + t + 1)
                    act.activation(sq[:, t], banks[:, 2 + t % 2, 0:QKC], ACT.Square).then_inc(qkv_ok, 1)

                copy_xh(0)
                copy_xh(1)
                copy_qkv(0)
                copy_xh(2)
                copy_qkv(1)
                copy_xh(3)
                copy_qkv(2)
                copy_qkv(3)
            act.wait_ge(ss_ok, NT + TILES)
            act.activation(s0[:], ss[:], ACT.Sqrt).then_inc(s0_ok, 1)
            act.activation(primer[:], sd[:], ACT.Exp)

            def high_heads(f, t):
                act.wait_ge(r_ok, f + 1)
                act.activation(hl[:, t % 2, 0:NH, 0:2, :], rb[:, 0:NH].unsqueeze(2).broadcast_to([P, NH, 2, HD]), ACT.Copy)
                act.activation(hl[:, t % 2, NH:QKH, 0:4:2, :], rb[:, NH:QKH].unsqueeze(2).broadcast_to([P, NKV, 2, HD]),
                               ACT.Copy).then_inc(hi_ok, 1)

            def place_v(tile, t):
                tile = slice(tile, tile + 1) if isinstance(tile, int) else bass.ds(tile, 1)
                for r in range(REP):
                    last = act.activation(va[:, t % TILES, :, r, r * HD:(r + 1) * HD],
                                          qkv[:, tile, QKC:QKV].rearrange("p o (g d) -> p (o g) d", g=NKV), ACT.Copy)
                last.then_inc(v_placed, 1)

            def even_heads(f, t, k):
                act.wait_ge(qkT_ps, f * 3 + k + 1)
                src = banks[0:64, 2, :].rearrange("p (h n) -> p h n", n=P)
                if k < 2:
                    act.activation(qT[:, t % 2, 8 * k:8 * k + 8:2], src, ACT.Copy).then_inc(even_ok, 1)
                else:
                    act.activation(kT[:, t % TILES, 0:NKV:2], src[:, 0:NKV // 2], ACT.Copy).then_inc(even_ok, 1)

            def exp_unit(unit, n):
                act.wait_ge(s_ps, unit + 1)
                act.wait_ge(pv_done, unit + 1)
                k0 = 0 if n // NKV else 1
                r = 4 + 2 * (n % 2)
                act.activation(E[:, n % 2, k0:2], banks[:, r + k0:r + 2, :].rearrange("p a (h n) -> p a h n", n=P),
                               ACT.Exp, scale=SCALE_A).then_inc(exp_ok, 1)

            def copy_out(unit, n):
                t, g = n // NKV, n % NKV
                act.wait_ge(pv_done, unit + 3)
                rows = slice(GW * (g % 2), GW * (g % 2) + GW)
                act.activation(rowsum[rows, t % 2, g // 2], banks[GW:2 * GW, n % 2, 0:P], ACT.Copy)
                act.activation(y[rows, t % 2, g // 2], banks[0:GW, n % 2, 0:P], ACT.Copy).then_inc(y_ok, 1)

            act.wait_ge(ones_ok, REP + 1)
            for f in range(2):
                place_v(f, f)
            high_heads(0, 0)
            for k in range(3):
                even_heads(0, 0, k)
            high_heads(1, 1)
            with act.Fori(0, B) as b:
                exp_unit(b * UNITS, 0)
                for n in range(UNITS):
                    t, g = n // NKV, n % NKV
                    if n + 1 < UNITS:
                        exp_unit(b * UNITS + n + 1, n + 1)
                    if g < 3:
                        even_heads(b * TILES + t + 1, t + 1, g)
                    if g == 1:
                        place_v(ahead(b, t), t + 2)
                    if g == 1 and t >= 1:
                        copy_yh(b, t - 1)
                    if g == 3:
                        high_heads(b * TILES + t + 2, t + 2)
                    copy_out(b * UNITS + n, n)
                copy_yh(b, TILES - 1)

            def high_x(j):
                act.wait_ge(nT2_ps, j + 1)
                act.activation(nT_h[:, :, j * P:(j + 1) * P], banks[:, j, 0:C].rearrange("p (k n) -> p k n", k=KC),
                               ACT.Copy).then_inc(nTh2_ok, 1)

            def high_x1(k):
                act.wait_ge(nT2_ps, TILES + k + 1)
                act.activation(nT_h[:, :, T + k * 2 * P:T + (k + 1) * 2 * P].rearrange("p k (t n) -> p t k n", n=P),
                               banks[:, PT_BANK + k].rearrange("p (t k n) -> p t k n", t=2, k=KC), ACT.Copy)\
                    .then_inc(nTh2_ok, 1)

            def high_q(unit, b, heads_=(0, 1)):
                act.wait_ge(misc_ps, place(unit, "q") + 1)
                for h in heads_:
                    for rows in (slice(64 * h, 64 * h + 64), slice(64 - 64 * h, P - 64 * h)):
                        act.activation(q_hh[rows, b, h], banks[64 * h:64 * h + 64, MISC], ACT.Copy, scale=SCALE_X)\
                            .then_inc(mh_ok, 1)

            def high_k(unit, b, c, heads_=(0, 1), bank=MISC):
                act.wait_ge(misc_ps, place(unit, f"k{c}") + 1)
                for h in heads_:
                    rows = slice(64 * h, 64 * h + 64)
                    act.activation(k_st[rows, b, h, c * 512:c * 512 + 512], banks[rows, bank], ACT.Copy)\
                        .then_inc(mh_ok, 1)

            def copy_v(unit, a):
                act.wait_ge(misc_ps, place(unit, f"v{a}") + 1)
                if not (isinstance(unit, int) and unit == 0):
                    act.wait_ge(v_ok, unit * 2 - 1 + a)
                act.activation(v_raw[:, a], banks[:, MISC], ACT.Copy).then_inc(misc_out, 1)

            def exp_x(head, h, q):
                act.wait_ge(max_ok, head * QB + q + 1)
                act.activation(probs[:, h, q], banks[:, S_BANK + 2 * (q % 2):S_BANK + 2 * (q % 2) + 2]
                               .rearrange("p a n -> p (a n)"), ACT.Exp, bias=nmax[:, h * QB + q:h * QB + q + 1],
                               accum_out=sums[:, bass.ds(head * QB + q, 1)]).then_inc(ex_ok, 1)

            def high_p(head, kb):
                act.wait_ge(pT_ps, head * KB + kb + 1)
                act.activation(pT_h[:, kb % 4], banks[:, PT_BANK + kb % 2], ACT.Copy).then_inc(pTh_ok, 1)

            def copy_o(head, h, unit):
                act.wait_ge(o_ps, head + 1)
                rows = slice(64 * h, 64 * h + 64)
                act.activation(o_all[rows, bass.ds(unit, 1), :].rearrange("p o n -> p (o n)"), banks[0:64, O_BANK], ACT.Copy)
                act.wait_ge(o_sum, head + 1)
                act.activation(o_low[rows], banks[64:P, O_BANK], ACT.Copy).then_inc(o_free, 1)

            def half(unit, b, h, jobs, scored, more=True):
                head = unit * 2 + h
                for kb in range(KB):
                    high_p(head, kb)
                    if kb == 1 and h == 0 and scored:
                        exp_x(head + 1, 1 - h, 0)
                    if jobs and h == 0 and kb in (1, 3):
                        high_q(unit + 1, 1 - b, (kb // 2,))
                    if jobs and h == 0 and kb == 5:
                        copy_v(unit + 1, 0)
                    if jobs and h == 1 and kb == 1:
                        copy_v(unit + 1, 1)
                    if jobs and more and h == 1 and kb == 3:
                        high_k(unit + 2, b, 0)
                    if jobs and more and h == 1 and kb in (5, 7):
                        high_k(unit + 2, b, 1, (kb // 2 - 2,))
                    if kb % 2 == 1 and scored and (h, kb) != (0, 1):
                        exp_x(head + 1, 1 - h, kb // 2)
                copy_o(head, h, unit)

            act.wait_ge(var2_ok, 1)
            act.activation(sd[:], ve[:], ACT.Sqrt).then_inc(sqrt2_ok, 1)
            act.activation(rsum[:, 0, 0, 0:1], ve[:, 0:1], ACT.Exp)
            high_k(0, 0, 0)
            for j in range(TILES):
                high_x(j)
            high_k(0, 0, 1, bank=O_BANK)
            high_q(0, 0)
            exp_x(0, 0, 0)
            for k in range(2):
                high_x1(k)
            high_k(1, 1, 0)
            exp_x(0, 0, 1)
            copy_v(0, 0)
            exp_x(0, 0, 2)
            high_k(1, 1, 1)
            exp_x(0, 0, 3)
            copy_v(0, 1)
            with act.Fori(0, PAIRS - 1) as p:
                for b in range(B):
                    for h in range(2):
                        half(p * 2 + b, b, h, True, True)
            for b in range(B):
                for h in range(2):
                    half(UNITS_X - 2 + b, b, h, b == 0, b + h < 2, more=False)
            act.activation(sd[:, 0:1], ve[:, 0:1], ACT.Sqrt)
            act.wait_ge(rs_ok, 1)

            def spread_sums(unit, j):
                act.activation(rexp[:, j].rearrange("p q (h d) -> p q h d", h=2),
                               rsum[:, bass.ds(unit, 1)].rearrange("p o h q -> p q (o h)").unsqueeze(3)
                               .broadcast_to([P, QB, 2, XD]), ACT.Copy).then_inc(rexp_ok, 1)

            def high_on(unit, j):
                act.wait_ge(on_ok, unit + 1)
                act.activation(on_h[:, j], on[:, j], ACT.Copy).then_inc(onh_ok, 1)

            for j in range(4):
                spread_sums(2 * j, j)
            with act.Fori(0, PAIRS // 4) as i:
                for j in range(4):
                    high_on(i * 4 + j, j)
                    spread_sums((i + 1) % 2 * 8 + i + 2 * j, j)

            def root3(b):
                act.wait_ge(var3_ok, b + 1)
                act.activation(sd[:, b * TILES:(b + 1) * TILES], ve[:, b * TILES:(b + 1) * TILES], ACT.Sqrt)\
                    .then_inc(sqrt3_ok, 1)

            def high_n(b, k):
                act.wait_ge(nT3_ps, b * 2 + k + 1)
                act.activation(nT_h[:, :, b * T + k * 2 * P:b * T + (k + 1) * 2 * P].rearrange("p k (t n) -> p t k n", n=P),
                               banks[:, 2 * b + k].rearrange("p (t k n) -> p t k n", t=2, k=KC), ACT.Copy)\
                    .then_inc(nTh3_ok, 1)

            def high_w(j, cols):
                act.wait_ge(wf_in[j], 16)
                act.activation(wf_h[:, j, cols], wf_raw[:, j, cols], ACT.Copy).then_inc(wf_step, 1)

            for v in range(PAIRS):
                high_on(PAIRS + v, v % 4)
                if v < 4:
                    spread_sums(9 + 2 * v, v)
                if v == 3:
                    root3(0)
                if v == 1:
                    act.wait_ge(gate_in, 48)
                    act.activation(wg_h[:], wg[:], ACT.Copy).then_inc(wg_hi, 1)
                if v == 2:
                    high_w(0, slice(0, GU))
                if v == 4:
                    high_w(0, slice(GU, WEXP))
                if v == 5:
                    high_w(1, slice(0, GU))
                if v == 6:
                    high_w(1, slice(GU, WEXP))
            for k in range(2):
                high_n(0, k)

            def silu(n, c):
                act.wait_ge(g_ps, n + 1)
                act.activation(sg[:, c], banks[:, G_BANK + c], ACT.Silu).then_inc(sg_ok, 1)

            def high_h(n, c):
                act.wait_ge(hid_ok, n + 1)
                act.activation(hid_h[:, c], hid[:, c], ACT.Copy).then_inc(hh_ok, 1)

            root3(1)
            act.wait_ge(lg_ps, 1)
            act.activation(lgT[:, 0:512], banks[0:NE, L_BANKS[0]], ACT.Copy).then_inc(lgT_ok, 1)
            silu(0, 0)
            for k in range(2):
                high_n(1, k)
            high_h(0, 0)
            act.wait_ge(lg_ps, 2)
            act.activation(lgT[:, 512:], banks[0:NE, L_BANKS[1]], ACT.Copy).then_inc(lgT_ok, 1)
            act.wait_ge(lgN_ps, 1)
            act.activation(sc[:], banks[:, C_BANK, 0:NT * NE].rearrange("p (t e) -> p t e", e=NE), ACT.Sigmoid)\
                .then_inc(sc_ok, 1)
            silu(1, 1)
            for m in range(1, 4):
                high_h(m, m % 2)
                if m < 3:
                    silu(m + 1, (m + 1) % 2)
                if m == 3:
                    silu(4, 0)
                    act.wait_ge(combT_ps, 1)
                    act.activation(combT[:], banks[0:PARTS * NE, C_BANK].bitcast(BF16), ACT.Copy).then_inc(combT_ok, 1)
            with act.Fori(1, EXPERTS // 2 - 1) as i:
                for m in range(4):
                    high_h(i * 4 + m, m % 2)
                    silu(i * 4 + m + 1, (m + 1) % 2)
            last_n = 2 * EXPERTS - 4
            for m in range(4):
                high_h(last_n + m, m % 2)
                if m < 3:
                    silu(last_n + m + 1, (m + 1) % 2)
            act.wait_ge(d_ps, 2 * EXPERTS)
            for r in range(2):
                act.activation(yT[:, r], banks[:, YF_BANK + r], ACT.Copy).then_inc(yT_a, 1)

        @block.vector
        def _(dve):
            def add_x1(dve, b, t):
                dve.wait_ge(proj_ps, b * TILES + t + 1)
                xt = x_sb[:, bass.ds(b * TILES + t, 1), :].rearrange("p o c -> p (o c)")
                dve.tensor_tensor(xt, banks[:, 3, 0:C], xt, ALU.add).then_inc(x1_ok, 1)

            steps = [0]

            def step(ins_, base=0):
                steps[0] += 1
                ins_.then_inc(dve_step, 1)
                dve.wait_ge(dve_step, base + steps[0])

            for t in range(NT):
                if t % TILES == 0:
                    dve.wait_ge(x_in[t // TILES], 16)
                last = dve.bn_stats(stats[:, t, :], x_sb[:, t, :])
            step(last)
            for t in range(NT):
                last = dve.bn_aggr(mv[:, t, :], stats[:, t, :])
            step(last)
            dve.tensor_scalar(ve[:], mv[:, :, 1], EPS_LN, None, ALU.add).then_inc(var_ok, 1)
            dve.wait_ge(sqrt_ok, 1)
            step(dve.reciprocal(sr[:], sd[:]))
            step(dve.tensor_tensor(sr[:], sr[:], ve[:], ALU.mult))
            step(dve.tensor_tensor(sd[:], sd[:], sr[:], ALU.add))
            step(dve.tensor_scalar(sd[:], sd[:], 0.5, None, ALU.mult))
            step(dve.reciprocal(rstd[:], sd[:]))
            first = steps[0]
            with dve.Fori(0, B) as b:
                def norm_x(t):
                    dve.tensor_scalar(xn[:, t % 2], x_sb[:, bass.ds(b * TILES + t, 1), :].rearrange("p o c -> p (o c)"),
                                      mv[:, bass.ds(b * TILES + t, 1), 0], rstd[:, bass.ds(b * TILES + t, 1)],
                                      ALU.subtract, ALU.mult).then_inc(xn_ok, 1)

                def low_x(t):
                    dve.wait_ge(xh_ok, b * TILES + t + 1)
                    dve.tensor_tensor(xl[:, :, t * P:(t + 1) * P],
                                      banks[:, t % 2, 0:C].rearrange("p (k n) -> p k n", k=KC),
                                      xh[:, :, t * P:(t + 1) * P].bitcast(F32), ALU.subtract).then_inc(xl_ok, 1)

                def sum_squares(t):
                    dve.wait_ge(qkv_ok, b * TILES + t + 1)
                    dve.tensor_reduce(ss[:, bass.ds((b * TILES + t) * QKH, QKH)],
                                      sq[:, t].rearrange("p (h d) -> p h d", d=HD), AX.X, ALU.add).then_inc(ss_ok, 1)

                norm_x(0)
                norm_x(1)
                low_x(0)
                norm_x(2)
                low_x(1)
                norm_x(3)
                low_x(2)
                sum_squares(0)
                low_x(3)
                for t in range(1, TILES):
                    sum_squares(t)
            dve.wait_ge(ss_ok, NT + TILES)
            dve.wait_ge(s0_ok, 1)
            step(dve.tensor_scalar(s1[:], s0[:], 1e-30, None, ALU.max))
            step(dve.reciprocal(s1[:], s1[:]))
            step(dve.tensor_tensor(s1[:], s1[:], ss[:], ALU.mult))
            step(dve.tensor_tensor(s1[:], s1[:], s0[:], ALU.add))
            step(dve.tensor_scalar(s1[:], s1[:], 0.5, EPS_NORM, ALU.mult, ALU.add))
            step(dve.reciprocal(s0[:], s1[:]))
            dve.wait_ge(const_in, 64)

            def norm_heads(f, tile):
                if not isinstance(f, int) or f:
                    dve.wait_ge(r_ok, f)
                one = slice(tile, tile + 1) if isinstance(tile, int) else bass.ds(tile, 1)
                dve.tensor_tensor(qn[:], qkv[:, one, 0:QKC].rearrange("p o (h d) -> p (o h) d", d=HD),
                                  s0[:, bass.ds(tile * QKH, QKH)].unsqueeze(2).broadcast_to([P, QKH, HD]),
                                  ALU.mult).then_inc(qn_ok, 1)

            def cosine(f, t):
                dve.wait_ge(qn_ok, f + 1)
                dve.tensor_tensor(ra[:], qn[:], cosv[:, t % TILES].unsqueeze(1).broadcast_to([P, QKH, HD]),
                                  ALU.mult).then_inc(ra_ok, 1)

            def odd_heads(f, t, k):
                dve.wait_ge(qkT_ps, f * 3 + k + 1)
                src = banks[64:P, 2, :].rearrange("p (h n) -> p h n", n=P)
                if k < 2:
                    dve.tensor_copy(qT[:, t % 2, 8 * k + 1:8 * k + 8:2], src).then_inc(odd_ok, 1)
                else:
                    dve.tensor_copy(kT[:, t % TILES, 1:NKV:2], src[:, 0:NKV // 2]).then_inc(odd_ok, 1)

            for f in range(2):
                norm_heads(f, f)
                cosine(f, f)
            for k in range(3):
                odd_heads(0, 0, k)
            with dve.Fori(0, B) as b:
                def mask_unit(n):
                    if n >= NKV:
                        dve.wait_ge(exp_ok, b * UNITS + n + 1)
                        dve.tensor_tensor(E[:, n % 2, 0], E[:, n % 2, 0], window[:].unsqueeze(1).broadcast_to([P, REP, P]),
                                          ALU.mult).then_inc(mask_ok, 1)

                def divide(t, k):
                    count = (b * TILES + t) * KC + k + 1
                    dve.wait_ge(y_ok, b * UNITS + t * NKV + 2 * k + 4)
                    dve.reciprocal(rowsum[:, t % 2, k], rowsum[:, t % 2, k]).then_inc(rec_ok, 1)
                    dve.wait_ge(rec_ok, count)
                    dve.tensor_tensor(y[:, t % 2, k], y[:, t % 2, k], rowsum[:, t % 2, k], ALU.mult).then_inc(yn_ok, 1)

                def low_y(t):
                    dve.wait_ge(yh_ok, b * TILES + t + 1)
                    dve.wait_ge(yn_ok, (b * TILES + t + 1) * KC)
                    dve.tensor_tensor(yl[:], y[:, t % 2], yh[:].bitcast(F32), ALU.subtract).then_inc(yl_ok, 1)

                def measure(t):
                    dve.wait_ge(x1_ok, b * TILES + t + 1)
                    tt = b * TILES + t
                    dve.bn_stats(stats[:, bass.ds(tt, 1), :].rearrange("p o s -> p (o s)"),
                                 x_sb[:, bass.ds(tt, 1), :].rearrange("p o c -> p (o c)")).then_inc(stats_ok, 1)

                for n in range(UNITS):
                    t, g = n // NKV, n % NKV
                    if n + 1 < UNITS:
                        mask_unit(n + 1)
                    if g < 3:
                        odd_heads(b * TILES + t + 1, t + 1, g)
                    if g == 0 and t >= 1:
                        divide(t - 1, 1)
                    if g == 2:
                        divide(t, 0)
                    if g == 0:
                        norm_heads(b * TILES + t + 2, ahead(b, t))
                    if g == 1:
                        cosine(b * TILES + t + 2, t + 2)
                    if n >= NKV and n % NKV == 1:
                        low_y(n // NKV - 1)
                        if n >= 2 * NKV:
                            measure(n // NKV - 2)
                    if n >= NKV and n % NKV == 3:
                        add_x1(dve, b, n // NKV - 1)
                divide(TILES - 1, 1)
                low_y(TILES - 1)
                add_x1(dve, b, TILES - 1)
                measure(TILES - 2)
                measure(TILES - 1)

            def invert(part, base):
                s_, r_, v_ = sd[:, part], sr[:, part], ve[:, part]
                step(dve.reciprocal(r_, s_), base)
                step(dve.tensor_tensor(r_, r_, v_, ALU.mult), base)
                step(dve.tensor_tensor(s_, s_, r_, ALU.add), base)
                step(dve.tensor_scalar(s_, s_, 0.5, None, ALU.mult), base)
                step(dve.reciprocal(rstd[:, part], s_), base)

            def spread(done, var_sem, sqrt_sem, base, measured=False):
                for s_, v_ in done:
                    dve.wait_ge(s_, v_)
                if not measured:
                    for t in range(NT):
                        last = dve.bn_stats(stats[:, t, :], x_sb[:, t, :])
                    step(last, base)
                for t in range(NT):
                    last = dve.bn_aggr(mv[:, t, :], stats[:, t, :])
                step(last, base)
                dve.tensor_scalar(ve[:], mv[:, :, 1], EPS_LN, None, ALU.add).then_inc(var_sem, 1)
                dve.wait_ge(sqrt_sem, 1)
                invert(slice(0, NT), base)

            def norm_x2(tt):
                dve.tensor_scalar(xn2[:, tt], x_sb[:, tt, :], mv[:, tt:tt + 1, 0], rstd[:, tt:tt + 1],
                                  ALU.subtract, ALU.mult).then_inc(xn2_ok, 1)

            def low_x2(j):
                dve.wait_ge(nTh2_ok, j + 1)
                cols = slice(j * P, (j + 1) * P)
                dve.tensor_tensor(nT_l[:, :, cols], banks[:, j, 0:C].rearrange("p (k n) -> p k n", k=KC),
                                  nT_h[:, :, cols].bitcast(F32), ALU.subtract).then_inc(nTl2_ok, 1)

            def low_x21(k):
                dve.wait_ge(nTh2_ok, TILES + k + 1)
                cols = slice(T + k * 2 * P, T + (k + 1) * 2 * P)
                dve.tensor_tensor(nT_l[:, :, cols].rearrange("p k (t n) -> p t k n", n=P),
                                  banks[:, PT_BANK + k].rearrange("p (t k n) -> p t k n", t=2, k=KC),
                                  nT_h[:, :, cols].rearrange("p k (t n) -> p t k n", n=P).bitcast(F32),
                                  ALU.subtract).then_inc(nTl2_ok, 1)

            def low_q(unit, b, heads_=(0, 1), doubled=False):
                for h in heads_:
                    rows, other = slice(64 * h, 64 * h + 64), slice(64 - 64 * h, P - 64 * h)
                    dve.wait_ge(mh_ok, halves(unit, "q") + 2 * h + 2)
                    if doubled:
                        dve.scalar_tensor_tensor(q_ll[other, b, h], banks[rows, MISC], SCALE_X,
                                                 q_hh[rows, b, h].bitcast(F32), ALU.mult, ALU.subtract)
                    dve.scalar_tensor_tensor(q_ll[rows, b, h], banks[rows, MISC], SCALE_X, q_hh[rows, b, h].bitcast(F32),
                                             ALU.mult, ALU.subtract).then_inc(misc_out if h else half_out, 1)
                if 1 in heads_:
                    dve.wait_ge(misc_out, place(unit, "q") + 1)
                    dve.sem_inc(q_ok if doubled else qlo_ok, 1)

            def low_k(unit, b, c, heads_=(0, 1), bank=MISC):
                cols = slice(c * 512, c * 512 + 512)
                for h in heads_:
                    rows, other = slice(64 * h, 64 * h + 64), slice(64 - 64 * h, P - 64 * h)
                    dve.wait_ge(mh_ok, halves(unit, f"k{c}") + h + 1)
                    dve.tensor_tensor(k_st[other, b, h, cols], banks[rows, bank], k_st[rows, b, h, cols].bitcast(F32),
                                      ALU.subtract).then_inc(misc_out if h else half_out, 1)

            def max_x(head, h, q):
                dve.wait_ge(sx_ps, head * QB + q + 1)
                dve.tensor_reduce(nmax[:, h * QB + q:h * QB + q + 1],
                                  banks[:, S_BANK + 2 * (q % 2):S_BANK + 2 * (q % 2) + 2]
                                  .rearrange("p a n -> p (a n)"), AX.X, ALU.max, negate=True).then_inc(max_ok, 1)

            def low_p(head, kb):
                dve.wait_ge(pTh_ok, head * KB + kb + 1)
                dve.tensor_tensor(pT_l[:, kb % 4], banks[:, PT_BANK + kb % 2], pT_h[:, kb % 4].bitcast(F32),
                                  ALU.subtract).then_inc(pTl_ok, 1)

            def half(unit, b, h, jobs, scored, begun, more=True):
                head = unit * 2 + h
                for kb in range(KB):
                    if kb in (2, 4, 6) and scored:
                        max_x(head + 1, 1 - h, kb // 2)
                    low_p(head, kb)
                    if jobs and h == 0 and kb in (2, 3):
                        low_q(unit + 1, 1 - b, (kb - 2,))
                    if jobs and more and h == 1 and kb == 3:
                        low_k(unit + 2, b, 0)
                    if jobs and more and h == 1 and kb in (5, 7):
                        low_k(unit + 2, b, 1, (kb // 2 - 2,))
                if begun:
                    max_x(head + 2, h, 0)

            spread([(stats_ok, NT)], var2_ok, sqrt2_ok, 0, measured=True)
            dve.wait_ge(hl_ok, 2 * (NT + 2))
            for t in range(TILES):
                norm_x2(t)
            low_k(0, 0, 0)
            for j in range(TILES):
                low_x2(j)
            low_k(0, 0, 1, bank=O_BANK)
            low_q(0, 0, doubled=True)
            for t in range(TILES, NT):
                norm_x2(t)
            max_x(0, 0, 0)
            max_x(0, 0, 1)
            for k in range(2):
                low_x21(k)
            low_k(1, 1, 0)
            max_x(0, 0, 2)
            max_x(0, 0, 3)
            low_k(1, 1, 1)
            max_x(1, 1, 0)
            with dve.Fori(0, PAIRS - 1) as p:
                for b in range(B):
                    for h in range(2):
                        half(p * 2 + b, b, h, True, True, True)
            for b in range(B):
                for h in range(2):
                    half(UNITS_X - 2 + b, b, h, b == 0, b + h < 2, b == 0, more=False)
            dve.wait_ge(ex_ok, 2 * UNITS_X * QB)
            dve.reciprocal(rsum[:].rearrange("p u h q -> p (u h q)"), sums[:]).then_inc(rs_ok, 1)
            dve.wait_ge(o_sum, 2 * UNITS_X + 2)
            def scale_o(v, unit, j):
                dve.wait_ge(rT_ps, v + 1)
                dve.tensor_tensor(on[:, j], banks[:, R_BANK + j], o_all[:, bass.ds(unit, 1), :].rearrange("p o n -> p (o n)"),
                                  ALU.mult).then_inc(on_ok, 1)

            def add_x2(b):
                dve.wait_ge(y_used, PAIRS * (b + 1))
                xt = x_sb[:, b * TILES:(b + 1) * TILES, :].rearrange("p t c -> p (t c)")
                dve.tensor_tensor(xt, banks[:, Y_BANK + 2 * b:Y_BANK + 2 * b + 2].rearrange("p a n -> p (a n)"), xt, ALU.add)\
                    .then_inc(x2_ok, 1)

            def measure3(b):
                dve.wait_ge(x2_ok, b + 1)
                tiles = range(b * TILES, (b + 1) * TILES)
                for t in tiles:
                    last = dve.bn_stats(stats[:, t, :], x_sb[:, t, :])
                step(last)
                for t in tiles:
                    last = dve.bn_aggr(mv[:, t, :], stats[:, t, :])
                step(last)
                part = slice(b * TILES, (b + 1) * TILES)
                dve.tensor_scalar(ve[:, part], mv[:, part, 1], EPS_LN, None, ALU.add).then_inc(var3_ok, 1)

            def norm3(b):
                part = slice(b * TILES, (b + 1) * TILES)
                dve.wait_ge(sqrt3_ok, b + 1)
                invert(part, 0)
                if b:
                    dve.wait_ge(nT3_ps, 2)
                for t in range(TILES):
                    tt = b * TILES + t
                    dve.tensor_scalar(xn3[:, t], x_sb[:, tt, :], mv[:, tt:tt + 1, 0], rstd[:, tt:tt + 1],
                                      ALU.subtract, ALU.mult).then_inc(xn3_ok, 1)

            def low_n(b, k):
                dve.wait_ge(nTh3_ok, b * 2 + k + 1)
                cols = slice(b * T + k * 2 * P, b * T + (k + 1) * 2 * P)
                dve.tensor_tensor(nT_l[:, :, cols].rearrange("p k (t n) -> p t k n", n=P),
                                  banks[:, 2 * b + k].rearrange("p (t k n) -> p t k n", t=2, k=KC),
                                  nT_h[:, :, cols].rearrange("p k (t n) -> p t k n", n=P).bitcast(F32),
                                  ALU.subtract).then_inc(nTl3_ok, 1)

            with dve.Fori(0, PAIRS // 4) as i:
                for j in range(4):
                    scale_o(i * 4 + j, i * 8 + 2 * j, j)
            for v in range(PAIRS):
                scale_o(PAIRS + v, 2 * v + 1, v % 4)
                if v == 1:
                    add_x2(0)
                if v == 2:
                    measure3(0)
                if v == 4:
                    norm3(0)
            for k in range(2):
                low_n(0, k)
            add_x2(1)
            measure3(1)
            norm3(1)
            for k in range(2):
                low_n(1, k)
            base_f = 0
            def weigh_gate(n, c):
                dve.wait_ge(sg_ok, n + 1)
                dve.wait_ge(c_ps, n + 1 - 2 * SHARED)
                dve.tensor_tensor(gc[:, c], banks[:, C_BANK], sg[:, c], ALU.mult).then_inc(gc_ok, 1)

            def hidden(n, c):
                dve.wait_ge(u_ps, n + 1)
                if isinstance(n, int) and n < 2 * SHARED:
                    dve.wait_ge(sg_ok, n + 1)
                    dve.tensor_tensor(hid[:, c], banks[:, U_BANK], sg[:, c], ALU.mult).then_inc(hid_ok, 1)
                else:
                    dve.wait_ge(gc_ok, n + 1 - 2 * SHARED)
                    dve.tensor_tensor(hid[:, c], banks[:, U_BANK], gc[:, c], ALU.mult).then_inc(hid_ok, 1)
                dve.wait_ge(hh_ok, n + 1)
                dve.tensor_tensor(hid_l[:, c], hid[:, c], hid_h[:, c].bitcast(F32), ALU.subtract).then_inc(hlo_ok, 1)

            hidden(0, 0)
            dve.memset(gval[:], NONE)
            step(dve.memset(evalue[:], NONE), base_f)
            dve.wait_ge(sc_ok, 1)
            dve.wait_ge(gate_in, 48)
            step(dve.tensor_tensor(sfc[:], sc[:], ebias[:].unsqueeze(1).broadcast_to([P, NT, NE]), ALU.add), base_f)
            step(dve.tensor_reduce(gval[:, :, 0:GROUPS], sfc[:].rearrange("p t (g s) -> p t g s", s=GS),
                                   AX.X, ALU.max), base_f)
            for t in range(NT):
                last = dve.max(gtop[:, t], gval[:, t, 0:GROUPS])
            step(last, base_f)
            step(dve.memset(gtop[:, :, TOP_GROUPS:8], NONE), base_f)
            for t in range(NT):
                last = dve.match_replace(gout[:, t], gtop[:, t], gval[:, t], TAKEN)
            step(last, base_f)
            hidden(1, 1)
            step(dve.tensor_scalar(gmask[:], gout[:, :, 0:GROUPS], TAKEN, None, ALU.is_ge), base_f)
            step(dve.tensor_tensor(evalue[:, :, 0:NE].rearrange("p t (g s) -> p t g s", s=GS),
                                   sfc[:].rearrange("p t (g s) -> p t g s", s=GS),
                                   gmask[:].unsqueeze(3).broadcast_to([P, NT, GROUPS, GS]), ALU.mult), base_f)
            for t in range(NT):
                last = dve.max(etop[:, t], evalue[:, t, 0:NE])
            step(last, base_f)
            step(dve.memset(etop[:, :, TOP_K:8], NONE), base_f)
            for t in range(NT):
                last = dve.match_replace(eout[:, t], etop[:, t], evalue[:, t], TAKEN)
            step(last, base_f)
            step(dve.tensor_scalar(tw[:], eout[:, :, 0:NE], TAKEN, None, ALU.is_ge), base_f)
            step(dve.tensor_tensor(tw[:], tw[:], sc[:], ALU.mult), base_f)
            hidden(2, 0)
            step(dve.tensor_reduce(tsum[:], tw[:], AX.X, ALU.add), base_f)
            step(dve.tensor_scalar(tsum[:], tsum[:], 1e-20, None, ALU.add), base_f)
            step(dve.reciprocal(tsum[:], tsum[:]), base_f)
            step(dve.tensor_tensor(comb[:], tw[:], tsum[:].unsqueeze(2).broadcast_to([P, NT, NE]),
                                   ALU.mult), base_f)
            step(dve.tensor_scalar(comb[:], comb[:], ROUTE_SCALE, None, ALU.mult), base_f)
            hidden(3, 1)
            step(dve.tensor_copy(parts[:, :, 0], comb[:]), base_f)
            step(dve.tensor_tensor(cres[:], comb[:], parts[:, :, 0], ALU.subtract), base_f)
            step(dve.tensor_copy(parts[:, :, 1], cres[:]), base_f)
            step(dve.tensor_tensor(comb[:], cres[:], parts[:, :, 1], ALU.subtract), base_f)
            dve.tensor_copy(parts[:, :, 2], comb[:]).then_inc(parts_ok, 1)

            with dve.Fori(1, EXPERTS // 2) as i:
                for m in range(4):
                    weigh_gate(i * 4 + m, m % 2)
                    hidden(i * 4 + m, m % 2)
            dve.wait_ge(d_ps, 2 * EXPERTS)
            for r in range(2, 4):
                dve.tensor_copy(yT[:, r], banks[:, YF_BANK + r]).then_inc(yT_d, 1)
            for r in range(NT // 2):
                dve.wait_ge(yN_ps, r + 1)
                dve.tensor_tensor(y_out[:, 2 * r:2 * r + 2].rearrange("p t c -> p (t c)"), banks[:, 4 + r],
                                  x_sb[:, 2 * r:2 * r + 2].rearrange("p t c -> p (t c)"), ALU.add).then_inc(y_fin, 1)

        @block.tensor
        def _(pe):
            pe.wait_ge(ident_ok, 2)
            with pe.Fori(0, B) as b:
                def turn_x(t):
                    pe.wait_ge(xn_ok, b * TILES + t + 1)
                    for k in range(KC):
                        mm = pe.transpose(banks[:, t % 2, k * P:(k + 1) * P], xn[:, t % 2, k * P:(k + 1) * P], ident[:])
                    mm.then_inc(xT_ps, 1)

                def project_qkv(t):
                    pe.wait_ge(xl_ok, b * TILES + t + 1)
                    if t >= 2:
                        pe.wait_ge(qkv_ok, b * TILES + t - 1)
                    three_products(pe, banks[:, 2 + t % 2, 0:QKV],
                                   [(xh[:, k, t * P:(t + 1) * P], xl[:, k, t * P:(t + 1) * P],
                                     wqkv_h[:, k, :], wqkv_l[:, k, :]) for k in range(KC)]).then_inc(qkv_ps, 1)

                turn_x(0)
                turn_x(1)
                pe.wait_ge(wa_ok, 1)
                project_qkv(0)
                turn_x(2)
                project_qkv(1)
                turn_x(3)
                project_qkv(2)
                project_qkv(3)

            def turn_heads(f, t, k):
                if k == 0:
                    pe.wait_ge(hl_ok, f * 2 + 2)
                if not (isinstance(f, int) and f * 3 + k == 0):
                    pe.wait_ge(even_ok, f * 3 + k)
                    pe.wait_ge(odd_ok, f * 3 + k)
                for i in range(4 if k < 2 else NKV // 2):
                    h0 = 8 * k + 2 * i
                    mm = pe.transpose(banks[:, 2, i * P:(i + 1) * P],
                                      hl[:, t % 2, h0:h0 + 2].rearrange("p h c d -> p (h c d)").bitcast(F32), ident[:])
                mm.then_inc(qkT_ps, 1)

            def scores(f, t, g):
                if g == 0:
                    pe.wait_ge(even_ok, f * 3 + 3)
                    pe.wait_ge(odd_ok, f * 3 + 3)
                if t:
                    pe.matmul(banks[:, 4 + 2 * (g % 2), :], kT[:, t - 1, g], qT[:, t % 2, REP * g:REP * (g + 1)],
                              start=True, stop=True)
                own = banks[:, 5 + 2 * (g % 2), :]
                pe.matmul(own, kT[:, t, g], qT[:, t % 2, REP * g:REP * (g + 1)], start=True, stop=False)
                pe.matmul(own, identb[:], causal[:].unsqueeze(1).broadcast_to([P, REP, P]), start=False, stop=True)\
                    .then_inc(s_ps, 1)

            def weigh(b, n):
                t, g = n // NKV, n % NKV
                pe.wait_ge(exp_ok, b * UNITS + n + 1)
                pe.wait_ge(y_ok, b * UNITS + n + 1)
                for r in range(REP):
                    mm = pe.matmul(banks[:, n % 2, 0:P], va[:, t, g, r], E[:, n % 2, 1, r, :], start=(r == 0),
                                   stop=(t == 0 and r == REP - 1))
                if t:
                    pe.wait_ge(mask_ok, b * (UNITS - NKV) + n - NKV + 1)
                    for r in range(REP):
                        mm = pe.matmul(banks[:, n % 2, 0:P], va[:, t - 1, g, r], E[:, n % 2, 0, r, :], start=False,
                                       stop=(r == REP - 1))
                mm.then_inc(pv_done, 1)

            def project_y(b, t):
                pe.wait_ge(yl_ok, b * TILES + t + 1)
                if t:
                    pe.wait_ge(x1_ok, b * TILES + t)
                three_products(pe, banks[:, 3, 0:C],
                               [(yh[:, k, :], yl[:, k, :], wp_h[:, k, :], wp_l[:, k, :]) for k in range(KC)])\
                    .then_inc(proj_ps, 1)

            for k in range(3):
                turn_heads(0, 0, k)
            pe.wait_ge(v_placed, 2)
            pe.wait_ge(ident_ok, 4)
            pe.wait_ge(const_in, 64)
            pe.wait_ge(wp_ok, 1)
            scores(0, 0, 0)
            with pe.Fori(0, B) as b:
                for n in range(UNITS):
                    t, g = n // NKV, n % NKV
                    f = b * TILES + t
                    if g < 3:
                        scores(f, t, g + 1)
                        turn_heads(f + 1, t + 1, g)
                    else:
                        scores(f + 1, (t + 1) % TILES, 0)
                    if g == 0:
                        pe.wait_ge(v_placed, f + 1)
                    weigh(b, n)
                    if n >= NKV and g == 2:
                        project_y(b, t - 1)
                project_y(b, TILES - 1)

            pe.wait_ge(x1_ok, NT)

            def turn2(tt):
                pe.wait_ge(xn2_ok, tt + 1)
                bank, at = (tt, 0) if tt < TILES else (PT_BANK + (tt - TILES) // 2, tt % 2 * C)
                for k in range(KC):
                    mm = pe.transpose(banks[:, bank, at + k * P:at + (k + 1) * P], xn2[:, tt, k * P:(k + 1) * P], ident[:])
                if tt < TILES or tt % 2 == 1:
                    mm.then_inc(nT2_ps, 1)

            def begin(job):
                if not (isinstance(job, int) and job == 0):
                    pe.wait_ge(misc_out, job)

            def pair_cols(block):
                return slice(block * P, (block + 1) * P)

            def q_job(unit, pair, b):
                begin(1 if isinstance(unit, int) and unit == 0 else place(unit, "q"))
                pe.wait_ge(wq_ok, pair + 1)
                src = slice(b * T, (b + 1) * T)
                three_products(pe, banks[:, MISC], [(wx_h[:, pair_cols(k)], wx_l[:, pair_cols(k)], nT_h[:, k, src],
                                                     nT_l[:, k, src]) for k in range(KC)]).then_inc(misc_ps, 1)

            def k_job(unit, pair, b, c, bank=MISC):
                if bank == MISC:
                    begin(place(unit, f"k{c}"))
                pe.wait_ge(wk_ok, pair + 1)
                src = slice(b * M + c * 512, b * M + c * 512 + 512)
                wk = pair_cols(KC)
                three_products(pe, banks[:, bank], [(wx_h[:, wk], wx_l[:, wk], ctx_h[:, src], ctx_l[:, src])])\
                    .then_inc(misc_ps, 1)

            def v_job(unit, pair, b, a):
                begin(place(unit, f"v{a}"))
                pe.wait_ge(wv_ok, pair + 1)
                wv = pair_cols(KC + 1)
                for t in range(4):
                    src = slice(b * M + (4 * a + t) * P, b * M + (4 * a + t + 1) * P)
                    mm = three_products(pe, banks[:, MISC, t * P:(t + 1) * P],
                                        [(ctx_h[:, src], ctx_l[:, src], wx_h[:, wv], wx_l[:, wv])])
                mm.then_inc(misc_ps, 1)

            def score(head, unit, b, h, q, prologue=False):
                if q == 0:
                    pe.wait_ge(misc_out, place(unit, "q") + 1)
                    pe.wait_ge(q_ok, unit + 1)
                if not prologue or q >= 2:
                    pe.wait_ge(ex_ok, head * QB + q - 1)
                for c in range(2):
                    dst = banks[:, S_BANK + 2 * (q % 2) + c]
                    keys = k_st[:, b, h, c * 512:(c + 1) * 512]
                    pe.matmul(dst, q_hh[:, b, h, q * P:(q + 1) * P], keys, start=True, stop=False)
                    mm = pe.matmul(dst, q_ll[:, b, h, q * P:(q + 1) * P], keys, start=False, stop=True)
                mm.then_inc(sx_ps, 1)

            def turn_p(head, h, kb):
                if kb == 0:
                    pe.wait_ge(ex_ok, (head + 1) * QB)
                if kb >= 2:
                    pe.wait_ge(pTl_ok, head * KB + kb - 1)
                for q in range(QB):
                    mm = pe.transpose(banks[:, PT_BANK + kb % 2, q * P:(q + 1) * P],
                                      probs[:, h, q, kb * P:(kb + 1) * P], ident[:])
                mm.then_inc(pT_ps, 1)

            def weigh_x(head, unit, b, h, kb):
                pe.wait_ge(pTl_ok, head * KB + kb + 1)
                if kb == 0:
                    pe.wait_ge(o_free, head + 1)
                if kb % 4 == 0 and h == 0:
                    pe.wait_ge(v_ok, unit * 2 + 1 + kb // 4)
                v = v_hl[:, b, kb, h].rearrange("p r d -> p (r d)")
                pe.matmul(banks[:, O_BANK], v, pT_h[:, kb % 4], start=(kb == 0), stop=False)
                mm = pe.matmul(banks[:, O_BANK], v, pT_l[:, kb % 4], start=False, stop=(kb == KB - 1))
                if kb == KB - 1:
                    mm.then_inc(o_ps, 1)

            def half(unit, pair, b, h, jobs, scored, begun, more=True):
                head = unit * 2 + h
                nb = 1 - b

                def score_next(q):
                    if scored:
                        score(head + 1, unit + h, b if h == 0 else nb, 1 - h, q)

                def job(i):
                    if jobs and h == 0 and i == 0:
                        q_job(unit + 1, pair + b, nb)
                    if jobs and h == 0 and i == 2:
                        v_job(unit + 1, pair + b, nb, 0)
                    if jobs and h == 1 and i == 0:
                        v_job(unit + 1, pair + b, nb, 1)
                    if jobs and more and h == 1 and i > 0:
                        k_job(unit + 2, pair + 1, b, i - 1)

                turn_p(head, h, 0)
                turn_p(head, h, 1)
                for q in range(1, QB):
                    job(q - 1)
                    score_next(q)
                    for kb in (2 * q, 2 * q + 1):
                        turn_p(head, h, kb)
                        weigh_x(head, unit, b, h, kb - 2)
                if begun:
                    score(head + 2, unit + 1, nb, h, 0)
                weigh_x(head, unit, b, h, 6)
                weigh_x(head, unit, b, h, 7)

            pe.wait_ge(ctx_ok, NT)
            k_job(0, 0, 0, 0)
            k_job(0, 0, 0, 1, O_BANK)
            for t in range(TILES):
                turn2(t)
            pe.wait_ge(nTl2_ok, TILES)
            q_job(0, 0, 0)
            for q in range(2):
                score(0, 0, 0, 0, q, prologue=True)
            for t in range(TILES, NT):
                turn2(t)
            k_job(1, 0, 1, 0)
            score(0, 0, 0, 0, 2, prologue=True)
            v_job(0, 0, 0, 0)
            score(0, 0, 0, 0, 3, prologue=True)
            k_job(1, 0, 1, 1)
            score(1, 0, 0, 1, 0)
            v_job(0, 0, 0, 1)
            pe.wait_ge(nTl2_ok, TILES + 2)
            with pe.Fori(0, PAIRS - 1) as p:
                for b in range(B):
                    for h in range(2):
                        half(p * 2 + b, p, b, h, True, True, True)
            for b in range(B):
                for h in range(2):
                    half(UNITS_X - 2 + b, PAIRS - 1, b, h, b == 0, b + h < 2, b == 0, more=False)

            pe.wait_ge(wo_ok, PAIRS)
            pe.wait_ge(ones_ok, REP + 2)
            pe.wait_ge(bo_in, 16)
            for c in range(2 * B):
                pe.matmul(banks[:, Y_BANK + c], ones1[:], bo2[:], start=True, stop=False, skip_group_check=True)

            def turn_sums(unit, j):
                pe.wait_ge(rexp_ok, unit + 1)
                for q in range(QB):
                    mm = pe.transpose(banks[:, R_BANK + j, q * P:(q + 1) * P], rexp[:, j, q], ident[:])
                mm.then_inc(rT_ps, 1)

            def project_o(v, pair, b, j):
                pe.wait_ge(onl_ok, v + 1)
                wh, wl = (w[:, bass.ds(pair, 1), :].rearrange("p o n -> p (o n)") for w in (wo_h, wo_l))
                for q in range(QB):
                    dst = banks[:, Y_BANK + 2 * b + q // 2, (q % 2) * C:(q % 2 + 1) * C]
                    oh, ol = on_h[:, j, q * P:(q + 1) * P], on_l[:, j, q * P:(q + 1) * P]
                    pe.matmul(dst, oh, wh, start=False, stop=False, skip_group_check=True)
                    pe.matmul(dst, oh, wl, start=False, stop=False, skip_group_check=True)
                    mm = pe.matmul(dst, ol, wh, start=False, stop=False, skip_group_check=True)
                mm.then_inc(y_used, 1)

            def turn3(b):
                for k in range(2):
                    pe.wait_ge(xn3_ok, b * TILES + 2 * k + 2)
                    for t in range(2):
                        for f in range(KC):
                            mm = pe.transpose(banks[:, 2 * b + k, (t * KC + f) * P:(t * KC + f + 1) * P],
                                              xn3[:, 2 * k + t, f * P:(f + 1) * P], ident[:])
                    mm.then_inc(nT3_ps, 1)

            def logits(c):
                pe.wait_ge(nTl3_ok, 2 * c + 2)
                src = slice(c * 512, (c + 1) * 512)
                for k in range(KC):
                    for a in range(2):
                        for w in (wg_h, wg_l):
                            mm = pe.matmul(banks[0:NE, L_BANKS[c]], w[:, k], (nT_h if a == 0 else nT_l)[:, k, src],
                                           start=(k == 0 and a == 0 and w is wg_h),
                                           stop=(k == KC - 1 and a == 1 and w is wg_l))
                mm.then_inc(lg_ps, 1)

            for j in range(3):
                turn_sums(j, j)
            with pe.Fori(0, PAIRS // 4) as i:
                for j in range(4):
                    turn_sums(i * 4 + j + 3, (j + 3) % 4)
                    project_o(i * 4 + j, i * 4 + j, 0, j)
            for v in range(PAIRS):
                if v + 3 < PAIRS:
                    turn_sums(PAIRS + v + 3, (v + 3) % 4)
                project_o(PAIRS + v, v, 1, v % 4)
                if v == 5:
                    turn3(0)

            def spread_weight(n, c, e):
                if isinstance(n, int) and n == 2 * SHARED:
                    pe.wait_ge(combT_ok, 1)
                else:
                    pe.wait_ge(gc_ok, n - 2 * SHARED)
                pe.matmul(banks[:, C_BANK], sel[:, bass.ds((e - SHARED) * P, P)], combT[:, c * 512:(c + 1) * 512],
                          start=True, stop=True).then_inc(c_ps, 1)

            def gate_up(n, j, c, e, first_step=False, routed=True):
                src = slice(c * 512, (c + 1) * 512)
                if c == 0:
                    pe.wait_ge(wgu_ok, e + 1)

                def product(bank, off):
                    return three_products(pe, banks[:, bank], [
                        (wf_h[:, j, k * 2 * NI + off:k * 2 * NI + off + NI],
                         wf_l[:, j, k * 2 * NI + off:k * 2 * NI + off + NI],
                         nT_h[:, k, src], nT_l[:, k, src]) for k in range(KC)])

                product(G_BANK + c, 0).then_inc(g_ps, 1)
                if routed:
                    spread_weight(n, c, e)
                if not first_step:
                    pe.wait_ge(hid_ok, n)
                product(U_BANK, NI).then_inc(u_ps, 1)

            pe.wait_ge(wg_ok, 1)
            logits(0)
            gate_up(0, 0, 0, 0, first_step=True, routed=False)
            turn3(1)
            logits(1)
            pe.wait_ge(nTl3_ok, 4)

            def turn_logits():
                for t in range(NT):
                    mm = pe.transpose(banks[:, C_BANK, t * NE:(t + 1) * NE], lgT[:, t * P:(t + 1) * P],
                                      ident[0:NE, 0:NE])
                mm.then_inc(lgN_ps, 1)

            def turn_weights():
                pe.wait_ge(parts_ok, 1)
                for t in range(NT):
                    mm = pe.transpose(banks[0:PARTS * NE, C_BANK, t * 64:(t + 1) * 64].bitcast(BF16),
                                      parts[:, t].rearrange("p r e -> p (r e)"), identb[:])
                mm.then_inc(combT_ps, 1)

            def down(n, j, c, e):
                pe.wait_ge(hlo_ok, n + 1)
                if c == 0:
                    pe.wait_ge(wdn_ok, e + 1)
                off = GU
                for f in range(KC):
                    dst = banks[:, YF_BANK + 2 * c + f]
                    wh = wf_h[:, j, off + f * P:off + (f + 1) * P]
                    wl = wf_l[:, j, off + f * P:off + (f + 1) * P]
                    first = isinstance(n, int) and n < 2
                    pe.matmul(dst, wh, hid_h[:, c], start=first, stop=False, skip_group_check=True)
                    pe.matmul(dst, wh, hid_l[:, c], start=False, stop=False, skip_group_check=True)
                    mm = pe.matmul(dst, wl, hid_h[:, c], start=False, stop=False, skip_group_check=True)
                mm.then_inc(d_ps, 1)

            pe.wait_ge(lgT_ok, 2)
            turn_logits()
            for m in range(4):
                m1 = m + 1
                gate_up(m1, (m1 // 2) % 2, m1 % 2, m1 // 2, routed=False)
                down(m, m // 2, m % 2, m // 2)
            turn_weights()
            spread_weight(2 * SHARED, 0, SHARED)
            with pe.Fori(1, EXPERTS // 2 - 1) as i:
                for m in range(4):
                    m1 = m + 1
                    gate_up(i * 4 + m1, (m1 // 2) % 2, m1 % 2, i * 2 + m1 // 2)
                    down(i * 4 + m, m // 2, m % 2, i * 2 + m // 2)
            for m in range(4):
                n = 2 * EXPERTS - 4 + m
                if m < 3:
                    gate_up(n + 1, (m + 1) // 2, (m + 1) % 2, EXPERTS - 2 + (m + 1) // 2)
                down(n, m // 2, m % 2, EXPERTS - 2 + m // 2)
            for r in range(NT // 2):
                c = r // 2
                if r % 2 == 0:
                    pe.wait_ge(yT_a if c == 0 else yT_d, 2)
                for tt in range(2):
                    for f in range(KC):
                        tok = ((2 * r + tt) * P) % 512
                        mm = pe.transpose(banks[:, 4 + r, tt * C + f * P:tt * C + (f + 1) * P],
                                          yT[:, 2 * c + f, tok:tok + P], ident[:])
                mm.then_inc(yN_ps, 1)


def three_products(pe, dst, parts):
    n = len(parts)
    for k, (ah, al, bh, bl) in enumerate(parts):
        pe.matmul(dst, ah, bh, start=(k == 0), stop=False)
        pe.matmul(dst, ah, bl, start=False, stop=False)
        mm = pe.matmul(dst, al, bh, start=False, stop=(k == n - 1))
    return mm


def rope_table():
    theta = (1.0 / 10000.0 ** (np.arange(0, HD, 2, dtype=np.float32) / np.float32(HD))).astype(np.float32)
    freqs = np.outer(np.arange(T, dtype=np.float32), theta).astype(np.float32)
    cos, sin = np.cos(freqs), np.sin(freqs)
    return (np.concatenate([cos, cos], axis=1).astype(np.float32),
            np.concatenate([-sin, sin], axis=1).astype(np.float32))


def band_masks():
    key, query = np.arange(P)[:, None], np.arange(P)[None, :]
    return (key > query).astype(np.float32), np.where(key <= query, 0.0, NONE).astype(np.dtype("bfloat16"))


def pair_weights(wq, wk, wv, wo):
    q = wq.reshape(KC, P, PAIRS, P).transpose(2, 1, 0, 3).reshape(PAIRS, P, KC * P)
    k = wk.reshape(P, PAIRS, P).transpose(1, 0, 2)
    v = wv.reshape(P, PAIRS, P).transpose(1, 0, 2)
    return np.concatenate([q, k, v, wo.reshape(PAIRS, P, C)], axis=2)


def expert_weights(gate_up, down, sh_gate, sh_up, sh_down):
    g = np.concatenate([sh_gate.reshape(SHARED, NI, C), gate_up[:, :NI]])
    u = np.concatenate([sh_up.reshape(SHARED, NI, C), gate_up[:, NI:]])
    d = np.concatenate([sh_down.reshape(C, SHARED, NI).transpose(1, 0, 2), down])
    gu = np.concatenate([g, u], axis=1).transpose(0, 2, 1).reshape(EXPERTS, KC, P, 2 * NI).transpose(0, 2, 1, 3)
    return np.concatenate([gu.reshape(EXPERTS, P, KC * 2 * NI), d.transpose(0, 2, 1)], axis=2)


def selectors():
    one = np.equal(np.arange(PARTS * NE)[:, None] % NE, np.arange(NE)[None, :])
    return np.repeat(one, P, axis=1).astype(np.dtype("bfloat16"))


def kernel(**inputs):
    import concourse.bacc as bacc
    from concourse.bass_utils import run_bass_kernel_spmd

    a = {k: np.asarray(v) for k, v in inputs.items()}
    cosv, sinv = rope_table()
    window, causal = band_masks()
    arrays = {
        "x": a["x"],
        "wqkv": np.concatenate([a["L0_attn_Wq"], a["L0_attn_Wkv"]], axis=0).T,
        "wp": a["L0_attn_Wproj"].T,
        "ctxT": a["ctx_512"].reshape(B * M, CD).T,
        "wx": pair_weights(a["L0_xattn_Wq"], a["L0_xattn_Wk"], a["L0_xattn_Wv"],
                           a["L0_xattn_Wo"]),
        "bo2": np.concatenate([a["L0_xattn_bo"], a["L0_xattn_bo"]])[None, :],
        "wf": expert_weights(a["L0_ffn_experts_gate_up"], a["L0_ffn_experts_down"], a["L0_ffn_shared_gate_w"],
                             a["L0_ffn_shared_up_w"], a["L0_ffn_shared_down_w"]),
        "wg": a["L0_ffn_gate_weight"].T,
        "ebias": a["L0_ffn_e_score_correction_bias"],
        "sel": selectors(),
        "cosv": cosv, "sinv": sinv, "window": window, "causal": causal,
    }
    arrays = {k: np.ascontiguousarray(v) for k, v in arrays.items()}
    nc = bacc.Bacc("TRN2", target_bir_lowering=False, num_devices=1)
    ins = {k: nc.dram_tensor(f"{k}_dram", v.shape, mybir.dt.from_np(v.dtype), kind="ExternalInput").ap()
           for k, v in arrays.items()}
    out = nc.dram_tensor("out_dram", (B, T, C), F32, kind="ExternalOutput").ap()
    mk_decoder(nc, ins, out)
    r = run_bass_kernel_spmd(nc, [{f"{k}_dram": v for k, v in arrays.items()}], core_ids=[0])
    return r.results[0]["out_dram"]
```
